# Optimizing a Trainium2 kernel written in Bass

```python
import numpy as np
import jax
import jax.numpy as jnp

def _softmax(x, axis=-1):
    return jax.nn.softmax(x, axis=axis)

def _gelu(x):
    return jax.nn.gelu(x, approximate=True)

def _silu(x):
    return jax.nn.silu(x)

def _sigmoid(x):
    return jax.nn.sigmoid(x)

def _layernorm(x, axis=-1, eps=1e-05):
    m = jnp.mean(x, axis=axis, keepdims=True)
    v = jnp.var(x, axis=axis, keepdims=True)
    return (x - m) / jnp.sqrt(v + eps)

def _scatter_add(tgt, idx, src, axis=0):
    return tgt.at[idx].add(src)

def _segment_sum(src, seg, n):
    return jax.ops.segment_sum(src, seg, n)
kernel_name = 'mk_sandwich_d4_jaxref_r8_912e3f'

def setup_inputs(seed: int=0):
    np.random.seed(seed)
    _w = jnp.asarray

    def _L0_attn_setup():
        import jax, jax.numpy as jnp
        import numpy as np
        EPS = 1e-06

        def _rmsnorm(z, w):
            zf = z.astype(jnp.float32)
            zn = zf * jax.lax.rsqrt(jnp.mean(zf * zf, axis=-1, keepdims=True) + EPS)
            return zn.astype(z.dtype) * w
        key = jax.random.key(seed)
        ks = jax.random.split(key, 6)
        B, T, D, H = (4, 512, 128, 256)
        x = jax.random.normal(ks[0], (B, T, D), dtype=jnp.float32)
        input_norm_w = jnp.ones((D,), dtype=jnp.float32)
        a_log = jax.random.normal(ks[1], (D,), dtype=jnp.float32) * 0.5
        c_out = jax.random.normal(ks[2], (D,), dtype=jnp.float32)
        d_skip = jax.random.normal(ks[3], (D,), dtype=jnp.float32)
        ff_norm_w = jnp.ones((D,), dtype=jnp.float32)
        ff_fc_w = jax.random.normal(ks[4], (H, D), dtype=jnp.float32) * 0.02
        ff_proj_w = jax.random.normal(ks[5], (D, H), dtype=jnp.float32) * 0.02
        return {'x': x, 'input_norm_w': input_norm_w, 'a_log': a_log, 'c_out': c_out, 'd_skip': d_skip, 'ff_norm_w': ff_norm_w, 'ff_fc_w': ff_fc_w, 'ff_proj_w': ff_proj_w}
    _L0_attn_in = _L0_attn_setup()

    def _L0_ffn_setup():
        import jax, jax.numpy as jnp
        import numpy as np
        E = 8
        TOP_K = 2
        ROUTE_SCALE = 1.0
        ALPHA = 1.702
        LIMIT = 7.0
        D = 128
        F = 128
        B, S = (2, 128)

        def swiglu(h):
            g = jnp.minimum(h[..., ::2], LIMIT)
            l = jnp.clip(h[..., 1::2], -LIMIT, LIMIT)
            return g * jax.nn.sigmoid(ALPHA * g) * (l + 1.0)
        if __name__ == '__main__':
            out = reference(**setup_inputs())
            print(out.shape, out.dtype)
        key = jax.random.key(seed)
        ks = jax.random.split(key, 16)
        sd = 1.0 / np.sqrt(D)
        sf = 1.0 / np.sqrt(F)
        return {'x': jax.random.normal(ks[0], (B, S, D), jnp.float32), 'gate_w': jax.random.normal(ks[1], (E, D), jnp.float32) * sd, 'gate_b': jax.random.normal(ks[2], (E,), jnp.float32) * 0.01, 'w1': jax.random.normal(ks[3], (E, 2 * F, D), jnp.float32) * sd, 'b1': jax.random.normal(ks[4], (E, 2 * F), jnp.float32) * 0.01, 'w3': jax.random.normal(ks[5], (E, 2 * F, D), jnp.float32) * sd, 'b3': jax.random.normal(ks[6], (E, 2 * F), jnp.float32) * 0.01, 'w2': jax.random.normal(ks[7], (E, D, F), jnp.float32) * sf, 'b2': jax.random.normal(ks[8], (E, D), jnp.float32) * 0.01, 'sw1': jax.random.normal(ks[9], (2 * F, D), jnp.float32) * sd, 'sb1': jax.random.normal(ks[10], (2 * F,), jnp.float32) * 0.01, 'sw3': jax.random.normal(ks[11], (2 * F, D), jnp.float32) * sd, 'sb3': jax.random.normal(ks[12], (2 * F,), jnp.float32) * 0.01, 'sw2': jax.random.normal(ks[13], (D, F), jnp.float32) * sf, 'sb2': jax.random.normal(ks[14], (D,), jnp.float32) * 0.01}
    _L0_ffn_in = _L0_ffn_setup()

    def _L1_attn_setup():
        import jax, jax.numpy as jnp
        import numpy as np
        D = 128
        H = 16
        KVH = 4
        HD = D // H
        LAT = 32
        WIN = 32
        B, S = (1, 256)
        BASE_G, BASE_L = (1000000.0, 10000.0)
        EPS = 1e-06

        def rmsnorm(x, w):
            return x * jax.lax.rsqrt(jnp.mean(x * x, axis=-1, keepdims=True) + EPS) * w

        def qk_norm(x):
            return x * jax.lax.rsqrt(jnp.mean(x * x, axis=-1, keepdims=True) + EPS)

        def rope(x, base):
            s, hd = (x.shape[-2], x.shape[-1])
            inv_freq = 1.0 / base ** (jnp.arange(0, hd, 2, dtype=jnp.float32) / hd)
            freqs = jnp.arange(s, dtype=jnp.float32)[:, None] * inv_freq[None, :]
            cos, sin = (jnp.cos(freqs), jnp.sin(freqs))
            xe, xo = (x[..., ::2], x[..., 1::2])
            out = jnp.stack([xe * cos - xo * sin, xe * sin + xo * cos], axis=-1)
            return out.reshape(x.shape)

        def split_heads(x, n_heads):
            b, s, _ = x.shape
            return x.reshape(b, s, n_heads, HD).transpose(0, 2, 1, 3)

        def repeat_kv(x):
            return jnp.repeat(x, H // KVH, axis=1)

        def sdpa(q, k, v, mask):
            scores = jnp.einsum('bhqd,bhkd->bhqk', q, k) / np.sqrt(HD).astype(np.float32)
            scores = jnp.where(mask, scores, jnp.float32(-1e+30))
            probs = jax.nn.softmax(scores, axis=-1)
            return jnp.einsum('bhqk,bhkd->bhqd', probs, v)

        def merge_heads(x):
            b, h, s, hd = x.shape
            return x.transpose(0, 2, 1, 3).reshape(b, s, h * hd)

        def global_latent_attn(x, wq, w_kv_down, w_k_up, w_v_up, wo):
            q = split_heads(x @ wq, H)
            latent = x @ w_kv_down
            k = split_heads(latent @ w_k_up, KVH)
            v = split_heads(latent @ w_v_up, KVH)
            q, k = (rope(q, BASE_G), rope(k, BASE_G))
            q, k = (qk_norm(q), qk_norm(k))
            k, v = (repeat_kv(k), repeat_kv(v))
            i = jnp.arange(x.shape[1])
            causal = i[:, None] >= i[None, :]
            return merge_heads(sdpa(q, k, v, causal)) @ wo

        def local_gqa_attn(x, wq, wk, wv, wo):
            q = split_heads(x @ wq, H)
            k = split_heads(x @ wk, KVH)
            v = split_heads(x @ wv, KVH)
            q, k = (rope(q, BASE_L), rope(k, BASE_L))
            q, k = (qk_norm(q), qk_norm(k))
            k, v = (repeat_kv(k), repeat_kv(v))
            i = jnp.arange(x.shape[1])
            diff = i[:, None] - i[None, :]
            mask = (diff >= 0) & (diff < WIN)
            return merge_heads(sdpa(q, k, v, mask)) @ wo
        key = jax.random.key(seed)
        ks = jax.random.split(key, 12)
        std = 0.02
        return {'hidden': jax.random.normal(ks[0], (B, S, D), dtype=jnp.float32), 'norm1_w': jnp.ones((D,), jnp.float32), 'norm2_w': jnp.ones((D,), jnp.float32), 'g_wq': jax.random.normal(ks[1], (D, H * HD), jnp.float32) * std, 'g_kv_down': jax.random.normal(ks[2], (D, LAT), jnp.float32) * std, 'g_k_up': jax.random.normal(ks[3], (LAT, KVH * HD), jnp.float32) * std, 'g_v_up': jax.random.normal(ks[4], (LAT, KVH * HD), jnp.float32) * std, 'g_wo': jax.random.normal(ks[5], (D, D), jnp.float32) * std, 'l_wq': jax.random.normal(ks[6], (D, H * HD), jnp.float32) * std, 'l_wk': jax.random.normal(ks[7], (D, KVH * HD), jnp.float32) * std, 'l_wv': jax.random.normal(ks[8], (D, KVH * HD), jnp.float32) * std, 'l_wo': jax.random.normal(ks[9], (D, D), jnp.float32) * std}
    _L1_attn_in = _L1_attn_setup()

    def _L1_ffn_setup():
        import jax, jax.numpy as jnp
        import numpy as np
        B, S, D, H, L, E, K = (4, 128, 128, 16, 2, 8, 2)
        DFF = 4 * D

        def _ln(x, w, b):
            m = x.mean(-1, keepdims=True)
            v = x.var(-1, keepdims=True)
            return (x - m) / jnp.sqrt(v + 1e-05) * w + b

        def _attn(x, wq, wk, wv, wo, bq, bk, bv, bo):
            Bb, T, C = x.shape
            hd = C // H
            q = (x @ wq + bq).reshape(Bb, T, H, hd).transpose(0, 2, 1, 3)
            k = (x @ wk + bk).reshape(Bb, T, H, hd).transpose(0, 2, 1, 3)
            v = (x @ wv + bv).reshape(Bb, T, H, hd).transpose(0, 2, 1, 3)
            att = jnp.einsum('bhqd,bhkd->bhqk', q, k) * hd ** (-0.5)
            causal = jnp.tril(jnp.ones((T, T), bool))
            att = jnp.where(causal, att, -jnp.inf)
            att = jax.nn.softmax(att, axis=-1)
            y = jnp.einsum('bhqk,bhkd->bhqd', att, v).transpose(0, 2, 1, 3).reshape(Bb, T, C)
            return y @ wo + bo

        def _ffn(h, w1, b1, w2, b2):
            return jax.nn.gelu(h @ w1 + b1, approximate=False) @ w2 + b2

        def _combine_weights(logits):
            vals, idx = jax.lax.top_k(logits, K)
            w = jax.nn.softmax(vals, axis=-1)
            onehot = (idx[..., None] == jnp.arange(E)).astype(w.dtype)
            return jnp.sum(w[..., None] * onehot, axis=-2)

        def _token_moe(h, gw, gb, w1, b1, w2, b2):
            cw = _combine_weights(h @ gw + gb)
            out = jnp.zeros_like(h)
            for e in range(E):
                out = out + _ffn(h, w1[e], b1[e], w2[e], b2[e]) * cw[..., e:e + 1]
            return out

        def _seq_moe(h, gw, gb, w1, b1, w2, b2):
            cw = _combine_weights(h.mean(axis=1) @ gw + gb)
            out = jnp.zeros_like(h)
            for e in range(E):
                out = out + _ffn(h, w1[e], b1[e], w2[e], b2[e]) * cw[:, e, None, None]
            return out
        key = jax.random.key(seed)
        ks = jax.random.split(key, 9)
        n = lambda k, shp: jax.random.normal(k, shp, dtype=jnp.float32) * 0.02
        return {'x': jax.random.normal(ks[0], (B, S, D), dtype=jnp.float32), 'ln1_w': jnp.ones((L, D), jnp.float32), 'ln1_b': jnp.zeros((L, D), jnp.float32), 'ln2_w': jnp.ones((L, D), jnp.float32), 'ln2_b': jnp.zeros((L, D), jnp.float32), 'wq': n(ks[1], (L, D, D)), 'wk': n(ks[2], (L, D, D)), 'wv': n(ks[3], (L, D, D)), 'wo': n(ks[4], (L, D, D)), 'bq': jnp.zeros((L, D), jnp.float32), 'bk': jnp.zeros((L, D), jnp.float32), 'bv': jnp.zeros((L, D), jnp.float32), 'bo': jnp.zeros((L, D), jnp.float32), 'gate_w': n(ks[5], (L, D, E)), 'gate_b': jnp.zeros((L, E), jnp.float32), 'e_w1': n(ks[6], (L, E, D, DFF)), 'e_b1': jnp.zeros((L, E, DFF), jnp.float32), 'e_w2': n(ks[7], (L, E, DFF, D)), 'e_b2': jnp.zeros((L, E, D), jnp.float32)}
    _L1_ffn_in = _L1_ffn_setup()

    def _L2_attn_setup():
        import jax, jax.numpy as jnp
        import numpy as np
        import math
        B, S, DIM = (2, 256, 128)
        H, KVH = (16, 4)
        HD = DIM // H
        WINDOW = 32
        ROPE_BASE = 10000.0
        EPS = 1e-06

        def _rms_norm(v):
            return v * jax.lax.rsqrt(jnp.mean(v * v, axis=-1, keepdims=True) + EPS)

        def _rope_tables(seqlen, dtype):
            inv_freq = 1.0 / ROPE_BASE ** (jnp.arange(0, HD, 2, dtype=jnp.float32) / HD)
            t = jnp.arange(seqlen, dtype=jnp.float32)
            freqs = jnp.outer(t, inv_freq)
            return (jnp.cos(freqs).astype(dtype)[None, None], jnp.sin(freqs).astype(dtype)[None, None])

        def _apply_rotary(v, cos, sin):
            half = v.shape[-1] // 2
            v1, v2 = (v[..., :half], v[..., half:])
            return jnp.concatenate((v1 * cos + v2 * sin, -v1 * sin + v2 * cos), axis=-1)
        key = jax.random.key(seed)
        ks = jax.random.split(key, 6)
        s = 0.02
        return {'x': jax.random.normal(ks[0], (B, S, DIM), jnp.float32), 'Wq': jax.random.normal(ks[1], (DIM, DIM), jnp.float32) * s, 'Wk': jax.random.normal(ks[2], (KVH * HD, DIM), jnp.float32) * s, 'Wv': jax.random.normal(ks[3], (KVH * HD, DIM), jnp.float32) * s, 'Wo': jax.random.normal(ks[4], (DIM, DIM), jnp.float32) * s, 'q_gain': jnp.ones((H,), jnp.float32), 'pair_mix': jnp.tile(jnp.eye(2, dtype=jnp.float32), (H // 2, 1, 1)) + 0.01 * jax.random.normal(ks[5], (H // 2, 2, 2), jnp.float32)}
    _L2_attn_in = _L2_attn_setup()

    def _L2_ffn_setup():
        import jax, jax.numpy as jnp
        import numpy as np
        TOP_K = 2
        key = jax.random.key(seed)
        k1, k2, k3 = jax.random.split(key, 3)
        B, S, H, E = (4, 256, 128, 8)
        x = jax.random.normal(k1, (B, S, H), dtype=jnp.float32)
        gate_w = jax.random.normal(k2, (E, H), dtype=jnp.float32) / np.sqrt(H)
        gate_b = jnp.zeros((E,), dtype=jnp.float32)
        expert_w = jax.random.normal(k3, (E, H, H), dtype=jnp.float32) / np.sqrt(H)
        expert_b = jnp.zeros((E, H), dtype=jnp.float32)
        return {'x': x, 'gate_w': gate_w, 'gate_b': gate_b, 'expert_w': expert_w, 'expert_b': expert_b}
    _L2_ffn_in = _L2_ffn_setup()

    def _L3_attn_setup():
        import jax, jax.numpy as jnp
        import numpy as np
        B, N, D = (2, 256, 128)
        H, M = (8, 64)
        DK = D // H
        EPS = 1e-05

        def _gsa(q, k, v, s, g):
            b = q.shape[1]

            def step1(hk, t):
                q_t, k_t, s_t, g_t = t
                hk = hk * jnp.exp(g_t)[:, :, None, :] + k_t[..., :, None] * s_t[..., None, :]
                ok = jnp.einsum('bhk,bhkm->bhm', q_t, hk)
                return (hk, ok)
            hk0 = jnp.zeros((b, H, DK, M), q.dtype)
            _, ok = jax.lax.scan(step1, hk0, (q, k, s, g))
            qv = jax.nn.softmax(ok, axis=-1)

            def step2(hv, t):
                qv_t, s_t, v_t, g_t = t
                hv = hv * jnp.exp(g_t)[..., :, None] + s_t[..., :, None] * v_t[..., None, :]
                ov = jnp.einsum('bhm,bhmv->bhv', qv_t, hv)
                return (hv, ov)
            hv0 = jnp.zeros((b, H, M, DK), q.dtype)
            _, ov = jax.lax.scan(step2, hv0, (qv, s, v, g))
            return ov
        key = jax.random.key(seed)
        ks = jax.random.split(key, 9)
        std = 0.02
        return {'x': jax.random.normal(ks[0], (B, N, D), jnp.float32), 'Wq': jax.random.normal(ks[1], (D, D), jnp.float32) * std, 'Wk': jax.random.normal(ks[2], (D, D), jnp.float32) * std, 'Wv': jax.random.normal(ks[3], (D, D), jnp.float32) * std, 'Wf1': jax.random.normal(ks[4], (D, DK), jnp.float32) * std, 'Wf2': jax.random.normal(ks[5], (DK, H * M), jnp.float32) * std, 'Wg1': jax.random.normal(ks[6], (D, DK), jnp.float32) * std, 'Wg2': jax.random.normal(ks[7], (DK, D), jnp.float32) * std, 'Wo': jax.random.normal(ks[8], (D, D), jnp.float32) * std, 'norm_w': jnp.ones((D,), jnp.float32)}
    _L3_attn_in = _L3_attn_setup()

    def _L3_ffn_setup():
        import jax, jax.numpy as jnp
        import numpy as np
        BS, SLEN, DIM = (1, 256, 128)
        NUM_EXPERTS, TOP_K = (8, 2)
        HID = 176

        def _masked_grouped_mm(x, w, onehot):
            g = jnp.einsum('tk,gnk->tgn', x, w, preferred_element_type=jnp.float32)
            return jnp.einsum('tgn,tg->tn', g, onehot)

        def moe_forward(x, gate_w, expert_bias, w_up, w_down, shared_w_up, shared_w_down):
            bs, slen, dim = x.shape
            xf = x.reshape(-1, dim)
            scores = jax.nn.sigmoid((xf @ gate_w.T).astype(jnp.float32))
            biased = scores + expert_bias
            _, sel = jax.lax.top_k(biased, TOP_K)
            top_scores = jnp.take_along_axis(scores, sel, axis=-1)
            flat_sel = sel.reshape(-1)
            counts = jnp.bincount(flat_sel, length=NUM_EXPERTS)
            order = jnp.argsort(flat_sel, stable=True)
            scores_sorted = top_scores.reshape(-1)[order]
            token_ids = order // TOP_K
            routed_in = (xf[token_ids] * scores_sorted[:, None]).astype(x.dtype)
            seg = jnp.repeat(jnp.arange(NUM_EXPERTS), counts, total_repeat_length=flat_sel.shape[0])
            onehot = jax.nn.one_hot(seg, NUM_EXPERTS, dtype=jnp.float32)
            h = _masked_grouped_mm(routed_in.astype(jnp.bfloat16), w_up.astype(jnp.bfloat16), onehot)
            h = jnp.square(jax.nn.relu(h.astype(jnp.bfloat16)))
            routed_out = _masked_grouped_mm(h.astype(jnp.bfloat16), w_down.astype(jnp.bfloat16), onehot)
            routed_out = routed_out.astype(jnp.bfloat16).astype(x.dtype)
            hs = jnp.square(jax.nn.relu(xf @ shared_w_up.T))
            shared_out = hs @ shared_w_down.T
            combined = jnp.zeros((flat_sel.shape[0], dim), routed_out.dtype).at[order].set(routed_out)
            out = combined.reshape(-1, TOP_K, dim).sum(axis=1) + shared_out
            return out.reshape(bs, slen, dim)
        key = jax.random.key(seed)
        k = jax.random.split(key, 6)
        s = 0.02
        return {'x': jax.random.normal(k[0], (BS, SLEN, DIM), jnp.float32), 'gate_w': jax.random.normal(k[1], (NUM_EXPERTS, DIM), jnp.float32) * s, 'expert_bias': jnp.zeros((NUM_EXPERTS,), jnp.float32), 'w_up': jax.random.normal(k[2], (NUM_EXPERTS, HID, DIM), jnp.float32) * s, 'w_down': jax.random.normal(k[3], (NUM_EXPERTS, DIM, HID), jnp.float32) * s, 'shared_w_up': jax.random.normal(k[4], (HID, DIM), jnp.float32) * s, 'shared_w_down': jax.random.normal(k[5], (DIM, HID), jnp.float32) * s}
    _L3_ffn_in = _L3_ffn_setup()
    _d = {'L0_attn_x': _L0_attn_in['x'], 'L0_attn_input_norm_w': _L0_attn_in['input_norm_w'], 'L0_attn_a_log': _L0_attn_in['a_log'], 'L0_attn_c_out': _L0_attn_in['c_out'], 'L0_attn_d_skip': _L0_attn_in['d_skip'], 'L0_attn_ff_norm_w': _L0_attn_in['ff_norm_w'], 'L0_attn_ff_fc_w': _L0_attn_in['ff_fc_w'], 'L0_attn_ff_proj_w': _L0_attn_in['ff_proj_w'], 'L0_ffn_gate_w': _L0_ffn_in['gate_w'], 'L0_ffn_gate_b': _L0_ffn_in['gate_b'], 'L0_ffn_w1': _L0_ffn_in['w1'], 'L0_ffn_b1': _L0_ffn_in['b1'], 'L0_ffn_w3': _L0_ffn_in['w3'], 'L0_ffn_b3': _L0_ffn_in['b3'], 'L0_ffn_w2': _L0_ffn_in['w2'], 'L0_ffn_b2': _L0_ffn_in['b2'], 'L0_ffn_sw1': _L0_ffn_in['sw1'], 'L0_ffn_sb1': _L0_ffn_in['sb1'], 'L0_ffn_sw3': _L0_ffn_in['sw3'], 'L0_ffn_sb3': _L0_ffn_in['sb3'], 'L0_ffn_sw2': _L0_ffn_in['sw2'], 'L0_ffn_sb2': _L0_ffn_in['sb2'], 'L1_attn_norm1_w': _L1_attn_in['norm1_w'], 'L1_attn_norm2_w': _L1_attn_in['norm2_w'], 'L1_attn_g_wq': _L1_attn_in['g_wq'], 'L1_attn_g_kv_down': _L1_attn_in['g_kv_down'], 'L1_attn_g_k_up': _L1_attn_in['g_k_up'], 'L1_attn_g_v_up': _L1_attn_in['g_v_up'], 'L1_attn_g_wo': _L1_attn_in['g_wo'], 'L1_attn_l_wq': _L1_attn_in['l_wq'], 'L1_attn_l_wk': _L1_attn_in['l_wk'], 'L1_attn_l_wv': _L1_attn_in['l_wv'], 'L1_attn_l_wo': _L1_attn_in['l_wo'], 'L1_ffn_ln1_w': _L1_ffn_in['ln1_w'], 'L1_ffn_ln1_b': _L1_ffn_in['ln1_b'], 'L1_ffn_ln2_w': _L1_ffn_in['ln2_w'], 'L1_ffn_ln2_b': _L1_ffn_in['ln2_b'], 'L1_ffn_wq': _L1_ffn_in['wq'], 'L1_ffn_wk': _L1_ffn_in['wk'], 'L1_ffn_wv': _L1_ffn_in['wv'], 'L1_ffn_wo': _L1_ffn_in['wo'], 'L1_ffn_bq': _L1_ffn_in['bq'], 'L1_ffn_bk': _L1_ffn_in['bk'], 'L1_ffn_bv': _L1_ffn_in['bv'], 'L1_ffn_bo': _L1_ffn_in['bo'], 'L1_ffn_gate_w': _L1_ffn_in['gate_w'], 'L1_ffn_gate_b': _L1_ffn_in['gate_b'], 'L1_ffn_e_w1': _L1_ffn_in['e_w1'], 'L1_ffn_e_b1': _L1_ffn_in['e_b1'], 'L1_ffn_e_w2': _L1_ffn_in['e_w2'], 'L1_ffn_e_b2': _L1_ffn_in['e_b2'], 'L2_attn_Wq': _L2_attn_in['Wq'], 'L2_attn_Wk': _L2_attn_in['Wk'], 'L2_attn_Wv': _L2_attn_in['Wv'], 'L2_attn_Wo': _L2_attn_in['Wo'], 'L2_attn_q_gain': _L2_attn_in['q_gain'], 'L2_attn_pair_mix': _L2_attn_in['pair_mix'], 'L2_ffn_gate_w': _L2_ffn_in['gate_w'], 'L2_ffn_gate_b': _L2_ffn_in['gate_b'], 'L2_ffn_expert_w': _L2_ffn_in['expert_w'], 'L2_ffn_expert_b': _L2_ffn_in['expert_b'], 'L3_attn_Wq': _L3_attn_in['Wq'], 'L3_attn_Wk': _L3_attn_in['Wk'], 'L3_attn_Wv': _L3_attn_in['Wv'], 'L3_attn_Wf1': _L3_attn_in['Wf1'], 'L3_attn_Wf2': _L3_attn_in['Wf2'], 'L3_attn_Wg1': _L3_attn_in['Wg1'], 'L3_attn_Wg2': _L3_attn_in['Wg2'], 'L3_attn_Wo': _L3_attn_in['Wo'], 'L3_attn_norm_w': _L3_attn_in['norm_w'], 'L3_ffn_gate_w': _L3_ffn_in['gate_w'], 'L3_ffn_expert_bias': _L3_ffn_in['expert_bias'], 'L3_ffn_w_up': _L3_ffn_in['w_up'], 'L3_ffn_w_down': _L3_ffn_in['w_down'], 'L3_ffn_shared_w_up': _L3_ffn_in['shared_w_up'], 'L3_ffn_shared_w_down': _L3_ffn_in['shared_w_down']}
    _x0 = _d['L0_attn_x']
    _d['L0_attn_x'] = jax.random.normal(jax.random.fold_in(jax.random.key(seed), 1), (8, 256, 128), dtype=_x0.dtype)
    del _x0
    return _d

def reference(L0_attn_x, L0_attn_input_norm_w, L0_attn_a_log, L0_attn_c_out, L0_attn_d_skip, L0_attn_ff_norm_w, L0_attn_ff_fc_w, L0_attn_ff_proj_w, L0_ffn_gate_w, L0_ffn_gate_b, L0_ffn_w1, L0_ffn_b1, L0_ffn_w3, L0_ffn_b3, L0_ffn_w2, L0_ffn_b2, L0_ffn_sw1, L0_ffn_sb1, L0_ffn_sw3, L0_ffn_sb3, L0_ffn_sw2, L0_ffn_sb2, L1_attn_norm1_w, L1_attn_norm2_w, L1_attn_g_wq, L1_attn_g_kv_down, L1_attn_g_k_up, L1_attn_g_v_up, L1_attn_g_wo, L1_attn_l_wq, L1_attn_l_wk, L1_attn_l_wv, L1_attn_l_wo, L1_ffn_ln1_w, L1_ffn_ln1_b, L1_ffn_ln2_w, L1_ffn_ln2_b, L1_ffn_wq, L1_ffn_wk, L1_ffn_wv, L1_ffn_wo, L1_ffn_bq, L1_ffn_bk, L1_ffn_bv, L1_ffn_bo, L1_ffn_gate_w, L1_ffn_gate_b, L1_ffn_e_w1, L1_ffn_e_b1, L1_ffn_e_w2, L1_ffn_e_b2, L2_attn_Wq, L2_attn_Wk, L2_attn_Wv, L2_attn_Wo, L2_attn_q_gain, L2_attn_pair_mix, L2_ffn_gate_w, L2_ffn_gate_b, L2_ffn_expert_w, L2_ffn_expert_b, L3_attn_Wq, L3_attn_Wk, L3_attn_Wv, L3_attn_Wf1, L3_attn_Wf2, L3_attn_Wg1, L3_attn_Wg2, L3_attn_Wo, L3_attn_norm_w, L3_ffn_gate_w, L3_ffn_expert_bias, L3_ffn_w_up, L3_ffn_w_down, L3_ffn_shared_w_up, L3_ffn_shared_w_down):

    def _L0_attn_ref(x, input_norm_w, a_log, c_out, d_skip, ff_norm_w, ff_fc_w, ff_proj_w):
        import jax, jax.numpy as jnp
        import numpy as np
        EPS = 1e-06

        def _rmsnorm(z, w):
            zf = z.astype(jnp.float32)
            zn = zf * jax.lax.rsqrt(jnp.mean(zf * zf, axis=-1, keepdims=True) + EPS)
            return zn.astype(z.dtype) * w
        normed = _rmsnorm(x, input_norm_w)
        a = jnp.exp(-jnp.exp(a_log))
        A = jnp.broadcast_to(a, normed.shape)

        def combine(e1, e2):
            a1, b1 = e1
            a2, b2 = e2
            return (a1 * a2, a2 * b1 + b2)
        _, h = jax.lax.associative_scan(combine, (A, normed), axis=1)
        scan_out = h * c_out + normed * d_skip
        x1 = x + scan_out
        n2 = _rmsnorm(x1, ff_norm_w)
        hidden = jax.nn.silu(jnp.einsum('btd,hd->bth', n2, ff_fc_w))
        ff_out = jnp.einsum('bth,dh->btd', hidden, ff_proj_w)
        return x1 + ff_out

    def _L0_ffn_ref(x, gate_w, gate_b, w1, b1, w3, b3, w2, b2, sw1, sb1, sw3, sb3, sw2, sb2):
        import jax, jax.numpy as jnp
        import numpy as np
        E = 8
        TOP_K = 2
        ROUTE_SCALE = 1.0
        ALPHA = 1.702
        LIMIT = 7.0
        D = 128
        F = 128
        B, S = (2, 128)

        def swiglu(h):
            g = jnp.minimum(h[..., ::2], LIMIT)
            l = jnp.clip(h[..., 1::2], -LIMIT, LIMIT)
            return g * jax.nn.sigmoid(ALPHA * g) * (l + 1.0)
        if __name__ == '__main__':
            out = reference(**setup_inputs())
            print(out.shape, out.dtype)
        inp_shape = x.shape
        xt = x.reshape(-1, D)
        logits = xt @ gate_w.T
        scores = jax.nn.softmax(logits.astype(jnp.float32), axis=-1)
        biased = scores + gate_b.astype(jnp.float32)
        idx = jax.lax.top_k(biased, TOP_K)[1]
        weights = (jnp.take_along_axis(scores, idx, axis=-1) * ROUTE_SCALE).astype(x.dtype)
        cw = jnp.sum(jax.nn.one_hot(idx, E, dtype=x.dtype) * weights[..., None], axis=1)
        h1 = jnp.einsum('td,efd->etf', xt, w1) + b1[:, None, :]
        h3 = jnp.einsum('td,efd->etf', xt, w3) + b3[:, None, :]
        a = swiglu(h1 * h3)
        y = jnp.einsum('etf,edf->etd', a, w2) + b2[:, None, :]
        routed = jnp.einsum('te,etd->td', cw, y)
        sh = swiglu((xt @ sw1.T + sb1) * (xt @ sw3.T + sb3))
        shared = sh @ sw2.T + sb2
        return (routed + shared).reshape(inp_shape)

    def _L1_attn_ref(hidden, norm1_w, norm2_w, g_wq, g_kv_down, g_k_up, g_v_up, g_wo, l_wq, l_wk, l_wv, l_wo):
        import jax, jax.numpy as jnp
        import numpy as np
        D = 128
        H = 16
        KVH = 4
        HD = D // H
        LAT = 32
        WIN = 32
        B, S = (1, 256)
        BASE_G, BASE_L = (1000000.0, 10000.0)
        EPS = 1e-06

        def rmsnorm(x, w):
            return x * jax.lax.rsqrt(jnp.mean(x * x, axis=-1, keepdims=True) + EPS) * w

        def qk_norm(x):
            return x * jax.lax.rsqrt(jnp.mean(x * x, axis=-1, keepdims=True) + EPS)

        def rope(x, base):
            s, hd = (x.shape[-2], x.shape[-1])
            inv_freq = 1.0 / base ** (jnp.arange(0, hd, 2, dtype=jnp.float32) / hd)
            freqs = jnp.arange(s, dtype=jnp.float32)[:, None] * inv_freq[None, :]
            cos, sin = (jnp.cos(freqs), jnp.sin(freqs))
            xe, xo = (x[..., ::2], x[..., 1::2])
            out = jnp.stack([xe * cos - xo * sin, xe * sin + xo * cos], axis=-1)
            return out.reshape(x.shape)

        def split_heads(x, n_heads):
            b, s, _ = x.shape
            return x.reshape(b, s, n_heads, HD).transpose(0, 2, 1, 3)

        def repeat_kv(x):
            return jnp.repeat(x, H // KVH, axis=1)

        def sdpa(q, k, v, mask):
            scores = jnp.einsum('bhqd,bhkd->bhqk', q, k) / np.sqrt(HD).astype(np.float32)
            scores = jnp.where(mask, scores, jnp.float32(-1e+30))
            probs = jax.nn.softmax(scores, axis=-1)
            return jnp.einsum('bhqk,bhkd->bhqd', probs, v)

        def merge_heads(x):
            b, h, s, hd = x.shape
            return x.transpose(0, 2, 1, 3).reshape(b, s, h * hd)

        def global_latent_attn(x, wq, w_kv_down, w_k_up, w_v_up, wo):
            q = split_heads(x @ wq, H)
            latent = x @ w_kv_down
            k = split_heads(latent @ w_k_up, KVH)
            v = split_heads(latent @ w_v_up, KVH)
            q, k = (rope(q, BASE_G), rope(k, BASE_G))
            q, k = (qk_norm(q), qk_norm(k))
            k, v = (repeat_kv(k), repeat_kv(v))
            i = jnp.arange(x.shape[1])
            causal = i[:, None] >= i[None, :]
            return merge_heads(sdpa(q, k, v, causal)) @ wo

        def local_gqa_attn(x, wq, wk, wv, wo):
            q = split_heads(x @ wq, H)
            k = split_heads(x @ wk, KVH)
            v = split_heads(x @ wv, KVH)
            q, k = (rope(q, BASE_L), rope(k, BASE_L))
            q, k = (qk_norm(q), qk_norm(k))
            k, v = (repeat_kv(k), repeat_kv(v))
            i = jnp.arange(x.shape[1])
            diff = i[:, None] - i[None, :]
            mask = (diff >= 0) & (diff < WIN)
            return merge_heads(sdpa(q, k, v, mask)) @ wo
        x = hidden
        x = x + global_latent_attn(rmsnorm(x, norm1_w), g_wq, g_kv_down, g_k_up, g_v_up, g_wo)
        x = x + local_gqa_attn(rmsnorm(x, norm2_w), l_wq, l_wk, l_wv, l_wo)
        return x

    def _L1_ffn_ref(x, ln1_w, ln1_b, ln2_w, ln2_b, wq, wk, wv, wo, bq, bk, bv, bo, gate_w, gate_b, e_w1, e_b1, e_w2, e_b2):
        import jax, jax.numpy as jnp
        import numpy as np
        B, S, D, H, L, E, K = (4, 128, 128, 16, 2, 8, 2)
        DFF = 4 * D

        def _ln(x, w, b):
            m = x.mean(-1, keepdims=True)
            v = x.var(-1, keepdims=True)
            return (x - m) / jnp.sqrt(v + 1e-05) * w + b

        def _attn(x, wq, wk, wv, wo, bq, bk, bv, bo):
            Bb, T, C = x.shape
            hd = C // H
            q = (x @ wq + bq).reshape(Bb, T, H, hd).transpose(0, 2, 1, 3)
            k = (x @ wk + bk).reshape(Bb, T, H, hd).transpose(0, 2, 1, 3)
            v = (x @ wv + bv).reshape(Bb, T, H, hd).transpose(0, 2, 1, 3)
            att = jnp.einsum('bhqd,bhkd->bhqk', q, k) * hd ** (-0.5)
            causal = jnp.tril(jnp.ones((T, T), bool))
            att = jnp.where(causal, att, -jnp.inf)
            att = jax.nn.softmax(att, axis=-1)
            y = jnp.einsum('bhqk,bhkd->bhqd', att, v).transpose(0, 2, 1, 3).reshape(Bb, T, C)
            return y @ wo + bo

        def _ffn(h, w1, b1, w2, b2):
            return jax.nn.gelu(h @ w1 + b1, approximate=False) @ w2 + b2

        def _combine_weights(logits):
            vals, idx = jax.lax.top_k(logits, K)
            w = jax.nn.softmax(vals, axis=-1)
            onehot = (idx[..., None] == jnp.arange(E)).astype(w.dtype)
            return jnp.sum(w[..., None] * onehot, axis=-2)

        def _token_moe(h, gw, gb, w1, b1, w2, b2):
            cw = _combine_weights(h @ gw + gb)
            out = jnp.zeros_like(h)
            for e in range(E):
                out = out + _ffn(h, w1[e], b1[e], w2[e], b2[e]) * cw[..., e:e + 1]
            return out

        def _seq_moe(h, gw, gb, w1, b1, w2, b2):
            cw = _combine_weights(h.mean(axis=1) @ gw + gb)
            out = jnp.zeros_like(h)
            for e in range(E):
                out = out + _ffn(h, w1[e], b1[e], w2[e], b2[e]) * cw[:, e, None, None]
            return out
        for l in range(L):
            x = x + _attn(_ln(x, ln1_w[l], ln1_b[l]), wq[l], wk[l], wv[l], wo[l], bq[l], bk[l], bv[l], bo[l])
            h = _ln(x, ln2_w[l], ln2_b[l])
            moe = _token_moe if l % 2 == 0 else _seq_moe
            x = x + moe(h, gate_w[l], gate_b[l], e_w1[l], e_b1[l], e_w2[l], e_b2[l])
        return x

    def _L2_attn_ref(x, Wq, Wk, Wv, Wo, q_gain, pair_mix):
        import jax, jax.numpy as jnp
        import numpy as np
        import math
        B, S, DIM = (2, 256, 128)
        H, KVH = (16, 4)
        HD = DIM // H
        WINDOW = 32
        ROPE_BASE = 10000.0
        EPS = 1e-06

        def _rms_norm(v):
            return v * jax.lax.rsqrt(jnp.mean(v * v, axis=-1, keepdims=True) + EPS)

        def _rope_tables(seqlen, dtype):
            inv_freq = 1.0 / ROPE_BASE ** (jnp.arange(0, HD, 2, dtype=jnp.float32) / HD)
            t = jnp.arange(seqlen, dtype=jnp.float32)
            freqs = jnp.outer(t, inv_freq)
            return (jnp.cos(freqs).astype(dtype)[None, None], jnp.sin(freqs).astype(dtype)[None, None])

        def _apply_rotary(v, cos, sin):
            half = v.shape[-1] // 2
            v1, v2 = (v[..., :half], v[..., half:])
            return jnp.concatenate((v1 * cos + v2 * sin, -v1 * sin + v2 * cos), axis=-1)
        bsz, seqlen, dim = x.shape
        q = (x @ Wq.T).reshape(bsz, seqlen, H, HD).transpose(0, 2, 1, 3)
        k = (x @ Wk.T).reshape(bsz, seqlen, KVH, HD).transpose(0, 2, 1, 3)
        v = (x @ Wv.T).reshape(bsz, seqlen, KVH, HD).transpose(0, 2, 1, 3)
        q = _rms_norm(q)
        k = _rms_norm(k)
        cos, sin = _rope_tables(seqlen, q.dtype)
        q = _apply_rotary(q, cos, sin)
        k = _apply_rotary(k, cos, sin)
        q = q * q_gain.astype(q.dtype)[None, :, None, None]
        rep = H // KVH
        k_full = jnp.repeat(k, rep, axis=1)
        v_full = jnp.repeat(v, rep, axis=1)
        pos = jnp.arange(seqlen)
        mask = (pos[:, None] >= pos[None, :]) & (pos[:, None] - pos[None, :] < WINDOW)
        scale = 1.0 / math.sqrt(HD)
        scores = jnp.einsum('bhqd,bhkd->bhqk', q, k_full) * scale
        scores = jnp.where(mask[None, None], scores, jnp.finfo(scores.dtype).min)
        att = jax.nn.softmax(scores, axis=-1)
        y = jnp.einsum('bhqk,bhkd->bhqd', att, v_full)
        yp = y.reshape(bsz, H // 2, 2, seqlen, HD)
        y = jnp.einsum('bpitd,poi->bpotd', yp, pair_mix.astype(y.dtype)).reshape(bsz, H, seqlen, HD)
        out = y.transpose(0, 2, 1, 3).reshape(bsz, seqlen, dim) @ Wo.T
        return out

    def _L2_ffn_ref(x, gate_w, gate_b, expert_w, expert_b):
        import jax, jax.numpy as jnp
        import numpy as np
        TOP_K = 2
        gates = jax.nn.softmax(jnp.einsum('bsh,eh->bse', x, gate_w) + gate_b, axis=-1)
        top_gates, top_idx = jax.lax.top_k(gates, TOP_K)
        expert_out = jnp.einsum('bsh,eoh->bseo', x, expert_w) + expert_b
        selected = jnp.take_along_axis(expert_out, top_idx[..., None], axis=2)
        return (selected * top_gates[..., None]).sum(axis=2)

    def _L3_attn_ref(x, Wq, Wk, Wv, Wf1, Wf2, Wg1, Wg2, Wo, norm_w):
        import jax, jax.numpy as jnp
        import numpy as np
        B, N, D = (2, 256, 128)
        H, M = (8, 64)
        DK = D // H
        EPS = 1e-05

        def _gsa(q, k, v, s, g):
            b = q.shape[1]

            def step1(hk, t):
                q_t, k_t, s_t, g_t = t
                hk = hk * jnp.exp(g_t)[:, :, None, :] + k_t[..., :, None] * s_t[..., None, :]
                ok = jnp.einsum('bhk,bhkm->bhm', q_t, hk)
                return (hk, ok)
            hk0 = jnp.zeros((b, H, DK, M), q.dtype)
            _, ok = jax.lax.scan(step1, hk0, (q, k, s, g))
            qv = jax.nn.softmax(ok, axis=-1)

            def step2(hv, t):
                qv_t, s_t, v_t, g_t = t
                hv = hv * jnp.exp(g_t)[..., :, None] + s_t[..., :, None] * v_t[..., None, :]
                ov = jnp.einsum('bhm,bhmv->bhv', qv_t, hv)
                return (hv, ov)
            hv0 = jnp.zeros((b, H, M, DK), q.dtype)
            _, ov = jax.lax.scan(step2, hv0, (qv, s, v, g))
            return ov
        b, n, d = x.shape
        q = jax.nn.silu(x @ Wq).reshape(b, n, H, DK)
        k = jax.nn.silu(x @ Wk).reshape(b, n, H, DK)
        v = (x @ Wv).reshape(b, n, H, DK)
        f = x @ Wf1 @ Wf2
        log_f = jax.nn.log_sigmoid(f).reshape(b, n, H, M)
        s = 1.0 - jnp.exp(log_f)
        tm = lambda a: jnp.swapaxes(a, 0, 1)
        ov = _gsa(tm(q), tm(k), tm(v), tm(s), tm(log_f))
        out = tm(ov).reshape(b, n, d)
        gate = x @ Wg1 @ Wg2
        out = out * jax.nn.sigmoid(gate)
        og = out.reshape(b, n, H, DK)
        og = og * jax.lax.rsqrt(jnp.mean(og * og, axis=-1, keepdims=True) + EPS)
        out = og.reshape(b, n, d) * norm_w
        return out @ Wo

    def _L3_ffn_ref(x, gate_w, expert_bias, w_up, w_down, shared_w_up, shared_w_down):
        import jax, jax.numpy as jnp
        import numpy as np
        BS, SLEN, DIM = (1, 256, 128)
        NUM_EXPERTS, TOP_K = (8, 2)
        HID = 176

        def _masked_grouped_mm(x, w, onehot):
            g = jnp.einsum('tk,gnk->tgn', x, w, preferred_element_type=jnp.float32)
            return jnp.einsum('tgn,tg->tn', g, onehot)

        def moe_forward(x, gate_w, expert_bias, w_up, w_down, shared_w_up, shared_w_down):
            bs, slen, dim = x.shape
            xf = x.reshape(-1, dim)
            scores = jax.nn.sigmoid((xf @ gate_w.T).astype(jnp.float32))
            biased = scores + expert_bias
            _, sel = jax.lax.top_k(biased, TOP_K)
            top_scores = jnp.take_along_axis(scores, sel, axis=-1)
            flat_sel = sel.reshape(-1)
            counts = jnp.bincount(flat_sel, length=NUM_EXPERTS)
            order = jnp.argsort(flat_sel, stable=True)
            scores_sorted = top_scores.reshape(-1)[order]
            token_ids = order // TOP_K
            routed_in = (xf[token_ids] * scores_sorted[:, None]).astype(x.dtype)
            seg = jnp.repeat(jnp.arange(NUM_EXPERTS), counts, total_repeat_length=flat_sel.shape[0])
            onehot = jax.nn.one_hot(seg, NUM_EXPERTS, dtype=jnp.float32)
            h = _masked_grouped_mm(routed_in.astype(jnp.bfloat16), w_up.astype(jnp.bfloat16), onehot)
            h = jnp.square(jax.nn.relu(h.astype(jnp.bfloat16)))
            routed_out = _masked_grouped_mm(h.astype(jnp.bfloat16), w_down.astype(jnp.bfloat16), onehot)
            routed_out = routed_out.astype(jnp.bfloat16).astype(x.dtype)
            hs = jnp.square(jax.nn.relu(xf @ shared_w_up.T))
            shared_out = hs @ shared_w_down.T
            combined = jnp.zeros((flat_sel.shape[0], dim), routed_out.dtype).at[order].set(routed_out)
            out = combined.reshape(-1, TOP_K, dim).sum(axis=1) + shared_out
            return out.reshape(bs, slen, dim)
        return moe_forward(x, gate_w, expert_bias, w_up, w_down, shared_w_up, shared_w_down)
    x = L0_attn_x
    x = x + _layernorm(_L0_attn_ref(_layernorm(x, axis=-1), L0_attn_input_norm_w, L0_attn_a_log, L0_attn_c_out, L0_attn_d_skip, L0_attn_ff_norm_w, L0_attn_ff_fc_w, L0_attn_ff_proj_w), axis=-1)
    x = x + _layernorm(_L0_ffn_ref(_layernorm(x, axis=-1), L0_ffn_gate_w, L0_ffn_gate_b, L0_ffn_w1, L0_ffn_b1, L0_ffn_w3, L0_ffn_b3, L0_ffn_w2, L0_ffn_b2, L0_ffn_sw1, L0_ffn_sb1, L0_ffn_sw3, L0_ffn_sb3, L0_ffn_sw2, L0_ffn_sb2), axis=-1)
    x = x + _layernorm(_L1_attn_ref(_layernorm(x, axis=-1), L1_attn_norm1_w, L1_attn_norm2_w, L1_attn_g_wq, L1_attn_g_kv_down, L1_attn_g_k_up, L1_attn_g_v_up, L1_attn_g_wo, L1_attn_l_wq, L1_attn_l_wk, L1_attn_l_wv, L1_attn_l_wo), axis=-1)
    x = x + _layernorm(_L1_ffn_ref(_layernorm(x, axis=-1), L1_ffn_ln1_w, L1_ffn_ln1_b, L1_ffn_ln2_w, L1_ffn_ln2_b, L1_ffn_wq, L1_ffn_wk, L1_ffn_wv, L1_ffn_wo, L1_ffn_bq, L1_ffn_bk, L1_ffn_bv, L1_ffn_bo, L1_ffn_gate_w, L1_ffn_gate_b, L1_ffn_e_w1, L1_ffn_e_b1, L1_ffn_e_w2, L1_ffn_e_b2), axis=-1)
    x = x + _layernorm(_L2_attn_ref(_layernorm(x, axis=-1), L2_attn_Wq, L2_attn_Wk, L2_attn_Wv, L2_attn_Wo, L2_attn_q_gain, L2_attn_pair_mix), axis=-1)
    x = x + _layernorm(_L2_ffn_ref(_layernorm(x, axis=-1), L2_ffn_gate_w, L2_ffn_gate_b, L2_ffn_expert_w, L2_ffn_expert_b), axis=-1)
    x = x + _layernorm(_L3_attn_ref(_layernorm(x, axis=-1), L3_attn_Wq, L3_attn_Wk, L3_attn_Wv, L3_attn_Wf1, L3_attn_Wf2, L3_attn_Wg1, L3_attn_Wg2, L3_attn_Wo, L3_attn_norm_w), axis=-1)
    x = x + _layernorm(_L3_ffn_ref(_layernorm(x, axis=-1), L3_ffn_gate_w, L3_ffn_expert_bias, L3_ffn_w_up, L3_ffn_w_down, L3_ffn_shared_w_up, L3_ffn_shared_w_down), axis=-1)
    return x

_drawn_inputs = setup_inputs


def setup_inputs(seed=0):
    import zlib

    import numpy as np

    out = dict(_drawn_inputs(seed))
    spreads = {'L0_attn_input_norm_w': (1.0, 0.2),
     'L0_attn_ff_norm_w': (1.0, 0.6),
     'L1_attn_norm1_w': (1.0, 0.6),
     'L1_attn_norm2_w': (1.0, 0.6),
     'L1_ffn_ln1_w': (1.0, 0.6),
     'L1_ffn_ln1_b': (0.0, 0.655),
     'L1_ffn_ln2_w': (1.0, 0.6),
     'L1_ffn_ln2_b': (0.0, 0.1),
     'L1_ffn_bq': (0.0, 0.8),
     'L1_ffn_bk': (0.0, 0.8),
     'L1_ffn_bv': (0.0, 0.363),
     'L1_ffn_bo': (0.0, 0.1),
     'L1_ffn_gate_b': (0.0, 0.1),
     'L1_ffn_e_b1': (0.0, 0.311),
     'L1_ffn_e_b2': (0.0, 0.1),
     'L2_attn_q_gain': (1.0, 0.2),
     'L2_ffn_gate_b': (0.0, 0.1),
     'L2_ffn_expert_b': (0.0, 0.321),
     'L3_attn_norm_w': (1.0, 0.2),
     'L3_ffn_expert_bias': (0.0, 0.1)}
    factors = {'L0_ffn_b1': 5.207,
     'L0_ffn_b3': 5.865,
     'L0_ffn_b2': 5.88,
     'L0_ffn_sb1': 3.403,
     'L0_ffn_sb3': 3.833,
     'L0_ffn_sb2': 3.429,
     'L1_attn_g_wq': 8.0,
     'L1_attn_g_kv_down': 8.0,
     'L1_attn_g_k_up': 8.0,
     'L1_attn_g_v_up': 7.944,
     'L1_attn_g_wo': 8.0,
     'L1_attn_l_wq': 4.894,
     'L1_attn_l_wk': 5.121,
     'L1_attn_l_wv': 4.382,
     'L1_attn_l_wo': 3.95,
     'L1_ffn_wq': 8.0,
     'L1_ffn_wk': 8.0,
     'L1_ffn_wv': 3.625,
     'L3_attn_Wq': 8.0,
     'L3_attn_Wk': 8.0,
     'L3_attn_Wf1': 8.0,
     'L3_attn_Wf2': 8.0,
     'L3_attn_Wg1': 8.0,
     'L3_attn_Wg2': 8.0}
    for name, (base, spread) in spreads.items():
        noise = np.random.default_rng([zlib.crc32(name.encode()), seed]).standard_normal(out[name].shape)
        drawn = base * np.exp(spread * noise) if base else spread * noise
        out[name] = jnp.asarray(drawn.astype(out[name].dtype))
    for name, factor in factors.items():
        out[name] = (out[name] * factor).astype(out[name].dtype)
    return out
```

```python
from contextlib import ExitStack

import numpy as np

import concourse.bass as bass
from concourse import mybir

ACT = mybir.ActivationFunctionType
ALU = mybir.AluOpType
AX = mybir.AxisListType
F32 = mybir.dt.float32
BF16 = mybir.dt.bfloat16
U32 = mybir.dt.uint32

P = 128
SEQ = 256
PAIR = 2
NT = PAIR * SEQ // P
TOK = NT * P
TPS = SEQ // P
HEADS = 16
HD = P // HEADS
NS = 4
NI = HEADS // NS
WINDOW = 32
E = 8
MASKED = -1e30
LN_EPS = 1e-5
RMS_EPS = 1e-6


MASKS = ("mask_qk", "mask_kq", "lmask_qk", "lmask_kq")
IN_BF16 = ("L3f_up", "L3f_dnA", "L3f_dnB") + MASKS


class Chain:

    def __init__(self, eng, sem):
        self.eng, self.sem, self.n = eng, sem, 0

    def link(self, ins):
        self.n += 1
        ins.then_inc(self.sem, 1)
        self.eng.wait_ge(self.sem, self.n)


class Stage:

    def __init__(self, nc, pool, names):
        self.nc, self.sems = nc, pool[:len(names.split())]
        assert len(self.sems) == len(names.split())

    def __enter__(self):
        self.block = self.nc.Block()
        return [self.block.__enter__()] + self.sems

    def __exit__(self, *exc):
        self.block.__exit__(*exc)
        if exc[0] is None:
            self.nc.all_engine_barrier(sems_to_clear=range(self.sems[0].num, self.sems[-1].num + 1))


def bc(ap, shape):
    return ap.broadcast_to(shape)


class Net:
    def __init__(self, nc, ctx, w_dram):
        self.nc = nc
        self.sems = [ctx.enter_context(nc.semaphore(f"signal{i}")) for i in range(16)]
        assert [s.num for s in self.sems] == list(range(self.sems[0].num, self.sems[0].num + 16))

        def sb(name, shape, dt=F32):
            return ctx.enter_context(nc.sbuf_tensor(name, shape, dt))

        self.sb = sb
        self.w_dram = w_dram
        self.w = {n: sb("w_" + n, list(a.shape)) for n, a in w_dram.items() if n not in IN_BF16}
        self.PS = ctx.enter_context(nc.psum_tensor("PS", [P, 8, 512], F32))
        self.X = sb("X", [P, NT, P])
        self.U = sb("U", [P, NT, P])
        self.V = sb("V", [P, NT, P])
        self.Y = sb("Y", [P, NT, P])
        self.R = sb("R", [P, NT, P])
        self.UT = sb("UT", [P, TOK])
        self.RT = sb("RT", [P, TOK])
        self.ident_bf = sb("ident_bf", [P, P], BF16)
        self.mask_bf = {n: sb("bf_" + n, list(w_dram[n].shape), BF16)
                        for n in MASKS}
        self.stats = sb("stats", [P, NT, 6])
        self.mv = sb("mv", [P, NT, 2])
        self.m2 = sb("m2", [P, NT, 1])
        self.sd = sb("sd", [P, NT, 1])
        self.rs = sb("rs", [P, NT, 1])
        self.cw = sb("cw", [P, NT, E + 1])
        self.cwT = sb("cwT", [E + 1, TOK])
        self.g = [sb(f"gate{i}", [P, NT, E]) for i in range(6)]
        self.g1 = [sb(f"gate_row{i}", [P, NT, 1]) for i in range(3)]
        self.gidx = sb("gidx", [P, NT, E], U32)
        self.hm = sb("hm", [P, PAIR])
        self.hmb = sb("hmb", [P, PAIR, P])
        self.qtok = sb("qtok", [P, NT, HEADS, HD])
        self.ktok = sb("ktok", [P, NT, HEADS, HD])
        self.vaug = sb("vaug", [P, NT, HEADS, HD + 1])
        tmps = sb("tmps", [P, 4, TOK])
        self.tmp = [tmps[:, i, :].rearrange("p (t h d) -> p t h d", t=NT, h=HEADS) for i in range(4)]
        self.osb = tmps[:].rearrange("p a b -> p (a b)")[:, 0:NT * HEADS * (HD + 1)].rearrange(
            "p (t h d) -> p t h d", t=NT, h=HEADS)
        self.ss = sb("ss", [P, NT, 2 * HEADS])
        self.qT = sb("qT", [P, TOK])
        self.kT = sb("kT", [P, NI, TOK])
        self.negm = sb("negm", [P, NT, P])
        self.mT = sb("mT", [P, TOK])
        self.latT = sb("latT", [32, TOK])
        self.big = sb("big", [P, 8, 512])
        self.orec = sb("orec", [P, NT, HEADS])
        self.acc = self.Y
        self.g_q, self.g_k, self.g_v, self.g_dk = (self.kT[:, i, :] for i in range(4))
        self.g_dv = self.qT[:]
        self.g_f1, self.g_g1 = self.mT[0:16, :], self.latT[0:16, :]
        self.decay = sb("decay", [P, SEQ])
        self.kpad = self.big[:, 4:8, :].rearrange("p t (i c) -> p t i c", i=NI)
        flat = self.big[:].rearrange("p a b -> p (a b)")
        nu, nd = E * 176, E * P
        self.w["L3f_up"] = flat[:, 0:nu].rearrange("p (e h) -> p e h", e=E)
        self.w["L3f_dnA"] = flat[:, nu:nu + nd].rearrange("p (e d) -> p e d", e=E)
        self.w["L3f_dnB"] = flat[0:48, nu + nd:nu + 2 * nd].rearrange("p (e d) -> p e d", e=E)
        at = nu + 2 * nd
        for n in MASKS:
            self.w[n] = flat[:, at:at + w_dram[n].shape[1]]
            at += w_dram[n].shape[1]
        self.up_bf = sb("up_bf", [P, E, 176], BF16)
        self.dnA_bf = sb("dnA_bf", [P, E, P], BF16)
        self.dnB_bf = sb("dnB_bf", [48, E, P], BF16)

    def stage(self, tag, names):
        return Stage(self.nc, self.sems, names)


def load_weights(net):
    w, names = net.w, sorted(net.w)
    with net.stage("load", "loaded dve_chain act_chain") as (block, loaded, dve_chain, act_chain):
        @block.sync
        def _(sp):
            for n in names[0::2]:
                sp.dma_start(w[n][:], net.w_dram[n]).then_inc(loaded, 16)
            sp.wait_ge(loaded, 16 * len(names))

        @block.gpsimd
        def _(pool):
            pool.memset(net.vaug[:], 1.0)
            pool.memset(net.negm[:], 0.0)
            pool.memset(net.cw[:], 1.0)

        @block.vector
        def _(dve):
            dve.wait_ge(loaded, 16 * len(names))
            dve.tensor_copy(net.ident_bf[:], w["ident"][:])
            for n, m in net.mask_bf.items():
                dve.tensor_copy(m[:], w[n][:])
            dve.tensor_copy(net.up_bf[:], w["L3f_up"][:])
            dve.tensor_copy(net.dnA_bf[:], w["L3f_dnA"][:])
            dve.tensor_copy(net.dnB_bf[:], w["L3f_dnB"][:])
            dve.memset(net.decay[:], 0.0)

        @block.scalar
        def _(act):
            chain = Chain(act, act_chain)
            for n in names[1::2]:
                act.dma_start(w[n][:], net.w_dram[n]).then_inc(loaded, 16)
            act.wait_ge(loaded, 16 * len(names))
            chain.link(act.activation(w["L0a_alog"][:], w["L0a_alog"][:], ACT.Exp))
            chain.link(act.activation(w["L0a_alog"][:], w["L0a_alog"][:], ACT.Exp, scale=-1.0))
    with net.stage("decay", "dve_chain") as (block, dve_chain):
        @block.vector
        def _(dve):
            chain = Chain(dve, dve_chain)
            chain.link(dve.tensor_scalar(net.decay[:], net.decay[:], w["L0a_alog"][:, 0:1], None, ALU.add))


def norm(net, src, kind, tok=None, T=None, scale=None, bias=None, add_to=None):
    eps = net.w["eps"][:, 0:1] if kind == "ln" else net.w["eps"][:, 1:2]
    PS, w = net.PS, net.w
    tok = net.R if tok is None else tok
    with net.stage("norm", "var_ready sd_ready tok_ready turned T_ready dve_chain") as (
            block, var_ready, sd_ready, tok_ready, turned, T_ready, dve_chain):
        @block.vector
        def _(dve):
            chain = Chain(dve, dve_chain)
            for t in range(NT):
                last = dve.bn_stats(net.stats[:, t, :], src[:, t, :])
            chain.link(last)
            for t in range(NT):
                last = dve.bn_aggr(net.mv[:, t, :], net.stats[:, t, :])
            if kind == "rms":
                chain.link(last)
                chain.link(dve.tensor_tensor(net.m2[:], net.mv[:, :, 0:1], net.mv[:, :, 0:1], ALU.mult))
                last = dve.tensor_tensor(net.mv[:, :, 1:2], net.mv[:, :, 1:2], net.m2[:], ALU.add)
            last.then_inc(var_ready, 1)
            dve.wait_ge(sd_ready, 1)
            chain.link(dve.reciprocal(net.rs[:], net.sd[:]))
            for t in range(NT):
                if kind == "ln":
                    ins = dve.tensor_scalar(tok[:, t, :], src[:, t, :], net.mv[:, t, 0:1], net.rs[:, t, 0:1],
                                            ALU.subtract, ALU.mult)
                else:
                    ins = dve.tensor_scalar(tok[:, t, :], src[:, t, :], net.rs[:, t, 0:1], None, ALU.mult)
                ins.then_inc(tok_ready, 1)
            if add_to is not None:
                dve.wait_ge(tok_ready, NT)
                dve.tensor_tensor(add_to[:], add_to[:], tok[:], ALU.add)

        @block.scalar
        def _(act):
            act.wait_ge(var_ready, 1)
            act.activation(net.sd[:], net.mv[:, :, 1:2], ACT.Sqrt, bias=eps).then_inc(sd_ready, 1)
            if T is not None:
                act.wait_ge(turned, 1)
                act.activation(T[:], PS[:, 0, :], ACT.Identity, scale=1.0 if scale is None else scale,
                               bias=0.0 if bias is None else bias).then_inc(T_ready, 1)

        if T is not None:
            @block.tensor
            def _(pe):
                for t in range(NT):
                    pe.wait_ge(tok_ready, t + 1)
                    ins = pe.transpose(PS[:, 0, t * P:(t + 1) * P], tok[:, t, :], w["ident"][:])
                ins.then_inc(turned, 1)


def turn(net, src, T, scale=None):
    with net.stage("turn", "turned") as (block, turned):
        @block.tensor
        def _(pe):
            for t in range(NT):
                ins = pe.transpose(net.PS[:, 0, t * P:(t + 1) * P], src[:, t, :], net.w["ident"][:])
            ins.then_inc(turned, 1)

        @block.scalar
        def _(act):
            act.wait_ge(turned, 1)
            act.activation(T[:], net.PS[:, 0, :], ACT.Identity, scale=1.0 if scale is None else scale)


def l0_mixer(net):
    w, PS, big = net.w, net.PS, net.big
    norm(net, net.X, "ln", tok=net.U)
    norm(net, net.U, "rms", T=net.RT, scale=w["L0a_inw"][:, 0:1])
    scanT, skipT = big[:, 0, :], big[:, 1, :]
    with net.stage("l0scan", "mixed turned dve_chain") as (block, mixed, turned, dve_chain):
        @block.vector
        def _(dve):
            chain = Chain(dve, dve_chain)
            for b in range(PAIR):
                at = slice(b * SEQ, (b + 1) * SEQ)
                dve.tensor_tensor_scan(scanT[:, at], net.decay[:], net.RT[:, at], 0.0, ALU.mult, ALU.add)
            chain.link(dve.tensor_scalar(skipT, net.RT[:], w["L0a_dskip"][:, 0:1], None, ALU.mult))
            dve.scalar_tensor_tensor(out=scanT, in0=scanT, scalar=w["L0a_cout"][:, 0:1], in1=skipT,
                                     op0=ALU.mult, op1=ALU.add).then_inc(mixed, 1)
            dve.wait_ge(turned, 1)
            dve.tensor_tensor(net.V[:], PS[:, 0, :].rearrange("p (t d) -> p t d", t=NT), net.U[:], ALU.add)

        @block.tensor
        def _(pe):
            pe.wait_ge(mixed, 1)
            for t in range(NT):
                ins = pe.transpose(PS[:, 0, t * P:(t + 1) * P], scanT[:, t * P:(t + 1) * P], w["ident"][:])
            ins.then_inc(turned, 1)
    norm(net, net.V, "rms", T=net.RT, scale=w["L0a_ffw"][:, 0:1])
    with net.stage("l0mlp", "up hidden down") as (block, up, hidden, down):
        @block.tensor
        def _(pe):
            for f in range(2):
                pe.matmul(PS[:, f, :], w["L0a_fc"][:, f * P:(f + 1) * P], net.RT[:], start=True, stop=True).then_inc(up, 1)
            pe.wait_ge(hidden, 2)
            for t in range(NT):
                for f in range(2):
                    ins = pe.matmul(PS[:, 2, t * P:(t + 1) * P], big[:, f, t * P:(t + 1) * P], w["L0a_proj"][:, f, :],
                                    start=f == 0, stop=f == 1)
            ins.then_inc(down, 1)

        @block.scalar
        def _(act):
            for f in range(2):
                act.wait_ge(up, f + 1)
                act.activation(big[:, f, :], PS[:, f, :], ACT.Silu).then_inc(hidden, 1)

        @block.vector
        def _(dve):
            dve.wait_ge(down, 1)
            dve.tensor_tensor(net.Y[:], PS[:, 2, :].rearrange("p (t d) -> p t d", t=NT), net.V[:], ALU.add)
    norm(net, net.Y, "ln", add_to=net.X)


def route(net, mode, gate_w, logit_bias=None, select_bias=None, turn_weights=0, mean=False):
    w, PS = net.w, net.PS
    logits, ex, score, pick, sel0, sel1 = net.g
    top, total, rec = net.g1
    with net.stage("route", "mean_ready logits_ready centred exp_ready weights_ready turned dve_chain") as (
            block, mean_ready, logits_ready, centred, exp_ready, weights_ready, turned, dve_chain):
        @block.tensor
        def _(pe):
            if mean:
                pe.wait_ge(mean_ready, 1)
            for t in range(NT):
                rows = net.hmb[:, t // TPS, :] if mean else net.UT[:, t * P:(t + 1) * P]
                ins = pe.matmul(PS[:, 0, t * E:(t + 1) * E], rows, gate_w, start=True, stop=True)
            ins.then_inc(logits_ready, 1)
            if turn_weights:
                pe.wait_ge(weights_ready, 1)
                for t in range(NT):
                    ins = pe.transpose(PS[0:turn_weights, 1, t * P:(t + 1) * P], net.cw[:, t, 0:turn_weights], w["ident"][:])
                ins.then_inc(turned, 1)

        @block.scalar
        def _(act):
            act.wait_ge(centred, 1)
            act.activation(ex[:], logits[:], ACT.Sigmoid if mode == "sigmoid" else ACT.Exp).then_inc(exp_ready, 1)
            if turn_weights:
                act.wait_ge(turned, 1)
                act.activation(net.cwT[0:turn_weights, :], PS[0:turn_weights, 1, :], ACT.Identity)

        @block.vector
        def _(dve):
            chain = Chain(dve, dve_chain)
            if mean:
                chain.link(dve.tensor_reduce(net.hm[:], net.UT[:].rearrange("p (b s) -> p b s", b=PAIR), AX.X, ALU.add))
                chain.link(dve.tensor_scalar(net.hm[:], net.hm[:], 1.0 / SEQ, None, ALU.mult))
                for b in range(PAIR):
                    last = dve.tensor_scalar(net.hmb[:, b, :], w["zeros"][:], net.hm[:, b:b + 1], None, ALU.add)
                last.then_inc(mean_ready, 1)
            dve.wait_ge(logits_ready, 1)
            raw = PS[:, 0, 0:NT * E].rearrange("p (t e) -> p t e", t=NT)
            if logit_bias is not None:
                chain.link(dve.tensor_tensor(logits[:], raw, bc(logit_bias.unsqueeze(1), [P, NT, E]), ALU.add))
            else:
                chain.link(dve.tensor_copy(logits[:], raw))
            if mode == "sigmoid":
                last = dve.tensor_copy(sel0[:], logits[:])
            else:
                chain.link(dve.tensor_reduce(top[:], logits[:], AX.X, ALU.max))
                last = dve.tensor_tensor(logits[:], logits[:], bc(top[:], [P, NT, E]), ALU.subtract)
            last.then_inc(centred, 1)
            dve.wait_ge(exp_ready, 1)
            dve.wait_ge(centred, 1)
            if mode == "all":
                chain.link(dve.tensor_reduce(total[:], ex[:], AX.X, ALU.add))
                chain.link(dve.reciprocal(rec[:], total[:]))
                chain.link(dve.tensor_tensor(score[:], ex[:], bc(rec[:], [P, NT, E]), ALU.mult))
            else:
                chain.link(dve.tensor_copy(score[:], ex[:]))
            if select_bias is not None:
                chain.link(dve.tensor_tensor(pick[:], score[:], bc(select_bias.unsqueeze(1), [P, NT, E]), ALU.add))
            else:
                chain.link(dve.tensor_copy(pick[:], logits[:] if mode == "two" else score[:]))
            for t in range(NT):
                last = dve.max(sel0[:, t, :], pick[:, t, :])
            chain.link(last)
            for t in range(NT):
                last = dve.max_index(net.gidx[:, t, :], sel0[:, t, :], pick[:, t, :])
            chain.link(last)
            chain.link(dve.tensor_copy(pick[:], net.gidx[:]))
            places = bc(w["iota8"][:].unsqueeze(1), [P, NT, E])
            dve.tensor_tensor(sel0[:], places, bc(pick[:, :, 0:1], [P, NT, E]), ALU.is_equal)
            chain.link(dve.tensor_tensor(sel1[:], places, bc(pick[:, :, 1:2], [P, NT, E]), ALU.is_equal))
            chain.link(dve.tensor_tensor(sel0[:], sel0[:], sel1[:], ALU.add))
            last = dve.tensor_tensor(net.cw[:, :, 0:E], score[:], sel0[:], ALU.mult)
            if mode == "two":
                chain.link(last)
                chain.link(dve.tensor_reduce(total[:], net.cw[:, :, 0:E], AX.X, ALU.add))
                chain.link(dve.reciprocal(rec[:], total[:]))
                last = dve.tensor_tensor(net.cw[:, :, 0:E], net.cw[:, :, 0:E], bc(rec[:], [P, NT, E]), ALU.mult)
            last.then_inc(weights_ready, 1)


def weighted_biases(net, pe, rows, bank, biases, done):
    for t in range(NT):
        ins = pe.matmul(net.PS[:, bank, t * P:(t + 1) * P], net.cwT[0:rows, t * P:(t + 1) * P], biases, start=True, stop=True)
    ins.then_inc(done, 1)


def l0_experts(net):
    w, PS, big = net.w, net.PS, net.big
    norm(net, net.X, "ln", T=net.UT)
    route(net, "all", w["L0f_gate"][:], select_bias=w["L0f_gb"][:], turn_weights=E + 1)
    n = E + 1
    h1 = [big[:, i, :] for i in range(2)]
    prod = [big[:, 2 + i, :] for i in range(2)]
    gated, act_out = big[:, 4, :], [big[:, 6 + i, :] for i in range(2)]
    sig = big[:, 5, :]
    with net.stage("l0exp", "up h1_ready prod_ready gate_ready sig_ready lin_ready a_ready y_ready acc_ready bias_ready dve_chain") as (
            block, up, h1_ready, prod_ready, gate_ready, sig_ready, lin_ready, a_ready, y_ready, acc_ready, bias_ready, dve_chain):
        @block.tensor
        def _(pe):
            weighted_biases(net, pe, n, 7, w["L0f_b2"][:], bias_ready)

            def down(e):
                pe.wait_ge(a_ready, e + 1)
                if e == 1:
                    pe.wait_ge(acc_ready, 1)
                if e >= 2:
                    pe.wait_ge(acc_ready, e)
                for t in range(NT):
                    ins = pe.matmul(PS[:, 6 + e % 2, t * P:(t + 1) * P], act_out[e % 2][:, t * P:(t + 1) * P],
                                    w["L0f_w2"][:, e, :], start=True, stop=True)
                ins.then_inc(y_ready, 1)

            for e in range(n):
                for half in range(2):
                    u = 2 * e + half
                    b = 2 * (u % 3)
                    if u >= 3:
                        pe.wait_ge(h1_ready, u - 2)
                        pe.wait_ge(prod_ready, u - 2)
                    pe.matmul(PS[:, b, :], w["L0f_w1"][:, e, half, :], net.UT[:], start=True, stop=True)
                    pe.matmul(PS[:, b + 1, :], w["L0f_w3"][:, e, half, :], net.UT[:], start=True, stop=True).then_inc(up, 1)
                if e >= 1:
                    down(e - 1)
            down(n - 1)

        @block.scalar
        def _(act):
            for u in range(2 * n):
                e, half = u // 2, u % 2
                act.wait_ge(up, u + 1)
                if u >= 2:
                    act.wait_ge(prod_ready, u - 1)
                act.activation(h1[u % 2], PS[:, 2 * (u % 3), :], ACT.Identity,
                               bias=w["L0f_b1"][:, e, half:half + 1]).then_inc(h1_ready, 1)
                if half == 0:
                    act.wait_ge(gate_ready, e + 1)
                    if e >= 1:
                        act.wait_ge(a_ready, e)
                    act.activation(sig, gated, ACT.Sigmoid, scale=1.702).then_inc(sig_ready, 1)

        @block.vector
        def _(dve):
            chain = Chain(dve, dve_chain)
            dve.wait_ge(bias_ready, 1)
            dve.tensor_copy(net.acc[:], PS[:, 7, :].rearrange("p (t d) -> p t d", t=NT)).then_inc(acc_ready, 1)

            def add(e):
                dve.wait_ge(y_ready, e + 1)
                dve.wait_ge(acc_ready, e + 1)
                for t in range(NT):
                    ins = dve.scalar_tensor_tensor(out=net.acc[:, t, :], in0=PS[:, 6 + e % 2, t * P:(t + 1) * P],
                                                   scalar=net.cw[:, t, e:e + 1], in1=net.acc[:, t, :],
                                                   op0=ALU.mult, op1=ALU.add)
                ins.then_inc(acc_ready, 1)

            for u in range(2 * n):
                e, half = u // 2, u % 2
                dve.wait_ge(h1_ready, u + 1)
                dve.scalar_tensor_tensor(out=prod[half], in0=PS[:, 2 * (u % 3) + 1, :],
                                         scalar=w["L0f_b3"][:, e, half:half + 1], in1=h1[u % 2],
                                         op0=ALU.add, op1=ALU.mult).then_inc(prod_ready, 1)
                dve.wait_ge(prod_ready, u + 1)
                if half == 0:
                    if e >= 1:
                        dve.wait_ge(sig_ready, e)
                    dve.tensor_scalar(gated, prod[0], 7.0, None, ALU.min).then_inc(gate_ready, 1)
                else:
                    chain.link(dve.tensor_scalar(prod[1], prod[1], -7.0, 7.0, ALU.max, ALU.min))
                    if e >= 2:
                        dve.wait_ge(y_ready, e - 1)
                    chain.link(dve.scalar_tensor_tensor(out=prod[1], in0=prod[1], scalar=1.0, in1=gated,
                                                        op0=ALU.add, op1=ALU.mult))
                    dve.wait_ge(sig_ready, e + 1)
                    dve.tensor_tensor(act_out[e % 2], prod[1], sig, ALU.mult).then_inc(a_ready, 1)
                    if e >= 1:
                        add(e - 1)
            add(n - 1)
    norm(net, net.acc, "ln", add_to=net.X)


def rotate(dve, chain, net, src, dst, nh, cos, sin, halves):
    if halves:
        a, b = src[:, :, 0:nh, 0:4], src[:, :, 0:nh, 4:8]
        oa, ob = dst[:, :, 0:nh, 0:4], dst[:, :, 0:nh, 4:8]
    else:
        a, b = src[:, :, 0:nh, 0::2], src[:, :, 0:nh, 1::2]
        oa, ob = dst[:, :, 0:nh, 0::2], dst[:, :, 0:nh, 1::2]
    shape = [P, NT, nh, 4]
    c, s = bc(cos.unsqueeze(2), shape), bc(sin.unsqueeze(2), shape)
    t = net.tmp
    ac, bs = t[0][:, :, 0:nh, 0:4], t[0][:, :, 0:nh, 4:8]
    as_, bcs = t[1][:, :, 0:nh, 0:4], t[1][:, :, 0:nh, 4:8]
    dve.tensor_tensor(ac, a, c, ALU.mult)
    dve.tensor_tensor(bs, b, s, ALU.mult)
    dve.tensor_tensor(as_, a, s, ALU.mult)
    chain.link(dve.tensor_tensor(bcs, b, c, ALU.mult))
    dve.tensor_tensor(oa, ac, bs, ALU.add if halves else ALU.subtract)
    chain.link(dve.tensor_tensor(ob, bcs, as_, ALU.subtract if halves else ALU.add))


def project(net, kind, wqkv, nkv, cos=None, sin=None, bias=None, gain=None):
    w, PS = net.w, net.PS
    kvw = nkv * HD
    width = P + 2 * kvw
    with net.stage("proj", "lat_ready latT_ready proj_ready sq_ready sd_ready kpad_clear dve_chain") as (
            block, lat_ready, latT_ready, proj_ready, sq_ready, sd_ready, kpad_clear, dve_chain):
        @block.gpsimd
        def _(pool):
            pool.memset(net.kpad, 0.0).then_inc(kpad_clear, 1)

        @block.tensor
        def _(pe):
            if kind == "latent":
                pe.matmul(PS[0:32, 4, :], w["g_down"][:], net.UT[:], start=True, stop=True).then_inc(lat_ready, 1)
                pe.wait_ge(latT_ready, 1)
            for t in range(NT):
                u = net.UT[:, t * P:(t + 1) * P]
                if kind == "latent":
                    pe.matmul(PS[:, t, 0:P], u, w["g_wq"][:], start=True, stop=True)
                    ins = pe.matmul(PS[:, t, P:width], net.latT[:, t * P:(t + 1) * P], w["g_up"][:], start=True, stop=True)
                else:
                    ins = pe.matmul(PS[:, t, 0:width], u, wqkv, start=True, stop=True)
            ins.then_inc(proj_ready, 1)

        @block.scalar
        def _(act):
            if kind == "latent":
                act.wait_ge(lat_ready, 1)
                act.activation(net.latT[:], PS[0:32, 4, :], ACT.Identity).then_inc(latT_ready, 1)
            if kind != "plain":
                act.wait_ge(sq_ready, 1)
                act.activation(net.ss[:, :, 0:HEADS + nkv], net.ss[:, :, 0:HEADS + nkv], ACT.Sqrt, scale=1.0 / HD,
                               bias=w["eps"][:, 1:2]).then_inc(sd_ready, 1)

        @block.vector
        def _(dve):
            chain = Chain(dve, dve_chain)
            dve.wait_ge(proj_ready, 1)
            q = PS[:, 0:NT, 0:P].rearrange("p t (h d) -> p t h d", d=HD)
            k = PS[:, 0:NT, P:P + kvw].rearrange("p t (h d) -> p t h d", d=HD)
            v = PS[:, 0:NT, P + kvw:width].rearrange("p t (h d) -> p t h d", d=HD)
            K = net.ktok[:, :, 0:nkv, :]
            if kind == "plain":
                for src, dst, o in ((q, net.qtok, 0), (k, net.ktok, P)):
                    brow = bias[:, o:o + P].rearrange("p (h d) -> p h d", d=HD).unsqueeze(1)
                    last = dve.tensor_tensor(dst[:], src, bc(brow, [P, NT, HEADS, HD]), ALU.add)
                brow = bias[:, 2 * P:3 * P].rearrange("p (h d) -> p h d", d=HD).unsqueeze(1)
                dve.tensor_tensor(net.vaug[:, :, :, 0:HD], v, bc(brow, [P, NT, HEADS, HD]), ALU.add)
                chain.link(last)
            else:
                dve.tensor_copy(net.vaug[:, :, 0:nkv, 0:HD], v)
                if kind == "norm_rope":
                    dve.tensor_copy(net.qtok[:], q)
                    chain.link(dve.tensor_copy(K, k))
                else:
                    rotate(dve, chain, net, q, net.qtok, HEADS, cos, sin, False)
                    rotate(dve, chain, net, k, net.ktok, nkv, cos, sin, False)
                dve.tensor_tensor(net.tmp[2], net.qtok[:], net.qtok[:], ALU.mult)
                chain.link(dve.tensor_tensor(net.tmp[3][:, :, 0:nkv, :], K, K, ALU.mult))
                dve.tensor_reduce(net.ss[:, :, 0:HEADS], net.tmp[2], AX.X, ALU.add)
                dve.tensor_reduce(net.ss[:, :, HEADS:HEADS + nkv], net.tmp[3][:, :, 0:nkv, :], AX.X, ALU.add).then_inc(sq_ready, 1)
                dve.wait_ge(sd_ready, 1)
                chain.link(dve.reciprocal(net.ss[:, :, 0:HEADS + nkv], net.ss[:, :, 0:HEADS + nkv]))
                dve.tensor_tensor(net.qtok[:], net.qtok[:], bc(net.ss[:, :, 0:HEADS].unsqueeze(3), [P, NT, HEADS, HD]), ALU.mult)
                chain.link(dve.tensor_tensor(K, K, bc(net.ss[:, :, HEADS:HEADS + nkv].unsqueeze(3), [P, NT, nkv, HD]), ALU.mult))
                if kind == "norm_rope":
                    rotate(dve, chain, net, net.qtok, net.tmp[2], HEADS, cos, sin, True)
                    rotate(dve, chain, net, net.ktok, net.tmp[3], nkv, cos, sin, True)
                    g = gain.unsqueeze(1).unsqueeze(3)
                    dve.tensor_tensor(net.qtok[:], net.tmp[2], bc(g, [P, NT, HEADS, HD]), ALU.mult)
                    chain.link(dve.tensor_copy(K, net.tmp[3][:, :, 0:nkv, :]))
            dve.wait_ge(kpad_clear, 1)
            for i in range(NI):
                at = net.kpad[:, :, i, :].rearrange("p t (s r) -> p t s r", s=NS)[:, :, :, i * HD:(i + 1) * HD]
                src = net.ktok[:, :, i:HEADS:NI, :] if nkv == HEADS else K
                dve.tensor_copy(at, src)


def attend(net, local, with_max, scale, nkv):
    w, PS = net.w, net.PS
    pre = "l" if local else ""
    mask_qk, mask_kq = net.mask_bf[pre + "mask_qk"], net.mask_bf[pre + "mask_kq"]
    wide = P + WINDOW if local else 2 * P
    cols = wide + P
    O_AT = 2 * P + P
    units = [(b, i) for b in range(PAIR) for i in range(NI)]
    NU = len(units)
    ex = [net.big[:, 4 * n:4 * n + 4, :] for n in range(2)]

    with net.stage("turnqk", "turned copied") as (block, turned, copied):
        @block.tensor
        def _(pe):
            for t in range(NT):
                ins = pe.transpose(PS[:, 0, t * P:(t + 1) * P], net.qtok[:, t].rearrange("p h d -> p (h d)"), w["ident"][:])
            ins.then_inc(turned, 1)
            for i in range(NI):
                for t in range(NT):
                    ins = pe.transpose(PS[:, 1 + i, t * P:(t + 1) * P], net.kpad[:, t, i, :], w["ident"][:])
                ins.then_inc(turned, 1)

        @block.scalar
        def _(act):
            for i in (1, 3):
                act.wait_ge(turned, 2 + i)
                act.activation(net.kT[:, i, :], PS[:, 1 + i, :], ACT.Identity)

        @block.vector
        def _(dve):
            dve.wait_ge(turned, 1)
            dve.tensor_copy(net.qT[:], PS[:, 0, :])
            for i in (0, 2):
                dve.wait_ge(turned, 2 + i)
                dve.tensor_copy(net.kT[:, i, :], PS[:, 1 + i, :])

    def strip(t, s):
        return t[32 * s:32 * s + 32]

    if with_max:
        with net.stage("rowmax", "scores_ready max_ready turned") as (block, scores_ready, max_ready, turned):
            @block.tensor
            def _(pe):
                for n, (b, i) in enumerate(units):
                    if n >= 2:
                        pe.wait_ge(max_ready, n - 1)
                    base = 4 * (n % 2)
                    k0 = P - WINDOW if local else 0
                    for t, (c, klo) in enumerate(((0, 0), (P, k0))):
                        wd = P if t == 0 else wide
                        for s in range(NS):
                            pe.matmul(PS[:, base + s, c:c + wd], strip(net.qT, s)[:, b * SEQ + t * P:b * SEQ + (t + 1) * P],
                                      strip(net.kT, s)[:, i, b * SEQ + klo:b * SEQ + klo + wd], start=True, stop=False, skip_group_check=True)
                        for s in range(NS):
                            if local and t == 1:
                                ins = pe.matmul(PS[:, base + s, c:c + wd], net.ident_bf[:], mask_qk[:, 0:wd], start=False, stop=True,
                                                skip_group_check=True)
                            else:
                                ins = pe.matmul(PS[:, base + s, c + wd - P:c + wd], net.ident_bf[:],
                                                mask_qk[:, mask_qk.shape[1] - P:], start=False, stop=True,
                                                skip_group_check=True)
                    ins.then_inc(scores_ready, 1)
                pe.wait_ge(max_ready, NU)
                for t in range(NT):
                    ins = pe.transpose(PS[:, 0, t * P:(t + 1) * P], net.negm[:, t, :], w["ident"][:])
                ins.then_inc(turned, 1)

            @block.vector
            def _(dve):
                for n, (b, i) in enumerate(units):
                    dve.wait_ge(scores_ready, n + 1)
                    base = 4 * (n % 2)
                    heads = slice(i, P, P // NS)
                    dve.tensor_reduce(net.negm[:, TPS * b, heads], PS[:, base:base + 4, 0:P], AX.X, ALU.max, negate=True)
                    dve.tensor_reduce(net.negm[:, TPS * b + 1, heads], PS[:, base:base + 4, P:cols], AX.X, ALU.max,
                                      negate=True).then_inc(max_ready, 1)
                dve.wait_ge(turned, 1)
                dve.tensor_copy(net.mT[:], PS[:, 0, :])

    with net.stage("attend", "scores_ready exp_ready out_ready out_read rec_ready") as (
            block, scores_ready, exp_ready, out_ready, out_read, rec_ready):
        @block.tensor
        def _(pe):
            def scores(n):
                b, i = units[n]
                if n >= 2:
                    pe.wait_ge(out_read, n - 1)
                base = 4 * (n % 2)
                for kt, (c, wd) in enumerate(((0, wide), (wide, P))):
                    q0 = b * SEQ + kt * P
                    for s in range(NS):
                        pe.matmul(PS[:, base + s, c:c + wd], strip(net.kT, s)[:, i, q0:q0 + P],
                                  strip(net.qT, s)[:, q0:q0 + wd], start=True, stop=False, skip_group_check=True)
                    for s in range(NS):
                        m = wd if local else P
                        ins = pe.matmul(PS[:, base + s, c:c + m], net.ident_bf[:], mask_kq[:, 0:m], start=False, stop=not with_max,
                                        skip_group_check=True)
                    if with_max:
                        for s in range(NS):
                            ins = pe.matmul(PS[:, base + s, c:c + wd], strip(w["onerow"], s)[:, i, :], strip(net.mT, s)[:, q0:q0 + wd],
                                            start=False, stop=True, skip_group_check=True)
                ins.then_inc(scores_ready, 1)

            def outputs(n):
                b, i = units[n]
                base = 4 * (n % 2)
                pe.wait_ge(exp_ready, n + 1)
                e = ex[n % 2]
                for s in range(NS):
                    vh = NI * s + i if nkv == HEADS else s
                    v0, v1 = net.vaug[:, TPS * b, vh, :], net.vaug[:, TPS * b + 1, vh, :]
                    o = [PS[:, base, O_AT + (qt * NS + s) * (HD + 1):O_AT + (qt * NS + s + 1) * (HD + 1)] for qt in range(2)]
                    pe.matmul(o[0], e[:, s, 0:P], v0, start=True, stop=True, skip_group_check=True)
                    pe.matmul(o[1], e[:, s, wide:cols], v1, start=True, stop=False, skip_group_check=True)
                    ins = pe.matmul(o[1][0:wide - P], e[:, s, P:wide], v0, start=False, stop=True, skip_group_check=True)
                ins.then_inc(out_ready, 1)

            for n in range(NU + 1):
                if n < NU:
                    scores(n)
                if n >= 1:
                    outputs(n - 1)

        @block.scalar
        def _(act):
            for n in range(NU):
                act.wait_ge(scores_ready, n + 1)
                if n >= 2:
                    act.wait_ge(out_ready, n - 1)
                act.activation(ex[n % 2][:, :, 0:cols], PS[:, 4 * (n % 2):4 * (n % 2) + 4, 0:cols], ACT.Exp,
                               scale=scale).then_inc(exp_ready, 1)

        @block.vector
        def _(dve):
            for n, (b, i) in enumerate(units):
                dve.wait_ge(out_ready, n + 1)
                src = PS[:, 4 * (n % 2), O_AT:O_AT + 2 * NS * (HD + 1)].rearrange("p (t s d) -> p t s d", t=2, s=NS)
                dve.tensor_copy(net.osb[:, TPS * b:TPS * b + TPS, i:HEADS:NI, :], src).then_inc(out_read, 1)
            dve.wait_ge(out_read, NU)
            dve.reciprocal(net.orec[:], net.osb[:, :, :, HD]).then_inc(rec_ready, 1)
            dve.wait_ge(rec_ready, 1)
            dve.tensor_tensor(net.V[:].rearrange("p t (h d) -> p t h d", d=HD), net.osb[:, :, :, 0:HD],
                              bc(net.orec[:].unsqueeze(3), [P, NT, HEADS, HD]), ALU.mult)


def out_project(net, src, wo, dst, add=None, bias=None):
    turn(net, src, net.RT)
    with net.stage("wo", "ready dve_chain") as (block, ready, dve_chain):
        @block.tensor
        def _(pe):
            for t in range(NT):
                ins = pe.matmul(net.PS[:, 1, t * P:(t + 1) * P], net.RT[:, t * P:(t + 1) * P], wo, start=True, stop=True)
            ins.then_inc(ready, 1)

        @block.vector
        def _(dve):
            chain = Chain(dve, dve_chain)
            dve.wait_ge(ready, 1)
            y = net.PS[:, 1, :].rearrange("p (t d) -> p t d", t=NT)
            if add is None:
                dve.tensor_copy(dst[:], y)
            else:
                if bias is not None:
                    chain.link(dve.tensor_tensor(net.R[:], add[:], bc(bias.unsqueeze(1), [P, NT, P]), ALU.add))
                dve.tensor_tensor(dst[:], y, net.R[:] if bias is not None else add[:], ALU.add)


def l1_mixer(net):
    w = net.w
    norm(net, net.X, "ln", tok=net.U)
    norm(net, net.U, "rms", T=net.UT, scale=w["L1a_n1"][:, 0:1])
    project(net, "latent", None, 4, w["cosG"][:], w["sinG"][:])
    attend(net, False, False, HD ** -0.5, 4)
    out_project(net, net.V, w["g_wo"][:], net.U, add=net.U)
    norm(net, net.U, "rms", T=net.UT, scale=w["L1a_n2"][:, 0:1])
    project(net, "rope_norm", w["l_wqkv"][:], 4, w["cosL"][:], w["sinL"][:])
    attend(net, True, False, HD ** -0.5, 4)
    out_project(net, net.V, w["l_wo"][:], net.Y, add=net.U)
    norm(net, net.Y, "ln", add_to=net.X)


def gelu_experts(net, l):
    w, PS, big = net.w, net.PS, net.big
    NF = 4
    hid = [big[:, 4 * i:4 * i + 4, :] for i in range(2)]
    with net.stage("l1exp", "up h_ready y_ready acc_ready bias_ready") as (block, up, h_ready, y_ready, acc_ready, bias_ready):
        @block.tensor
        def _(pe):
            weighted_biases(net, pe, E, 7, w["L1f_b2"][:, l, :], bias_ready)

            def down(e):
                pe.wait_ge(h_ready, NF * (e + 1))
                if e >= 1:
                    pe.wait_ge(acc_ready, e)
                for t in range(NT):
                    for f in range(NF):
                        ins = pe.matmul(PS[:, 6 + e % 2, t * P:(t + 1) * P], hid[e % 2][:, f, t * P:(t + 1) * P],
                                        w["L1f_w2"][:, l, e, f, :], start=f == 0, stop=f == NF - 1)
                ins.then_inc(y_ready, 1)

            for e in range(E):
                for f in range(NF):
                    u = NF * e + f
                    if u >= 6:
                        pe.wait_ge(h_ready, u - 5)
                    pe.matmul(PS[:, u % 6, :], w["L1f_w1"][:, l, e, f * P:(f + 1) * P], net.UT[:], start=True, stop=True).then_inc(up, 1)
                if e >= 1:
                    down(e - 1)
            down(E - 1)

        @block.scalar
        def _(act):
            for u in range(NF * E):
                e, f = u // NF, u % NF
                act.wait_ge(up, u + 1)
                if e >= 2:
                    act.wait_ge(y_ready, e - 1)
                act.activation(hid[e % 2][:, f, :], PS[:, u % 6, :], ACT.Gelu,
                               bias=w["L1f_b1"][:, l, e, f:f + 1]).then_inc(h_ready, 1)

        @block.vector
        def _(dve):
            dve.wait_ge(bias_ready, 1)
            dve.tensor_copy(net.acc[:], PS[:, 7, :].rearrange("p (t d) -> p t d", t=NT)).then_inc(acc_ready, 1)
            for e in range(E):
                dve.wait_ge(y_ready, e + 1)
                dve.wait_ge(acc_ready, e + 1)
                for t in range(NT):
                    ins = dve.scalar_tensor_tensor(out=net.acc[:, t, :], in0=PS[:, 6 + e % 2, t * P:(t + 1) * P],
                                                   scalar=net.cw[:, t, e:e + 1], in1=net.acc[:, t, :],
                                                   op0=ALU.mult, op1=ALU.add)
                ins.then_inc(acc_ready, 1)
            dve.wait_ge(acc_ready, E + 1)
            dve.tensor_tensor(net.U[:], net.U[:], net.acc[:], ALU.add)


def l1_experts(net):
    w = net.w
    norm(net, net.X, "ln", tok=net.U)
    for l in range(2):
        norm(net, net.U, "ln", T=net.UT, scale=w["L1f_ln1w"][:, l:l + 1], bias=w["L1f_ln1b"][:, l:l + 1])
        project(net, "plain", w["L1f_wqkv"][:, l, :], HEADS, bias=w["L1f_bqkv"][:, l, :])
        attend(net, False, True, HD ** -0.5, HEADS)
        out_project(net, net.V, w["L1f_wo"][:, l, :], net.U, add=net.U, bias=w["L1f_bo"][:, l, :])
        norm(net, net.U, "ln", T=net.UT, scale=w["L1f_ln2w"][:, l:l + 1], bias=w["L1f_ln2b"][:, l:l + 1])
        route(net, "two", w["L1f_gw"][:, l, :], logit_bias=w["L1f_gb"][:, l, :], turn_weights=E, mean=l % 2 == 1)
        gelu_experts(net, l)
    norm(net, net.U, "ln", add_to=net.X)


def l2_mixer(net):
    w = net.w
    norm(net, net.X, "ln", T=net.UT)
    project(net, "norm_rope", w["L2a_wqkv"][:], 4, w["cosL"][:], w["sinL"][:], gain=w["L2a_gain"][:])
    attend(net, True, True, HD ** -0.5, 4)
    with net.stage("pairmix", "dve_chain") as (block, dve_chain):
        @block.vector
        def _(dve):
            chain = Chain(dve, dve_chain)
            y = net.V[:].rearrange("p t (q i d) -> p t q i d", i=2, d=HD)
            out = net.R[:].rearrange("p t (q o d) -> p t q o d", o=2, d=HD)
            t = net.tmp[0][:, :, 0:HEADS // 2, :]
            mix = w["L2a_mix"]
            shape = [P, NT, HEADS // 2, HD]
            for o in range(2):
                dve.tensor_tensor(out[:, :, :, o, :], y[:, :, :, 0, :], bc(mix[:, :, o, 0].unsqueeze(1).unsqueeze(3), shape), ALU.mult)
                chain.link(dve.tensor_tensor(t, y[:, :, :, 1, :], bc(mix[:, :, o, 1].unsqueeze(1).unsqueeze(3), shape), ALU.mult))
                chain.link(dve.tensor_tensor(out[:, :, :, o, :], out[:, :, :, o, :], t, ALU.add))
    out_project(net, net.R, w["L2a_wo"][:], net.Y)
    norm(net, net.Y, "ln", add_to=net.X)


def l2_experts(net):
    w, PS = net.w, net.PS
    norm(net, net.X, "ln", T=net.UT)
    route(net, "all", w["L2f_gate"][:], logit_bias=w["L2f_gb"][:], turn_weights=E)
    with net.stage("l2exp", "y_ready y_read bias_ready dve_chain") as (block, y_ready, y_read, bias_ready, dve_chain):
        @block.tensor
        def _(pe):
            weighted_biases(net, pe, E, 7, w["L2f_b"][:], bias_ready)
            for t in range(NT):
                b = 2 * (t % 3)
                if t >= 3:
                    pe.wait_ge(y_read, t - 2)
                for half in range(2):
                    ins = pe.matmul(PS[:, b + half, :], net.UT[:, t * P:(t + 1) * P], w["L2f_w"][:, half * 512:(half + 1) * 512],
                                    start=True, stop=True)
                ins.then_inc(y_ready, 1)

        @block.vector
        def _(dve):
            chain = Chain(dve, dve_chain)
            dve.wait_ge(bias_ready, 1)
            chain.link(dve.tensor_copy(net.acc[:], PS[:, 7, :].rearrange("p (t d) -> p t d", t=NT)))
            for t in range(NT):
                dve.wait_ge(y_ready, t + 1)
                for e in range(E):
                    ins = dve.scalar_tensor_tensor(out=net.acc[:, t, :], in0=PS[:, 2 * (t % 3) + e // 4, (e % 4) * P:(e % 4 + 1) * P],
                                                   scalar=net.cw[:, t, e:e + 1], in1=net.acc[:, t, :], op0=ALU.mult, op1=ALU.add)
                    if e < E - 1:
                        chain.link(ins)
                ins.then_inc(y_read, 1)
    norm(net, net.acc, "ln", add_to=net.X)


def l3_mixer(net):
    w, PS, big = net.w, net.PS, net.big
    M, DK, HP = 64, 16, 4
    norm(net, net.X, "ln", T=net.UT)
    with net.stage("l3proj", "p_ready s_ready g_ready dve_chain") as (block, p_ready, s_ready, g_ready, dve_chain):
        @block.tensor
        def _(pe):
            for n, name in enumerate(("L3a_wq", "L3a_wk", "L3a_wv")):
                pe.matmul(PS[:, n, :], w[name][:], net.UT[:], start=True, stop=True).then_inc(p_ready, 1)
            pe.matmul(PS[0:16, 3, :], w["L3a_wf1"][:], net.UT[:], start=True, stop=True).then_inc(p_ready, 1)
            pe.matmul(PS[0:16, 4, :], w["L3a_wg1"][:], net.UT[:], start=True, stop=True).then_inc(p_ready, 1)
            pe.wait_ge(s_ready, 5)
            for t in range(NT):
                ins = pe.matmul(PS[:, 5, t * P:(t + 1) * P], net.g_g1[:, t * P:(t + 1) * P], w["L3a_wg2"][:], start=True, stop=True)
            ins.then_inc(g_ready, 1)

        @block.scalar
        def _(act):
            for n, (dst, f) in enumerate(((net.g_q, ACT.Silu), (net.g_k, ACT.Silu), (net.g_v, ACT.Identity))):
                act.wait_ge(p_ready, n + 1)
                act.activation(dst[:], PS[:, n, :], f).then_inc(s_ready, 1)
            for n, dst in ((3, net.g_f1), (4, net.g_g1)):
                act.wait_ge(p_ready, n + 1)
                act.activation(dst[:], PS[0:16, n, :], ACT.Identity).then_inc(s_ready, 1)
            act.wait_ge(g_ready, 1)
            act.activation(net.U[:], PS[:, 5, :].rearrange("p (t d) -> p t d", t=NT), ACT.Sigmoid)

        @block.vector
        def _(dve):
            dve.wait_ge(s_ready, 3)
            for src, dst in ((net.g_k, net.g_dk), (net.g_v, net.g_dv)):
                s3, d3 = (a[:].rearrange("p (b t) -> p b t", b=PAIR) for a in (src, dst))
                dve.tensor_scalar(d3[:, :, 0:1], s3[:, :, 0:1], -1.0, None, ALU.mult)
                dve.tensor_tensor(d3[:, :, 1:], s3[:, :, 0:SEQ - 1], s3[:, :, 1:], ALU.subtract)

    F, QV, OK = big[:, 0, :], big[:, 1, :], big[:, 2, :]
    ebuf = [big[:, 3 + i, :] for i in range(2)]
    wbuf = [big[:, 5 + i, :] for i in range(2)]
    soft = net.R
    OUT = 7
    for hp in range(HP):
        rows = slice(32 * hp, 32 * hp + 32)
        with net.stage("l3a", "f_ready fs_ready spread prod_ready prod_used ok_ready okc turned centred exp_ready soft_ready back dve_chain") as (
                block, f_ready, fs_ready, spread, prod_ready, prod_used, ok_ready, okc, turned, centred, exp_ready, soft_ready, back, dve_chain):
            @block.tensor
            def _(pe):
                pe.matmul(PS[:, 5, :], w["L3a_wf2"][:, hp * P:(hp + 1) * P], net.g_f1[:], start=True, stop=True).then_inc(f_ready, 1)

                def reduce(k):
                    pe.wait_ge(prod_ready, k + 1)
                    pe.matmul(PS[:, 4, :], w["ident"][:], wbuf[k % 2], start=k == 0, stop=k == DK - 1).then_inc(prod_used, 1)

                for k in range(DK):
                    if k >= 2:
                        pe.wait_ge(prod_ready, k - 1)
                    b = 2 * (k % 2)
                    pe.matmul(PS[:, b, :], w["spread"][rows, k, :], net.g_dk[rows, :], start=True, stop=True)
                    pe.matmul(PS[:, b + 1, :], w["spread"][rows, k, :], net.g_q[rows, :], start=True, stop=True).then_inc(spread, 1)
                    if k >= 1:
                        reduce(k - 1)
                reduce(DK - 1)
                pe.wait_ge(okc, 1)
                for t in range(NT):
                    ins = pe.transpose(PS[:, 6, t * P:(t + 1) * P], OK[:, t * P:(t + 1) * P], w["ident"][:])
                ins.then_inc(turned, 1)
                pe.wait_ge(soft_ready, 1)
                for t in range(NT):
                    ins = pe.transpose(PS[:, 5, t * P:(t + 1) * P], soft[:, t, :], w["ident"][:])
                ins.then_inc(back, 1)

            @block.scalar
            def _(act):
                act.wait_ge(f_ready, 1)
                act.activation(F, PS[:, 5, :], ACT.Sigmoid).then_inc(fs_ready, 1)
                act.wait_ge(prod_used, DK)
                act.activation(OK, PS[:, 4, :], ACT.Identity).then_inc(okc, 1)
                act.wait_ge(centred, 1)
                act.activation(soft[:], soft[:], ACT.Exp).then_inc(exp_ready, 1)
                act.wait_ge(back, 1)
                act.activation(QV, PS[:, 5, :], ACT.Identity)

            @block.vector
            def _(dve):
                chain = Chain(dve, dve_chain)
                dve.wait_ge(fs_ready, 1)
                for k in range(DK):
                    dve.wait_ge(spread, k + 1)
                    for b in range(PAIR):
                        at = slice(b * SEQ, (b + 1) * SEQ)
                        ins = dve.tensor_tensor_scan(ebuf[k % 2][:, at], PS[:, 2 * (k % 2), at], F[:, at], 0.0, ALU.add, ALU.mult)
                    chain.link(ins)
                    if k >= 2:
                        dve.wait_ge(prod_used, k - 1)
                    dve.tensor_tensor(wbuf[k % 2], PS[:, 2 * (k % 2) + 1, :], ebuf[k % 2], ALU.mult).then_inc(prod_ready, 1)
                dve.wait_ge(turned, 1)
                s4 = PS[:, 6, :].rearrange("p (t h m) -> p t h m", t=NT, h=2)
                d4 = soft[:].rearrange("p t (h m) -> p t h m", h=2)
                top, tot = net.orec[:, :, 0:2], net.orec[:, :, 2:4]
                chain.link(dve.tensor_reduce(top, s4, AX.X, ALU.max))
                dve.tensor_tensor(d4, s4, bc(top.unsqueeze(3), [P, NT, 2, M]), ALU.subtract).then_inc(centred, 1)
                dve.wait_ge(exp_ready, 1)
                chain.link(dve.tensor_reduce(tot, d4, AX.X, ALU.add))
                chain.link(dve.reciprocal(tot, tot))
                dve.tensor_tensor(d4, d4, bc(tot.unsqueeze(3), [P, NT, 2, M]), ALU.mult).then_inc(soft_ready, 1)

        with net.stage("l3b", "spread e_ready prod_ready prod_used") as (block, spread, e_ready, prod_ready, prod_used):
            @block.tensor
            def _(pe):
                def reduce(k):
                    pe.wait_ge(prod_ready, k + 1)
                    pe.matmul(PS[rows, OUT, :], w["gather"][:, k, :], wbuf[k % 2], start=k == 0, stop=k == DK - 1).then_inc(prod_used, 1)

                for k in range(DK):
                    if k >= 2:
                        pe.wait_ge(e_ready, k - 1)
                    pe.matmul(PS[:, k % 2, :], w["spread"][rows, k, :], net.g_dv[rows, :], start=True, stop=True).then_inc(spread, 1)
                    if k >= 1:
                        reduce(k - 1)
                reduce(DK - 1)

            @block.vector
            def _(dve):
                for k in range(DK):
                    dve.wait_ge(spread, k + 1)
                    if k >= 2:
                        dve.wait_ge(prod_ready, k - 1)
                    for b in range(PAIR):
                        at = slice(b * SEQ, (b + 1) * SEQ)
                        ins = dve.tensor_tensor_scan(ebuf[k % 2][:, at], PS[:, k % 2, at], F[:, at], 0.0, ALU.add, ALU.mult)
                    ins.then_inc(e_ready, 1)

            @block.gpsimd
            def _(pool):
                for k in range(DK):
                    pool.wait_ge(e_ready, k + 1)
                    if k >= 2:
                        pool.wait_ge(prod_used, k - 1)
                    pool.tensor_tensor(wbuf[k % 2], ebuf[k % 2], QV, ALU.mult).then_inc(prod_ready, 1)

    with net.stage("l3out", "sum_ready turned sq_ready sd_ready dve_chain") as (block, sum_ready, turned, sq_ready, sd_ready, dve_chain):
        ovT = big[:, 0, :]

        @block.vector
        def _(dve):
            chain = Chain(dve, dve_chain)
            dve.tensor_tensor(ovT, PS[:, OUT, :], net.g_v[:], ALU.add).then_inc(sum_ready, 1)
            dve.wait_ge(turned, 1)
            chain.link(dve.tensor_tensor(net.V[:], PS[:, 0, :].rearrange("p (t d) -> p t d", t=NT), net.U[:], ALU.mult))
            chain.link(dve.tensor_tensor(net.R[:], net.V[:], net.V[:], ALU.mult))
            dve.tensor_reduce(net.ss[:, :, 0:8], net.R[:].rearrange("p t (h d) -> p t h d", h=8), AX.X, ALU.add).then_inc(sq_ready, 1)
            dve.wait_ge(sd_ready, 1)
            chain.link(dve.reciprocal(net.ss[:, :, 0:8], net.ss[:, :, 0:8]))
            v4 = net.V[:].rearrange("p t (h d) -> p t h d", h=8)
            dve.tensor_tensor(v4, v4, bc(net.ss[:, :, 0:8].unsqueeze(3), [P, NT, 8, DK]), ALU.mult)

        @block.tensor
        def _(pe):
            pe.wait_ge(sum_ready, 1)
            for t in range(NT):
                ins = pe.transpose(PS[:, 0, t * P:(t + 1) * P], ovT[:, t * P:(t + 1) * P], w["ident"][:])
            ins.then_inc(turned, 1)

        @block.scalar
        def _(act):
            act.wait_ge(sq_ready, 1)
            act.activation(net.ss[:, :, 0:8], net.ss[:, :, 0:8], ACT.Sqrt, scale=1.0 / DK, bias=w["eps"][:, 0:1]).then_inc(sd_ready, 1)
    with net.stage("l3wo", "turned scaled ready") as (block, turned, scaled, ready):
        @block.tensor
        def _(pe):
            for t in range(NT):
                ins = pe.transpose(PS[:, 0, t * P:(t + 1) * P], net.V[:, t, :], w["ident"][:])
            ins.then_inc(turned, 1)
            pe.wait_ge(scaled, 1)
            for t in range(NT):
                ins = pe.matmul(PS[:, 1, t * P:(t + 1) * P], net.RT[:, t * P:(t + 1) * P], w["L3a_wo"][:], start=True, stop=True)
            ins.then_inc(ready, 1)

        @block.scalar
        def _(act):
            act.wait_ge(turned, 1)
            act.activation(net.RT[:], PS[:, 0, :], ACT.Identity, scale=w["L3a_nw"][:, 0:1]).then_inc(scaled, 1)

        @block.vector
        def _(dve):
            dve.wait_ge(ready, 1)
            dve.tensor_copy(net.Y[:], PS[:, 1, :].rearrange("p (t d) -> p t d", t=NT))
    norm(net, net.Y, "ln", add_to=net.X)


def l3_experts(net):
    w, PS, big = net.w, net.PS, net.big
    norm(net, net.X, "ln", tok=net.U, T=net.UT)
    route(net, "sigmoid", w["L3f_gate"][:], select_bias=w["L3f_eb"][:])
    HID, HB = 176, 48
    bfv = big[:].rearrange("p a b -> p (a b)").bitcast(BF16)
    xin = [bfv[:, i * 512:(i + 1) * 512] for i in range(2)]
    xT = [bfv[:, 1024 + i * 512:1024 + (i + 1) * 512] for i in range(2)]
    hA = [bfv[:, 2048 + i * 512:2048 + (i + 1) * 512] for i in range(2)]
    hB = [bfv[0:HB, 3072 + i * 512:3072 + (i + 1) * 512] for i in range(2)]
    yb = bfv[:, 4096:4608]
    sA, sB = big[:, 5, :], big[0:HB, 6, :]
    psbf = PS[:, 0, :].bitcast(BF16)
    with net.stage("l3exp", "x_ready turned xT_ready up hr_ready h_ready y_ready yb_ready s_up s_relu s_sq s_down dve_chain") as (
            block, x_ready, turned, xT_ready, up, hr_ready, h_ready, y_ready, yb_ready, s_up, s_relu, s_sq, s_down, dve_chain):
        @block.tensor
        def _(pe):
            pe.matmul(PS[:, 6, :], w["L3f_sup"][:, 0:P], net.UT[:], start=True, stop=True)
            pe.matmul(PS[0:HB, 7, :], w["L3f_sup"][:, P:HID], net.UT[:], start=True, stop=True).then_inc(s_up, 1)
            pe.wait_ge(s_sq, 1)
            for t in range(NT):
                c = slice(t * P, (t + 1) * P)
                pe.matmul(PS[:, 6, c], sA[:, c], w["L3f_sdnA"][:], start=True, stop=False)
                ins = pe.matmul(PS[:, 6, c], sB[:, c], w["L3f_sdnB"][:], start=False, stop=True)
            ins.then_inc(s_down, 1)
            for e in range(E):
                pe.wait_ge(x_ready, e + 1)
                if e >= 1:
                    pe.wait_ge(xT_ready, e)
                for t in range(NT):
                    c = slice(t * P, (t + 1) * P)
                    ins = pe.transpose(psbf[:, c], xin[e % 2][:, c], net.ident_bf[:])
                ins.then_inc(turned, 1)
                pe.wait_ge(xT_ready, e + 1)
                if e >= 1:
                    pe.wait_ge(hr_ready, 2 * e)
                pe.matmul(PS[:, 1, :], net.up_bf[:, e, 0:P], xT[e % 2], start=True, stop=True)
                pe.matmul(PS[0:HB, 2, :], net.up_bf[:, e, P:HID], xT[e % 2], start=True, stop=True).then_inc(up, 1)
                pe.wait_ge(h_ready, 2 * (e + 1))
                if e >= 1:
                    pe.wait_ge(yb_ready, e)
                for t in range(NT):
                    c = slice(t * P, (t + 1) * P)
                    pe.matmul(PS[:, 3, c], hA[e % 2][:, c], net.dnA_bf[:, e, :], start=True, stop=False)
                    ins = pe.matmul(PS[:, 3, c], hB[e % 2][:, c], net.dnB_bf[:, e, :], start=False, stop=True)
                ins.then_inc(y_ready, 1)

        @block.scalar
        def _(act):
            act.wait_ge(s_up, 1)
            act.activation(sA, PS[:, 6, :], ACT.Relu)
            act.activation(sB, PS[0:HB, 7, :], ACT.Relu).then_inc(s_relu, 1)
            for e in range(E):
                act.wait_ge(turned, e + 1)
                act.activation(xT[e % 2], psbf[:, 0:512], ACT.Identity).then_inc(xT_ready, 1)
                act.wait_ge(up, e + 1)
                if e >= 2:
                    act.wait_ge(y_ready, e - 1)
                act.activation(hA[e % 2], PS[:, 1, :], ACT.Relu).then_inc(hr_ready, 1)
                act.activation(hB[e % 2], PS[0:HB, 2, :], ACT.Relu).then_inc(hr_ready, 1)
                act.wait_ge(y_ready, e + 1)
                if e >= 1:
                    act.wait_ge(h_ready, 2 * e)
                    act.wait_ge(x_ready, min(E, e + 1))
                    act.wait_ge(yb_ready, e)
                act.activation(yb, PS[:, 3, :], ACT.Identity).then_inc(yb_ready, 1)

        @block.vector
        def _(dve):
            chain = Chain(dve, dve_chain)
            dve.wait_ge(s_relu, 1)
            dve.tensor_tensor(sA, sA, sA, ALU.mult)
            dve.tensor_tensor(sB, sB, sB, ALU.mult).then_inc(s_sq, 1)

            def scale_rows(e):
                if e >= 2:
                    dve.wait_ge(turned, e - 1)
                for t in range(NT):
                    ins = dve.tensor_scalar(xin[e % 2][:, t * P:(t + 1) * P], net.U[:, t, :], net.cw[:, t, e:e + 1], None, ALU.mult)
                ins.then_inc(x_ready, 1)

            scale_rows(0)
            dve.wait_ge(s_down, 1)
            chain.link(dve.tensor_copy(net.acc[:], PS[:, 6, :].rearrange("p (t d) -> p t d", t=NT)))
            for e in range(E):
                if e + 1 < E:
                    scale_rows(e + 1)
                dve.wait_ge(hr_ready, 2 * (e + 1))
                dve.tensor_tensor(hA[e % 2], hA[e % 2], hA[e % 2], ALU.mult).then_inc(h_ready, 1)
                dve.tensor_tensor(hB[e % 2], hB[e % 2], hB[e % 2], ALU.mult).then_inc(h_ready, 1)
                dve.wait_ge(yb_ready, e + 1)
                chain.link(dve.tensor_tensor(net.acc[:], net.acc[:], yb.rearrange("p (t d) -> p t d", t=NT), ALU.add))
    norm(net, net.acc, "ln", add_to=net.X)


STAGES = [l0_mixer, l0_experts, l1_mixer, l1_experts, l2_mixer, l2_experts, l3_mixer, l3_experts]


def sandwich(nc, x, out, w_dram):
    x_d = x.rearrange("(i b) (t p) d -> i p (b t) d", b=PAIR, p=P)
    out_d = out.rearrange("(i b) (t p) d -> i p (b t) d", b=PAIR, p=P)
    with ExitStack() as ctx:
        net = Net(nc, ctx, w_dram)
        load_weights(net)
        with nc.Fori(0, x.shape[0] // PAIR) as i:
            with net.stage("fetch", "x_landed") as (block, x_landed):
                @block.sync
                def _(sp):
                    sp.dma_start(net.X[:], x_d[i]).then_inc(x_landed, 16)
                    sp.wait_ge(x_landed, 16)
            for f in STAGES:
                f(net)
            with net.stage("store", "stored") as (block, stored):
                @block.sync
                def _(sp):
                    sp.dma_start(out_d[i], net.X[:]).then_inc(stored, 16)
                    sp.wait_ge(stored, 16)


def constants():
    c = {"ident": np.eye(P), "zeros": np.zeros((P, P)), "iota8": np.tile(np.arange(E), (P, 1)),
         "eps": np.tile([LN_EPS, RMS_EPS], (P, 1))}
    for name, base in (("G", 1e6), ("L", 1e4)):
        inv = (1.0 / np.float32(base) ** (np.arange(0, HD, 2, dtype=np.float32) / np.float32(HD))).astype(np.float32)
        fr = (np.arange(SEQ, dtype=np.float32)[:, None] * inv[None, :]).astype(np.float32)
        for fn, tag in ((np.cos, "cos"), (np.sin, "sin")):
            t = fn(fr.astype(np.float64)).reshape(TPS, P, HD // 2)
            c[tag + name] = np.tile(t, (PAIR, 1, 1)).transpose(1, 0, 2)
    r = np.arange(P)
    c["mask_qk"] = np.where(r[:, None] >= r[None, :], 0.0, MASKED)
    c["mask_kq"] = np.ascontiguousarray(c["mask_qk"].T)
    k = np.arange(P + WINDOW) - WINDOW
    d = r[:, None] - k[None, :]
    c["lmask_qk"] = np.where((d >= 0) & (d < WINDOW), 0.0, MASKED)
    d = np.arange(P + WINDOW)[None, :] - r[:, None]
    c["lmask_kq"] = np.where((d >= 0) & (d < WINDOW), 0.0, MASKED)
    onerow = np.zeros((NS, P // NS, NI, P))
    onerow[:, np.arange(NI), np.arange(NI)] = 1.0
    c["onerow"] = onerow.reshape(P, NI, P)
    spread = np.zeros((4, 32, 16, 2, 64))
    gather = np.zeros((2, 64, 16, 32))
    for h in range(2):
        for k in range(16):
            spread[:, h * 16 + k, k, h, :] = 1.0
            gather[h, :, k, h * 16 + k] = 1.0
    c["spread"] = spread.reshape(P, 16, P)
    c["gather"] = gather.reshape(P, 16, 32)
    return {n: np.ascontiguousarray(a, dtype=np.float32) for n, a in c.items()}


def lay_out(a):
    def col(n):
        return a[n].reshape(P, 1)

    def row(n):
        return np.broadcast_to(a[n].reshape(1, -1), (P, a[n].size))

    cat = np.concatenate
    w = {
        "L0a_alog": col("L0_attn_a_log"), "L0a_inw": col("L0_attn_input_norm_w"), "L0a_cout": col("L0_attn_c_out"),
        "L0a_dskip": col("L0_attn_d_skip"), "L0a_ffw": col("L0_attn_ff_norm_w"),
        "L0a_fc": a["L0_attn_ff_fc_w"].T, "L0a_proj": a["L0_attn_ff_proj_w"].T.reshape(2, P, P).transpose(1, 0, 2),
        "L0f_gate": a["L0_ffn_gate_w"].T, "L0f_gb": row("L0_ffn_gate_b"),
        "L0f_b2": cat([a["L0_ffn_b2"], a["L0_ffn_sb2"][None]]),
        "L0f_w2": cat([a["L0_ffn_w2"], a["L0_ffn_sw2"][None]]).transpose(2, 0, 1),
        "L1a_n1": col("L1_attn_norm1_w"), "L1a_n2": col("L1_attn_norm2_w"),
        "g_wq": a["L1_attn_g_wq"], "g_down": a["L1_attn_g_kv_down"],
        "g_up": cat([a["L1_attn_g_k_up"], a["L1_attn_g_v_up"]], 1), "g_wo": a["L1_attn_g_wo"],
        "l_wqkv": cat([a["L1_attn_l_wq"], a["L1_attn_l_wk"], a["L1_attn_l_wv"]], 1), "l_wo": a["L1_attn_l_wo"],
        "L1f_wqkv": cat([a["L1_ffn_wq"], a["L1_ffn_wk"], a["L1_ffn_wv"]], 2).transpose(1, 0, 2),
        "L1f_wo": a["L1_ffn_wo"].transpose(1, 0, 2), "L1f_gw": a["L1_ffn_gate_w"].transpose(1, 0, 2),
        "L1f_w1": a["L1_ffn_e_w1"].transpose(2, 0, 1, 3),
        "L1f_w2": a["L1_ffn_e_w2"].reshape(2, E, 4, P, P).transpose(3, 0, 1, 2, 4),
        "L1f_b1": a["L1_ffn_e_b1"].reshape(2, E, 4, P).transpose(3, 0, 1, 2), "L1f_b2": a["L1_ffn_e_b2"].transpose(1, 0, 2),
        "L2a_wqkv": cat([a["L2_attn_Wq"], a["L2_attn_Wk"], a["L2_attn_Wv"]]).T, "L2a_wo": a["L2_attn_Wo"].T,
        "L2a_gain": row("L2_attn_q_gain"), "L2a_mix": row("L2_attn_pair_mix").reshape(P, 8, 2, 2),
        "L2f_gate": a["L2_ffn_gate_w"].T, "L2f_gb": row("L2_ffn_gate_b"),
        "L2f_w": a["L2_ffn_expert_w"].transpose(2, 0, 1).reshape(P, E * P), "L2f_b": a["L2_ffn_expert_b"],
        "L3a_wq": a["L3_attn_Wq"], "L3a_wk": a["L3_attn_Wk"], "L3a_wv": a["L3_attn_Wv"], "L3a_wf1": a["L3_attn_Wf1"],
        "L3a_wf2": a["L3_attn_Wf2"], "L3a_wg1": a["L3_attn_Wg1"], "L3a_wg2": a["L3_attn_Wg2"], "L3a_wo": a["L3_attn_Wo"],
        "L3a_nw": col("L3_attn_norm_w"), "L3f_gate": a["L3_ffn_gate_w"].T, "L3f_eb": row("L3_ffn_expert_bias"),
        "L3f_up": a["L3_ffn_w_up"].transpose(2, 0, 1),
        "L3f_sup": a["L3_ffn_shared_w_up"].T,
    }
    dn, sdn = a["L3_ffn_w_down"].transpose(2, 0, 1), a["L3_ffn_shared_w_down"].T
    w["L3f_dnA"], w["L3f_dnB"], w["L3f_sdnA"], w["L3f_sdnB"] = dn[:P], dn[P:], sdn[:P], sdn[P:]
    for j in ("1", "3"):
        ww = cat([a["L0_ffn_w" + j], a["L0_ffn_sw" + j][None]])
        bb = cat([a["L0_ffn_b" + j], a["L0_ffn_sb" + j][None]])
        w["L0f_w" + j] = ww.reshape(E + 1, P, 2, P).transpose(3, 0, 2, 1)
        w["L0f_b" + j] = bb.reshape(E + 1, P, 2).transpose(1, 0, 2)
    for n, dst in (("ln1_w", "ln1w"), ("ln1_b", "ln1b"), ("ln2_w", "ln2w"), ("ln2_b", "ln2b")):
        w["L1f_" + dst] = a["L1_ffn_" + n].T
    for n, parts in (("bqkv", ("bq", "bk", "bv")), ("bo", ("bo",)), ("gb", ("gate_b",))):
        r = cat([a["L1_ffn_" + p] for p in parts], 1)
        w["L1f_" + n] = np.broadcast_to(r[None], (P,) + r.shape)
    return {n: np.ascontiguousarray(v) for n, v in w.items()}


def kernel(**inputs):
    import concourse.bacc as _bacc
    from concourse.bass_utils import run_bass_kernel_spmd as _run

    a = {n: np.asarray(v) for n, v in inputs.items()}
    nc = _bacc.Bacc("TRN2", target_bir_lowering=False, num_devices=1)
    arrays = {**lay_out(a), **constants()}
    w_dram = {n: nc.dram_tensor("in_" + n, v.shape, F32, kind="ExternalInput").ap() for n, v in arrays.items()}
    xs = a["L0_attn_x"]
    x = nc.dram_tensor("in_x", xs.shape, F32, kind="ExternalInput").ap()
    out = nc.dram_tensor("out", xs.shape, F32, kind="ExternalOutput").ap()
    sandwich(nc, x, out, w_dram)
    feeds = {"in_" + n: v for n, v in arrays.items()}
    feeds["in_x"] = np.ascontiguousarray(xs)
    r = _run(nc, [feeds], core_ids=[0])
    return r.results[0]["out"]
```

```python
from contextlib import ExitStack

import numpy as np

import concourse.bass as bass
from concourse import mybir

ACT = mybir.ActivationFunctionType
ALU = mybir.AluOpType
AX = mybir.AxisListType
F32 = mybir.dt.float32
BF16 = mybir.dt.bfloat16
U32 = mybir.dt.uint32

P = 128
SEQ = 256
PAIR = 2
NT = PAIR * SEQ // P
TOK = NT * P
TPS = SEQ // P
HEADS = 16
HD = P // HEADS
TERMS = 8
NB = HEADS // 2
VW = 32
UH = 4
WINDOW = 32
E = 8
MASKED = -1e30
LN_EPS = 1e-5
RMS_EPS = 1e-6


MASKS = ("pick_max", "spread", "mask_qk", "mask_kq", "lmask_qk", "lmask_kq")
IN_BF16 = ("L3f_up", "L3f_dnA", "L3f_dnB") + MASKS


NSIG = 16


class Chain:

    def __init__(self, eng, sem):
        self.eng, self.sem, self.n = eng, sem, 0

    def link(self, ins):
        self.n += 1
        ins.then_inc(self.sem, 1)
        self.eng.wait_ge(self.sem, self.n)


class Stage:

    def __init__(self, nc, sets, turn, names):
        self.nc, self.sems, self.last = nc, sets[turn % 2][:len(names.split())], sets[(turn + 1) % 2]
        assert len(self.sems) == len(names.split())

    def __enter__(self):
        self.block = self.nc.Block(no_gpsimd_drain=True)
        block = self.block.__enter__()

        @block.sync
        def _(sp):
            sp.sem_clear(range(self.last[0].num, self.last[-1].num + 1))

        return [block] + self.sems

    def __exit__(self, *exc):
        self.block.__exit__(*exc)


def bc(ap, shape):
    return ap.broadcast_to(shape)


class Net:
    def __init__(self, nc, ctx, w_dram):
        self.nc = nc
        sems = [ctx.enter_context(nc.semaphore(f"signal{i}")) for i in range(2 * NSIG)]
        assert [s.num for s in sems] == list(range(sems[0].num, sems[0].num + 2 * NSIG))
        self.sems, self.stages = (sems[:NSIG], sems[NSIG:]), 0

        def sb(name, shape, dt=F32):
            return ctx.enter_context(nc.sbuf_tensor(name, shape, dt))

        self.sb = sb
        self.w_dram = w_dram
        self.w = {n: sb("w_" + n, list(a.shape)) for n, a in w_dram.items() if n not in IN_BF16}
        self.PS = ctx.enter_context(nc.psum_tensor("PS", [P, 8, 512], F32))
        self.X = sb("X", [P, NT, P])
        self.U = sb("U", [P, NT, P])
        self.V = sb("V", [P, NT, P])
        self.Y = sb("Y", [P, NT, P])
        self.R = sb("R", [P, NT, P])
        self.UT = sb("UT", [P, TOK])
        self.RT = sb("RT", [P, TOK])
        self.ident_bf = sb("ident_bf", [P, P], BF16)
        self.mask_bf = {n: sb("bf_" + n, list(w_dram[n].shape), BF16)
                        for n in MASKS}
        self.stats = sb("stats", [P, NT, 6])
        self.mv = sb("mv", [P, NT, 2])
        self.m2 = sb("m2", [P, NT, 1])
        self.sd = sb("sd", [P, NT, 1])
        self.rs = sb("rs", [P, NT, 1])
        self.cw = sb("cw", [P, NT, E + 1])
        self.cwT32 = sb("cwT", [32, TOK])
        self.cwT = self.cwT32[0:E + 1, :]
        self.g = [sb(f"gate{i}", [P, NT, E]) for i in range(6)]
        self.g1 = [sb(f"gate_row{i}", [P, NT, 1]) for i in range(3)]
        self.gidx = sb("gidx", [P, NT, E], U32)
        self.hm = sb("hm", [P, PAIR])
        self.hmb = sb("hmb", [P, PAIR, P])
        self.qtok = sb("qtok", [P, NT, HEADS, HD])
        self.ktok = sb("ktok", [P, NT, HEADS, HD])
        self.vflat = sb("vflat", [P, NT * HEADS * (HD + 1) + VW])
        self.vaug = self.vflat[:, 0:NT * HEADS * (HD + 1)].rearrange("p (t h d) -> p t h d", t=NT, h=HEADS)
        tmps = sb("tmps", [P, 4, TOK])
        self.tmps = tmps
        self.tmp = [tmps[:, i, :].rearrange("p (t h d) -> p t h d", t=NT, h=HEADS) for i in range(4)]
        self.ss = sb("ss", [P, NT, 2 * HEADS])
        self.turned = sb("turned", [P, 2 * NB // 2, TOK])
        halves = [self.turned[:, 4 * i:4 * i + 4, :].rearrange("p a b -> p (a b)").bitcast(BF16) for i in range(2)]
        self.qT, self.kT = (a.rearrange("p (j n) -> p j n", j=NB) for a in halves)
        self.negm = sb("negm", [P, NT, HEADS])
        self.mres = sb("mres", [P, NT, HEADS])
        self.mparts = sb("mparts", [P, NT, 8, HEADS], BF16)
        self.mT = sb("mT", [P, TOK], BF16)
        self.latT = sb("latT", [32, TOK])
        self.big = sb("big", [P, 8, 512])
        self.orec = sb("orec", [P, NT, HEADS])
        self.acc = self.Y
        self.g_q, self.g_k, self.g_v, self.g_dk, self.g_dv = (self.turned[:, i, :] for i in range(5))
        self.g_f1, self.g_g1 = self.cwT32[0:16, :], self.latT[0:16, :]
        self.decay = sb("decay", [P, SEQ])
        self.parts = [self.big[:, 4 * i:4 * i + 4, :].rearrange("p a b -> p (a b)").bitcast(BF16).rearrange(
            "p (t h j d) -> p t h j d", t=NT, h=HEADS, j=TERMS) for i in range(2)]
        flat = self.big[:].rearrange("p a b -> p (a b)")
        nu, nd = E * 176, E * P
        self.w["L3f_up"] = flat[:, 0:nu].rearrange("p (e h) -> p e h", e=E)
        self.w["L3f_dnA"] = flat[:, nu:nu + nd].rearrange("p (e d) -> p e d", e=E)
        self.w["L3f_dnB"] = flat[0:48, nu + nd:nu + 2 * nd].rearrange("p (e d) -> p e d", e=E)
        at = nu + 2 * nd
        self.w["pick_max"] = self.turned[:, 0:4, :].rearrange("p a b -> p (a b)")
        self.w["spread"] = self.turned[:, 4:8, :].rearrange("p a b -> p (a b)")
        for n in MASKS[2:]:
            self.w[n] = flat[:, at:at + w_dram[n].shape[1]]
            at += w_dram[n].shape[1]
        self.up_bf = sb("up_bf", [P, E, 176], BF16)
        self.dnA_bf = sb("dnA_bf", [P, E, P], BF16)
        self.dnB_bf = sb("dnB_bf", [48, E, P], BF16)

    def k_rows(self, nkv):
        return self.ktok[:].rearrange("p t h d -> p (t h d)")[:, 0:NT * nkv * HD].rearrange(
            "p (t h d) -> p t h d", t=NT, h=nkv)

    def stage(self, tag, names):
        self.stages += 1
        return Stage(self.nc, self.sems, self.stages, names)


def load_weights(net):
    w, names = net.w, sorted(net.w)
    with net.stage("load", "loaded cleared dve_chain act_chain") as (block, loaded, cleared, dve_chain, act_chain):
        @block.sync
        def _(sp):
            for n in names[0::2]:
                sp.dma_start(w[n][:], net.w_dram[n]).then_inc(loaded, 16)
            sp.wait_ge(loaded, 16 * len(names))

        @block.gpsimd
        def _(pool):
            pool.memset(net.vflat[:], 1.0).then_inc(cleared, 1)
            pool.memset(net.mparts[:], 0.0).then_inc(cleared, 1)
            pool.memset(net.cw[:], 1.0).then_inc(cleared, 1)
            pool.wait_ge(cleared, 3)

        @block.vector
        def _(dve):
            dve.wait_ge(loaded, 16 * len(names))
            dve.tensor_copy(net.ident_bf[:], w["ident"][:])
            for n, m in net.mask_bf.items():
                dve.tensor_copy(m[:], w[n][:])
            dve.tensor_copy(net.up_bf[:], w["L3f_up"][:])
            dve.tensor_copy(net.dnA_bf[:], w["L3f_dnA"][:])
            dve.tensor_copy(net.dnB_bf[:], w["L3f_dnB"][:])
            dve.memset(net.decay[:], 0.0)

        @block.scalar
        def _(act):
            chain = Chain(act, act_chain)
            for n in names[1::2]:
                act.dma_start(w[n][:], net.w_dram[n]).then_inc(loaded, 16)
            act.wait_ge(loaded, 16 * len(names))
            chain.link(act.activation(w["L0a_alog"][:], w["L0a_alog"][:], ACT.Exp))
            chain.link(act.activation(w["L0a_alog"][:], w["L0a_alog"][:], ACT.Exp, scale=-1.0))
    with net.stage("decay", "dve_chain") as (block, dve_chain):
        @block.vector
        def _(dve):
            chain = Chain(dve, dve_chain)
            chain.link(dve.tensor_scalar(net.decay[:], net.decay[:], w["L0a_alog"][:, 0:1], None, ALU.add))


def norm(net, src, kind, tok=None, T=None, scale=None, bias=None, add_to=None):
    eps = net.w["eps"][:, 0:1] if kind == "ln" else net.w["eps"][:, 1:2]
    PS, w = net.PS, net.w
    tok = net.R if tok is None else tok
    with net.stage("norm", "var_ready sd_ready tok_ready turned T_ready dve_chain") as (
            block, var_ready, sd_ready, tok_ready, turned, T_ready, dve_chain):
        @block.vector
        def _(dve):
            chain = Chain(dve, dve_chain)
            for t in range(NT):
                last = dve.bn_stats(net.stats[:, t, :], src[:, t, :])
            chain.link(last)
            for t in range(NT):
                last = dve.bn_aggr(net.mv[:, t, :], net.stats[:, t, :])
            if kind == "rms":
                chain.link(last)
                chain.link(dve.tensor_tensor(net.m2[:], net.mv[:, :, 0:1], net.mv[:, :, 0:1], ALU.mult))
                last = dve.tensor_tensor(net.mv[:, :, 1:2], net.mv[:, :, 1:2], net.m2[:], ALU.add)
            last.then_inc(var_ready, 1)
            dve.wait_ge(sd_ready, 1)
            chain.link(dve.reciprocal(net.rs[:], net.sd[:]))
            for t in range(NT):
                if kind == "ln":
                    ins = dve.tensor_scalar(tok[:, t, :], src[:, t, :], net.mv[:, t, 0:1], net.rs[:, t, 0:1],
                                            ALU.subtract, ALU.mult)
                else:
                    ins = dve.tensor_scalar(tok[:, t, :], src[:, t, :], net.rs[:, t, 0:1], None, ALU.mult)
                ins.then_inc(tok_ready, 1)
            if add_to is not None:
                dve.wait_ge(tok_ready, NT)
                dve.tensor_tensor(add_to[:], add_to[:], tok[:], ALU.add)

        @block.scalar
        def _(act):
            act.wait_ge(var_ready, 1)
            act.activation(net.sd[:], net.mv[:, :, 1:2], ACT.Sqrt, bias=eps).then_inc(sd_ready, 1)
            if T is not None:
                act.wait_ge(turned, 1)
                act.activation(T[:], PS[:, 0, :], ACT.Identity, scale=1.0 if scale is None else scale,
                               bias=0.0 if bias is None else bias).then_inc(T_ready, 1)

        if T is not None:
            @block.tensor
            def _(pe):
                for t in range(NT):
                    pe.wait_ge(tok_ready, t + 1)
                    ins = pe.transpose(PS[:, 0, t * P:(t + 1) * P], tok[:, t, :], w["ident"][:])
                ins.then_inc(turned, 1)


def turn(net, src, T, scale=None):
    with net.stage("turn", "turned") as (block, turned):
        @block.tensor
        def _(pe):
            for t in range(NT):
                ins = pe.transpose(net.PS[:, 0, t * P:(t + 1) * P], src[:, t, :], net.w["ident"][:])
            ins.then_inc(turned, 1)

        @block.scalar
        def _(act):
            act.wait_ge(turned, 1)
            act.activation(T[:], net.PS[:, 0, :], ACT.Identity, scale=1.0 if scale is None else scale)


def l0_mixer(net):
    w, PS, big = net.w, net.PS, net.big
    norm(net, net.X, "ln", tok=net.U)
    norm(net, net.U, "rms", T=net.RT, scale=w["L0a_inw"][:, 0:1])
    scanT, skipT = big[:, 0, :], big[:, 1, :]
    with net.stage("l0scan", "mixed turned dve_chain") as (block, mixed, turned, dve_chain):
        @block.vector
        def _(dve):
            chain = Chain(dve, dve_chain)
            for b in range(PAIR):
                at = slice(b * SEQ, (b + 1) * SEQ)
                dve.tensor_tensor_scan(scanT[:, at], net.decay[:], net.RT[:, at], 0.0, ALU.mult, ALU.add)
            chain.link(dve.tensor_scalar(skipT, net.RT[:], w["L0a_dskip"][:, 0:1], None, ALU.mult))
            dve.scalar_tensor_tensor(out=scanT, in0=scanT, scalar=w["L0a_cout"][:, 0:1], in1=skipT,
                                     op0=ALU.mult, op1=ALU.add).then_inc(mixed, 1)
            dve.wait_ge(turned, 1)
            dve.tensor_tensor(net.V[:], PS[:, 0, :].rearrange("p (t d) -> p t d", t=NT), net.U[:], ALU.add)

        @block.tensor
        def _(pe):
            pe.wait_ge(mixed, 1)
            for t in range(NT):
                ins = pe.transpose(PS[:, 0, t * P:(t + 1) * P], scanT[:, t * P:(t + 1) * P], w["ident"][:])
            ins.then_inc(turned, 1)
    norm(net, net.V, "rms", T=net.RT, scale=w["L0a_ffw"][:, 0:1])
    with net.stage("l0mlp", "up hidden down") as (block, up, hidden, down):
        @block.tensor
        def _(pe):
            for f in range(2):
                pe.matmul(PS[:, f, :], w["L0a_fc"][:, f * P:(f + 1) * P], net.RT[:], start=True, stop=True).then_inc(up, 1)
            pe.wait_ge(hidden, 2)
            for t in range(NT):
                for f in range(2):
                    ins = pe.matmul(PS[:, 2, t * P:(t + 1) * P], big[:, f, t * P:(t + 1) * P], w["L0a_proj"][:, f, :],
                                    start=f == 0, stop=f == 1)
            ins.then_inc(down, 1)

        @block.scalar
        def _(act):
            for f in range(2):
                act.wait_ge(up, f + 1)
                act.activation(big[:, f, :], PS[:, f, :], ACT.Silu).then_inc(hidden, 1)

        @block.vector
        def _(dve):
            dve.wait_ge(down, 1)
            dve.tensor_tensor(net.Y[:], PS[:, 2, :].rearrange("p (t d) -> p t d", t=NT), net.V[:], ALU.add)
    norm(net, net.Y, "ln", add_to=net.X)


def route(net, mode, gate_w, logit_bias=None, select_bias=None, turn_weights=0, mean=False):
    w, PS = net.w, net.PS
    logits, ex, score, pick, sel0, sel1 = net.g
    top, total, rec = net.g1
    with net.stage("route", "mean_ready logits_ready centred exp_ready weights_ready turned dve_chain") as (
            block, mean_ready, logits_ready, centred, exp_ready, weights_ready, turned, dve_chain):
        @block.tensor
        def _(pe):
            if mean:
                pe.wait_ge(mean_ready, 1)
            for t in range(NT):
                rows = net.hmb[:, t // TPS, :] if mean else net.UT[:, t * P:(t + 1) * P]
                ins = pe.matmul(PS[:, 0, t * E:(t + 1) * E], rows, gate_w, start=True, stop=True)
            ins.then_inc(logits_ready, 1)
            if turn_weights:
                pe.wait_ge(weights_ready, 1)
                for t in range(NT):
                    ins = pe.transpose(PS[0:turn_weights, 1, t * P:(t + 1) * P], net.cw[:, t, 0:turn_weights], w["ident"][:])
                ins.then_inc(turned, 1)

        @block.scalar
        def _(act):
            act.wait_ge(centred, 1)
            act.activation(ex[:], logits[:], ACT.Sigmoid if mode == "sigmoid" else ACT.Exp).then_inc(exp_ready, 1)
            if turn_weights:
                act.wait_ge(turned, 1)
                act.activation(net.cwT[0:turn_weights, :], PS[0:turn_weights, 1, :], ACT.Identity)

        @block.vector
        def _(dve):
            chain = Chain(dve, dve_chain)
            if mean:
                chain.link(dve.tensor_reduce(net.hm[:], net.UT[:].rearrange("p (b s) -> p b s", b=PAIR), AX.X, ALU.add))
                chain.link(dve.tensor_scalar(net.hm[:], net.hm[:], 1.0 / SEQ, None, ALU.mult))
                for b in range(PAIR):
                    last = dve.tensor_scalar(net.hmb[:, b, :], w["zeros"][:], net.hm[:, b:b + 1], None, ALU.add)
                last.then_inc(mean_ready, 1)
            dve.wait_ge(logits_ready, 1)
            raw = PS[:, 0, 0:NT * E].rearrange("p (t e) -> p t e", t=NT)
            if logit_bias is not None:
                chain.link(dve.tensor_tensor(logits[:], raw, bc(logit_bias.unsqueeze(1), [P, NT, E]), ALU.add))
            else:
                chain.link(dve.tensor_copy(logits[:], raw))
            if mode == "sigmoid":
                last = dve.tensor_copy(sel0[:], logits[:])
            else:
                chain.link(dve.tensor_reduce(top[:], logits[:], AX.X, ALU.max))
                last = dve.tensor_tensor(logits[:], logits[:], bc(top[:], [P, NT, E]), ALU.subtract)
            last.then_inc(centred, 1)
            dve.wait_ge(exp_ready, 1)
            dve.wait_ge(centred, 1)
            if mode == "all":
                chain.link(dve.tensor_reduce(total[:], ex[:], AX.X, ALU.add))
                chain.link(dve.reciprocal(rec[:], total[:]))
                chain.link(dve.tensor_tensor(score[:], ex[:], bc(rec[:], [P, NT, E]), ALU.mult))
            else:
                chain.link(dve.tensor_copy(score[:], ex[:]))
            if select_bias is not None:
                chain.link(dve.tensor_tensor(pick[:], score[:], bc(select_bias.unsqueeze(1), [P, NT, E]), ALU.add))
            else:
                chain.link(dve.tensor_copy(pick[:], logits[:] if mode == "two" else score[:]))
            for t in range(NT):
                last = dve.max(sel0[:, t, :], pick[:, t, :])
            chain.link(last)
            for t in range(NT):
                last = dve.max_index(net.gidx[:, t, :], sel0[:, t, :], pick[:, t, :])
            chain.link(last)
            chain.link(dve.tensor_copy(pick[:], net.gidx[:]))
            places = bc(w["iota8"][:].unsqueeze(1), [P, NT, E])
            dve.tensor_tensor(sel0[:], places, bc(pick[:, :, 0:1], [P, NT, E]), ALU.is_equal)
            chain.link(dve.tensor_tensor(sel1[:], places, bc(pick[:, :, 1:2], [P, NT, E]), ALU.is_equal))
            chain.link(dve.tensor_tensor(sel0[:], sel0[:], sel1[:], ALU.add))
            last = dve.tensor_tensor(net.cw[:, :, 0:E], score[:], sel0[:], ALU.mult)
            if mode == "two":
                chain.link(last)
                chain.link(dve.tensor_reduce(total[:], net.cw[:, :, 0:E], AX.X, ALU.add))
                chain.link(dve.reciprocal(rec[:], total[:]))
                last = dve.tensor_tensor(net.cw[:, :, 0:E], net.cw[:, :, 0:E], bc(rec[:], [P, NT, E]), ALU.mult)
            last.then_inc(weights_ready, 1)


def weighted_biases(net, pe, rows, bank, biases, done):
    for t in range(NT):
        ins = pe.matmul(net.PS[:, bank, t * P:(t + 1) * P], net.cwT[0:rows, t * P:(t + 1) * P], biases, start=True, stop=True)
    ins.then_inc(done, 1)


def l0_experts(net):
    w, PS, big = net.w, net.PS, net.big
    norm(net, net.X, "ln", T=net.UT)
    route(net, "all", w["L0f_gate"][:], select_bias=w["L0f_gb"][:], turn_weights=E + 1)
    n = E + 1
    h1 = [big[:, i, :] for i in range(2)]
    prod = [big[:, 2 + i, :] for i in range(2)]
    gated, act_out = big[:, 4, :], [big[:, 6 + i, :] for i in range(2)]
    sig = big[:, 5, :]
    with net.stage("l0exp", "up h1_ready prod_ready gate_ready sig_ready lin_ready a_ready y_ready acc_ready bias_ready dve_chain") as (
            block, up, h1_ready, prod_ready, gate_ready, sig_ready, lin_ready, a_ready, y_ready, acc_ready, bias_ready, dve_chain):
        @block.tensor
        def _(pe):
            weighted_biases(net, pe, n, 7, w["L0f_b2"][:], bias_ready)

            def down(e):
                pe.wait_ge(a_ready, e + 1)
                if e == 1:
                    pe.wait_ge(acc_ready, 1)
                if e >= 2:
                    pe.wait_ge(acc_ready, e)
                for t in range(NT):
                    ins = pe.matmul(PS[:, 6 + e % 2, t * P:(t + 1) * P], act_out[e % 2][:, t * P:(t + 1) * P],
                                    w["L0f_w2"][:, e, :], start=True, stop=True)
                ins.then_inc(y_ready, 1)

            for e in range(n):
                for half in range(2):
                    u = 2 * e + half
                    b = 2 * (u % 3)
                    if u >= 3:
                        pe.wait_ge(h1_ready, u - 2)
                        pe.wait_ge(prod_ready, u - 2)
                    pe.matmul(PS[:, b, :], w["L0f_w1"][:, e, half, :], net.UT[:], start=True, stop=True)
                    pe.matmul(PS[:, b + 1, :], w["L0f_w3"][:, e, half, :], net.UT[:], start=True, stop=True).then_inc(up, 1)
                if e >= 1:
                    down(e - 1)
            down(n - 1)

        @block.scalar
        def _(act):
            for u in range(2 * n):
                e, half = u // 2, u % 2
                act.wait_ge(up, u + 1)
                if u >= 2:
                    act.wait_ge(prod_ready, u - 1)
                act.activation(h1[u % 2], PS[:, 2 * (u % 3), :], ACT.Identity,
                               bias=w["L0f_b1"][:, e, half:half + 1]).then_inc(h1_ready, 1)
                if half == 0:
                    act.wait_ge(gate_ready, e + 1)
                    if e >= 1:
                        act.wait_ge(a_ready, e)
                    act.activation(sig, gated, ACT.Sigmoid, scale=1.702).then_inc(sig_ready, 1)

        @block.vector
        def _(dve):
            chain = Chain(dve, dve_chain)
            dve.wait_ge(bias_ready, 1)
            dve.tensor_copy(net.acc[:], PS[:, 7, :].rearrange("p (t d) -> p t d", t=NT)).then_inc(acc_ready, 1)

            def add(e):
                dve.wait_ge(y_ready, e + 1)
                dve.wait_ge(acc_ready, e + 1)
                for t in range(NT):
                    ins = dve.scalar_tensor_tensor(out=net.acc[:, t, :], in0=PS[:, 6 + e % 2, t * P:(t + 1) * P],
                                                   scalar=net.cw[:, t, e:e + 1], in1=net.acc[:, t, :],
                                                   op0=ALU.mult, op1=ALU.add)
                ins.then_inc(acc_ready, 1)

            for u in range(2 * n):
                e, half = u // 2, u % 2
                dve.wait_ge(h1_ready, u + 1)
                dve.scalar_tensor_tensor(out=prod[half], in0=PS[:, 2 * (u % 3) + 1, :],
                                         scalar=w["L0f_b3"][:, e, half:half + 1], in1=h1[u % 2],
                                         op0=ALU.add, op1=ALU.mult).then_inc(prod_ready, 1)
                dve.wait_ge(prod_ready, u + 1)
                if half == 0:
                    if e >= 1:
                        dve.wait_ge(sig_ready, e)
                    dve.tensor_scalar(gated, prod[0], 7.0, None, ALU.min).then_inc(gate_ready, 1)
                else:
                    chain.link(dve.tensor_scalar(prod[1], prod[1], -7.0, 7.0, ALU.max, ALU.min))
                    if e >= 2:
                        dve.wait_ge(y_ready, e - 1)
                    chain.link(dve.scalar_tensor_tensor(out=prod[1], in0=prod[1], scalar=1.0, in1=gated,
                                                        op0=ALU.add, op1=ALU.mult))
                    dve.wait_ge(sig_ready, e + 1)
                    dve.tensor_tensor(act_out[e % 2], prod[1], sig, ALU.mult).then_inc(a_ready, 1)
                    if e >= 1:
                        add(e - 1)
            add(n - 1)
    norm(net, net.acc, "ln", add_to=net.X)


def rotate(dve, chain, net, src, dst, nh, cos, sin, halves):
    if halves:
        a, b = src[:, :, 0:nh, 0:4], src[:, :, 0:nh, 4:8]
        oa, ob = dst[:, :, 0:nh, 0:4], dst[:, :, 0:nh, 4:8]
    else:
        a, b = src[:, :, 0:nh, 0::2], src[:, :, 0:nh, 1::2]
        oa, ob = dst[:, :, 0:nh, 0::2], dst[:, :, 0:nh, 1::2]
    shape = [P, NT, nh, 4]
    c, s = bc(cos.unsqueeze(2), shape), bc(sin.unsqueeze(2), shape)
    t = net.tmp
    ac, bs = t[0][:, :, 0:nh, 0:4], t[0][:, :, 0:nh, 4:8]
    as_, bcs = t[1][:, :, 0:nh, 0:4], t[1][:, :, 0:nh, 4:8]
    dve.tensor_tensor(ac, a, c, ALU.mult)
    dve.tensor_tensor(bs, b, s, ALU.mult)
    dve.tensor_tensor(as_, a, s, ALU.mult)
    chain.link(dve.tensor_tensor(bcs, b, c, ALU.mult))
    dve.tensor_tensor(oa, ac, bs, ALU.add if halves else ALU.subtract)
    chain.link(dve.tensor_tensor(ob, bcs, as_, ALU.subtract if halves else ALU.add))


def project(net, kind, wqkv, nkv, cos=None, sin=None, bias=None, gain=None):
    w, PS = net.w, net.PS
    kvw = nkv * HD
    width = P + 2 * kvw
    with net.stage("proj", "lat_ready latT_ready proj_ready sq_ready sd_ready dve_chain") as (
            block, lat_ready, latT_ready, proj_ready, sq_ready, sd_ready, dve_chain):
        @block.tensor
        def _(pe):
            if kind == "latent":
                pe.matmul(PS[0:32, 4, :], w["g_down"][:], net.UT[:], start=True, stop=True).then_inc(lat_ready, 1)
                pe.wait_ge(latT_ready, 1)
            for t in range(NT):
                u = net.UT[:, t * P:(t + 1) * P]
                if kind == "latent":
                    pe.matmul(PS[:, t, 0:P], u, w["g_wq"][:], start=True, stop=True)
                    ins = pe.matmul(PS[:, t, P:width], net.latT[:, t * P:(t + 1) * P], w["g_up"][:], start=True, stop=True)
                else:
                    ins = pe.matmul(PS[:, t, 0:width], u, wqkv, start=True, stop=True)
            ins.then_inc(proj_ready, 1)

        @block.scalar
        def _(act):
            if kind == "latent":
                act.wait_ge(lat_ready, 1)
                act.activation(net.latT[:], PS[0:32, 4, :], ACT.Identity).then_inc(latT_ready, 1)
            if kind != "plain":
                act.wait_ge(sq_ready, 1)
                act.activation(net.ss[:, :, 0:HEADS + nkv], net.ss[:, :, 0:HEADS + nkv], ACT.Sqrt, scale=1.0 / HD,
                               bias=w["eps"][:, 1:2]).then_inc(sd_ready, 1)

        @block.vector
        def _(dve):
            chain = Chain(dve, dve_chain)
            dve.wait_ge(proj_ready, 1)
            q = PS[:, 0:NT, 0:P].rearrange("p t (h d) -> p t h d", d=HD)
            k = PS[:, 0:NT, P:P + kvw].rearrange("p t (h d) -> p t h d", d=HD)
            v = PS[:, 0:NT, P + kvw:width].rearrange("p t (h d) -> p t h d", d=HD)
            K = net.k_rows(nkv)
            if kind == "plain":
                for src, dst, o in ((q, net.qtok, 0), (k, net.ktok, P)):
                    brow = bias[:, o:o + P].rearrange("p (h d) -> p h d", d=HD).unsqueeze(1)
                    last = dve.tensor_tensor(dst[:], src, bc(brow, [P, NT, HEADS, HD]), ALU.add)
                brow = bias[:, 2 * P:3 * P].rearrange("p (h d) -> p h d", d=HD).unsqueeze(1)
                dve.tensor_tensor(net.vaug[:, :, :, 0:HD], v, bc(brow, [P, NT, HEADS, HD]), ALU.add)
                chain.link(last)
            else:
                dve.tensor_copy(net.vaug[:, :, 0:nkv, 0:HD], v)
                if kind == "norm_rope":
                    dve.tensor_copy(net.qtok[:], q)
                    chain.link(dve.tensor_copy(K, k))
                else:
                    rotate(dve, chain, net, q, net.qtok, HEADS, cos, sin, False)
                    rotate(dve, chain, net, k, K, nkv, cos, sin, False)
                dve.tensor_tensor(net.tmp[2], net.qtok[:], net.qtok[:], ALU.mult)
                chain.link(dve.tensor_tensor(net.tmp[3][:, :, 0:nkv, :], K, K, ALU.mult))
                dve.tensor_reduce(net.ss[:, :, 0:HEADS], net.tmp[2], AX.X, ALU.add)
                dve.tensor_reduce(net.ss[:, :, HEADS:HEADS + nkv], net.tmp[3][:, :, 0:nkv, :], AX.X, ALU.add).then_inc(sq_ready, 1)
                dve.wait_ge(sd_ready, 1)
                chain.link(dve.reciprocal(net.ss[:, :, 0:HEADS + nkv], net.ss[:, :, 0:HEADS + nkv]))
                dve.tensor_tensor(net.qtok[:], net.qtok[:], bc(net.ss[:, :, 0:HEADS].unsqueeze(3), [P, NT, HEADS, HD]), ALU.mult)
                chain.link(dve.tensor_tensor(K, K, bc(net.ss[:, :, HEADS:HEADS + nkv].unsqueeze(3), [P, NT, nkv, HD]), ALU.mult))
                if kind == "norm_rope":
                    rotate(dve, chain, net, net.qtok, net.tmp[2], HEADS, cos, sin, True)
                    rotate(dve, chain, net, K, net.tmp[3], nkv, cos, sin, True)
                    g = gain.unsqueeze(1).unsqueeze(3)
                    dve.tensor_tensor(net.qtok[:], net.tmp[2], bc(g, [P, NT, HEADS, HD]), ALU.mult)
                    chain.link(dve.tensor_copy(K, net.tmp[3][:, :, 0:nkv, :]))


def attend(net, local, with_max, scale, nkv):
    w, PS = net.w, net.PS
    mask_qk, mask_kq = (net.mask_bf[("l" if local else "") + m] for m in ("mask_qk", "mask_kq"))
    pick_max = net.mask_bf["pick_max"].rearrange("p (h c) -> p h c", h=HEADS)
    wide = P + WINDOW if local else 2 * P
    cols = wide + P
    units = [(b, g) for b in range(PAIR) for g in range(HEADS // UH)]
    NU = len(units)
    ex = [net.big[:, 4 * n:4 * n + 4, :] for n in range(2)]
    gqa = nkv < HEADS
    nkb = nkv if gqa else NB
    Q = net.qtok
    q_parts, k_parts = net.parts
    psb = PS[:].bitcast(BF16)

    with net.stage("split", "q_split k_split k_rounded turned dve_chain pool_chain") as (
            block, q_split, k_split, k_rounded, turned, dve_chain, pool_chain):
        @block.vector
        def _(dve):
            chain = Chain(dve, dve_chain)
            qh = Q[:].rearrange("p t h d -> p (t h) d")
            parts = q_parts.rearrange("p t h j d -> p (t h) j d")
            r = net.tmp[0].rearrange("p t h d -> p (t h) d")
            src, at = qh, 0
            for n in (3, 3, 2):
                ins = dve.tensor_copy(parts[:, :, at:at + n, :], bc(src.unsqueeze(2), [P, NT * HEADS, n, HD]))
                if at < 6:
                    chain.link(ins)
                    chain.link(dve.tensor_tensor(r, src, parts[:, :, at, :], ALU.subtract))
                    src, at = r, at + n
            ins.then_inc(q_split, 1)
            for n in range(NB // 2):
                dve.wait_ge(turned, n + 1)
                dve.tensor_copy(net.qT[:, 2 * n:2 * n + 2, :], psb[:, n, :].rearrange("p (j n) -> p j n", j=2))

        if gqa:
            kk = k_parts.rearrange("p t h j d -> p (t h j d)")[:, 0:NT * nkv * P].rearrange(
                "p (t h u j d) -> p (t h) u j d", t=NT, h=nkv, u=2, j=TERMS)
            spots = [kk[:, :, u] for u in range(2)]
        else:
            spots = [k_parts.rearrange("p t h j d -> p (t h) j d")]
        nth = NT * nkv
        keys_all = net.k_rows(nkv).rearrange("p t h d -> p (t h) d")
        res = net.tmp[1].rearrange("p t h d -> p (t h) d")[:, 0:nth, :]

        @block.scalar
        def _(act):
            for m in range(3):
                if m:
                    act.wait_ge(k_split, m)
                for spot in spots:
                    at = spot[:, :, m::3, :]
                    n = at.shape[2]
                    src = keys_all if m == 0 else res
                    ins = act.activation(at, bc(src.unsqueeze(2), [P, nth, n, HD]), ACT.Identity)
                ins.then_inc(k_rounded, 1)
            for n in range(nkb // 2):
                act.wait_ge(turned, NB // 2 + n + 1)
                act.activation(net.kT[:, 2 * n:2 * n + 2, :], psb[:, 4 + n, :].rearrange("p (j n) -> p j n", j=2), ACT.Identity)

        @block.gpsimd
        def _(pool):
            for m in range(2):
                pool.wait_ge(k_rounded, m + 1)
                src = keys_all if m == 0 else res
                pool.tensor_tensor(res, src, spots[0][:, :, m, :], ALU.subtract).then_inc(k_split, 1)
                if m == 0:
                    pool.wait_ge(k_split, 1)

        @block.tensor
        def _(pe):
            pe.wait_ge(q_split, 1)
            for j in range(NB):
                for t in range(NT):
                    rows = q_parts[:, t, 2 * j:2 * j + 2].rearrange("p h j d -> p (h j d)")
                    ins = pe.transpose(psb[:, j // 2, (j % 2) * TOK + t * P:(j % 2) * TOK + (t + 1) * P], rows, net.ident_bf[:])
                if j % 2:
                    ins.then_inc(turned, 1)
            pe.wait_ge(k_rounded, 3)
            for j in range(nkb):
                for t in range(NT):
                    at = (t * nkb + j) * P
                    rows = k_parts.rearrange("p t h j d -> p (t h j d)")[:, at:at + P]
                    ins = pe.transpose(psb[:, 4 + j // 2, (j % 2) * TOK + t * P:(j % 2) * TOK + (t + 1) * P], rows, net.ident_bf[:])
                if j % 2:
                    ins.then_inc(turned, 1)

    def head_rows(h):
        return slice(64 * (h % 2), 64 * (h % 2) + 64)

    def queries(h, q0, n):
        return net.qT[head_rows(h), h // 2, q0:q0 + n]

    def keys(h, k0, n):
        return net.kT[head_rows(h), h // UH if gqa else h // 2, k0:k0 + n]

    if with_max:
        with net.stage("rowmax", "scores_ready max_ready turned parts_ready dve_chain") as (
                block, scores_ready, max_ready, turned, parts_ready, dve_chain):
            @block.tensor
            def _(pe):
                for n, (b, g) in enumerate(units):
                    if n >= 2:
                        pe.wait_ge(max_ready, n - 1)
                    base = 4 * (n % 2)
                    k0 = P - WINDOW if local else 0
                    for t, (c, klo) in enumerate(((0, 0), (P, k0))):
                        wd = P if t == 0 else wide
                        for s in range(UH):
                            h = UH * g + s
                            pe.matmul(PS[:, base + s, c:c + wd], queries(h, b * SEQ + t * P, P), keys(h, b * SEQ + klo, wd),
                                      start=t == 0, stop=False, skip_group_check=True)
                    for t, c in enumerate((0, P)):
                        wd = P if t == 0 else wide
                        m = wd if local and t == 1 else P
                        for s in range(UH):
                            ins = pe.matmul(PS[:, base + s, c + wd - m:c + wd], net.ident_bf[:],
                                            mask_qk[:, mask_qk.shape[1] - m:], start=False, stop=True, skip_group_check=True)
                    ins.then_inc(scores_ready, 1)
                pe.wait_ge(parts_ready, 1)
                for t in range(NT):
                    ins = pe.transpose(psb[:, 0, t * P:(t + 1) * P], net.mparts[:, t].rearrange("p a h -> p (a h)"), net.ident_bf[:])
                ins.then_inc(turned, 1)

            @block.vector
            def _(dve):
                chain = Chain(dve, dve_chain)
                for n, (b, g) in enumerate(units):
                    dve.wait_ge(scores_ready, n + 1)
                    base = 4 * (n % 2)
                    heads = slice(UH * g, UH * g + UH)
                    dve.tensor_reduce(net.negm[:, TPS * b, heads], PS[:, base:base + 4, 0:P], AX.X, ALU.max, negate=True)
                    dve.tensor_reduce(net.negm[:, TPS * b + 1, heads], PS[:, base:base + 4, P:cols], AX.X, ALU.max,
                                      negate=True).then_inc(max_ready, 1)
                dve.wait_ge(max_ready, NU)
                src = net.negm
                for m in range(3):
                    ins = dve.tensor_copy(net.mparts[:, :, m, :], src[:])
                    if m < 2:
                        chain.link(ins)
                        chain.link(dve.tensor_tensor(net.mres[:], src[:], net.mparts[:, :, m, :], ALU.subtract))
                        src = net.mres
                ins.then_inc(parts_ready, 1)
                dve.wait_ge(turned, 1)
                dve.tensor_copy(net.mT[:], psb[:, 0, 0:TOK])

    outT = net.tmps[:].rearrange("p a b -> p (a b)").rearrange("p (n q) -> p n q", n=NU)
    with net.stage("attend", "scores_ready exp_ready out_ready out_read turned rec_ready") as (
            block, scores_ready, exp_ready, out_ready, out_read, turned, rec_ready):
        @block.tensor
        def _(pe):
            def scores(n):
                b, g = units[n]
                if n >= 2:
                    pe.wait_ge(out_read, n - 1)
                base = 4 * (n % 2)
                tiles = [(c, wd, b * SEQ + kt * P) for kt, (c, wd) in enumerate(((0, wide), (wide, P)))]
                for c, wd, q0 in tiles:
                    for s in range(UH):
                        h = UH * g + s
                        pe.matmul(PS[:, base + s, c:c + wd], keys(h, q0, P), queries(h, q0, wd), start=c == 0, stop=False,
                                  skip_group_check=True)
                for c, wd, q0 in tiles:
                    m = wd if local else P
                    for s in range(UH):
                        ins = pe.matmul(PS[:, base + s, c:c + m], net.ident_bf[:], mask_kq[:, 0:m], start=False,
                                        stop=not with_max, skip_group_check=True)
                if with_max:
                    for c, wd, q0 in tiles:
                        for s in range(UH):
                            ins = pe.matmul(PS[:, base + s, c:c + wd], pick_max[:, UH * g + s, :], net.mT[:, q0:q0 + wd],
                                            start=False, stop=True, skip_group_check=True)
                ins.then_inc(scores_ready, 1)

            def outputs(n):
                b, g = units[n]
                base = 4 * (n % 2)
                pe.wait_ge(exp_ready, n + 1)
                for kt, (c, wd) in enumerate(((0, wide), (wide, P))):
                    for s in range(UH):
                        at = ((TPS * b + kt) * HEADS + (g if gqa else UH * g + s)) * (HD + 1)
                        ins = pe.matmul(PS[VW * s:VW * s + VW, base, kt * P:kt * P + wd], net.vflat[:, at:at + VW],
                                        ex[n % 2][:, s, c:c + wd], start=kt == 0, stop=kt == 1, skip_group_check=True)
                ins.then_inc(out_ready, 1)

            for n in range(NU + 1):
                if n < NU:
                    scores(n)
                if n >= 1:
                    outputs(n - 1)
            pe.wait_ge(out_read, NU)
            for n, (b, g) in enumerate(units):
                for qt in range(TPS):
                    ins = pe.transpose(PS[:, TPS * b + qt, g * P:(g + 1) * P], outT[:, n, qt * P:(qt + 1) * P], w["ident"][:])
            ins.then_inc(turned, 1)

        @block.scalar
        def _(act):
            for n in range(NU):
                act.wait_ge(scores_ready, n + 1)
                if n >= 2:
                    act.wait_ge(out_ready, n - 1)
                act.activation(ex[n % 2][:, :, 0:cols], PS[:, 4 * (n % 2):4 * (n % 2) + 4, 0:cols], ACT.Exp,
                               scale=scale).then_inc(exp_ready, 1)

        @block.vector
        def _(dve):
            for n, (b, g) in enumerate(units):
                dve.wait_ge(out_ready, n + 1)
                dve.tensor_copy(outT[:, n, :], PS[:, 4 * (n % 2), 0:SEQ]).then_inc(out_read, 1)
            dve.wait_ge(turned, 1)
            o4 = PS[:, 0:NT, :].rearrange("p t (h d) -> p t h d", h=HEADS)
            dve.reciprocal(net.orec[:], o4[:, :, :, HD]).then_inc(rec_ready, 1)
            dve.wait_ge(rec_ready, 1)
            dve.tensor_tensor(net.V[:].rearrange("p t (h d) -> p t h d", d=HD), o4[:, :, :, 0:HD],
                              bc(net.orec[:].unsqueeze(3), [P, NT, HEADS, HD]), ALU.mult)


def out_project(net, src, wo, dst, add=None, bias=None):
    turn(net, src, net.RT)
    with net.stage("wo", "ready dve_chain") as (block, ready, dve_chain):
        @block.tensor
        def _(pe):
            for t in range(NT):
                ins = pe.matmul(net.PS[:, 1, t * P:(t + 1) * P], net.RT[:, t * P:(t + 1) * P], wo, start=True, stop=True)
            ins.then_inc(ready, 1)

        @block.vector
        def _(dve):
            chain = Chain(dve, dve_chain)
            dve.wait_ge(ready, 1)
            y = net.PS[:, 1, :].rearrange("p (t d) -> p t d", t=NT)
            if add is None:
                dve.tensor_copy(dst[:], y)
            else:
                if bias is not None:
                    chain.link(dve.tensor_tensor(net.R[:], add[:], bc(bias.unsqueeze(1), [P, NT, P]), ALU.add))
                dve.tensor_tensor(dst[:], y, net.R[:] if bias is not None else add[:], ALU.add)


def l1_mixer(net):
    w = net.w
    norm(net, net.X, "ln", tok=net.U)
    norm(net, net.U, "rms", T=net.UT, scale=w["L1a_n1"][:, 0:1])
    project(net, "latent", None, 4, w["cosG"][:], w["sinG"][:])
    attend(net, False, False, HD ** -0.5, 4)
    out_project(net, net.V, w["g_wo"][:], net.U, add=net.U)
    norm(net, net.U, "rms", T=net.UT, scale=w["L1a_n2"][:, 0:1])
    project(net, "rope_norm", w["l_wqkv"][:], 4, w["cosL"][:], w["sinL"][:])
    attend(net, True, False, HD ** -0.5, 4)
    out_project(net, net.V, w["l_wo"][:], net.Y, add=net.U)
    norm(net, net.Y, "ln", add_to=net.X)


def gelu_experts(net, l):
    w, PS, big = net.w, net.PS, net.big
    NF = 4
    hid = [big[:, 4 * i:4 * i + 4, :] for i in range(2)]
    with net.stage("l1exp", "up h_ready y_ready acc_ready bias_ready") as (block, up, h_ready, y_ready, acc_ready, bias_ready):
        @block.tensor
        def _(pe):
            weighted_biases(net, pe, E, 7, w["L1f_b2"][:, l, :], bias_ready)

            def down(e):
                pe.wait_ge(h_ready, NF * (e + 1))
                if e >= 1:
                    pe.wait_ge(acc_ready, e)
                for t in range(NT):
                    for f in range(NF):
                        ins = pe.matmul(PS[:, 6 + e % 2, t * P:(t + 1) * P], hid[e % 2][:, f, t * P:(t + 1) * P],
                                        w["L1f_w2"][:, l, e, f, :], start=f == 0, stop=f == NF - 1)
                ins.then_inc(y_ready, 1)

            for e in range(E):
                for f in range(NF):
                    u = NF * e + f
                    if u >= 6:
                        pe.wait_ge(h_ready, u - 5)
                    pe.matmul(PS[:, u % 6, :], w["L1f_w1"][:, l, e, f * P:(f + 1) * P], net.UT[:], start=True, stop=True).then_inc(up, 1)
                if e >= 1:
                    down(e - 1)
            down(E - 1)

        @block.scalar
        def _(act):
            for u in range(NF * E):
                e, f = u // NF, u % NF
                act.wait_ge(up, u + 1)
                if e >= 2:
                    act.wait_ge(y_ready, e - 1)
                act.activation(hid[e % 2][:, f, :], PS[:, u % 6, :], ACT.Gelu,
                               bias=w["L1f_b1"][:, l, e, f:f + 1]).then_inc(h_ready, 1)

        @block.vector
        def _(dve):
            dve.wait_ge(bias_ready, 1)
            dve.tensor_copy(net.acc[:], PS[:, 7, :].rearrange("p (t d) -> p t d", t=NT)).then_inc(acc_ready, 1)
            for e in range(E):
                dve.wait_ge(y_ready, e + 1)
                dve.wait_ge(acc_ready, e + 1)
                for t in range(NT):
                    ins = dve.scalar_tensor_tensor(out=net.acc[:, t, :], in0=PS[:, 6 + e % 2, t * P:(t + 1) * P],
                                                   scalar=net.cw[:, t, e:e + 1], in1=net.acc[:, t, :],
                                                   op0=ALU.mult, op1=ALU.add)
                ins.then_inc(acc_ready, 1)
            dve.wait_ge(acc_ready, E + 1)
            dve.tensor_tensor(net.U[:], net.U[:], net.acc[:], ALU.add)


def l1_experts(net):
    w = net.w
    norm(net, net.X, "ln", tok=net.U)
    for l in range(2):
        norm(net, net.U, "ln", T=net.UT, scale=w["L1f_ln1w"][:, l:l + 1], bias=w["L1f_ln1b"][:, l:l + 1])
        project(net, "plain", w["L1f_wqkv"][:, l, :], HEADS, bias=w["L1f_bqkv"][:, l, :])
        attend(net, False, True, HD ** -0.5, HEADS)
        out_project(net, net.V, w["L1f_wo"][:, l, :], net.U, add=net.U, bias=w["L1f_bo"][:, l, :])
        norm(net, net.U, "ln", T=net.UT, scale=w["L1f_ln2w"][:, l:l + 1], bias=w["L1f_ln2b"][:, l:l + 1])
        route(net, "two", w["L1f_gw"][:, l, :], logit_bias=w["L1f_gb"][:, l, :], turn_weights=E, mean=l % 2 == 1)
        gelu_experts(net, l)
    norm(net, net.U, "ln", add_to=net.X)


def l2_mixer(net):
    w = net.w
    norm(net, net.X, "ln", T=net.UT)
    project(net, "norm_rope", w["L2a_wqkv"][:], 4, w["cosL"][:], w["sinL"][:], gain=w["L2a_gain"][:])
    attend(net, True, True, HD ** -0.5, 4)
    with net.stage("pairmix", "dve_chain") as (block, dve_chain):
        @block.vector
        def _(dve):
            chain = Chain(dve, dve_chain)
            y = net.V[:].rearrange("p t (q i d) -> p t q i d", i=2, d=HD)
            out = net.R[:].rearrange("p t (q o d) -> p t q o d", o=2, d=HD)
            t = net.tmp[0][:, :, 0:HEADS // 2, :]
            mix = w["L2a_mix"]
            shape = [P, NT, HEADS // 2, HD]
            for o in range(2):
                dve.tensor_tensor(out[:, :, :, o, :], y[:, :, :, 0, :], bc(mix[:, :, o, 0].unsqueeze(1).unsqueeze(3), shape), ALU.mult)
                chain.link(dve.tensor_tensor(t, y[:, :, :, 1, :], bc(mix[:, :, o, 1].unsqueeze(1).unsqueeze(3), shape), ALU.mult))
                chain.link(dve.tensor_tensor(out[:, :, :, o, :], out[:, :, :, o, :], t, ALU.add))
    out_project(net, net.R, w["L2a_wo"][:], net.Y)
    norm(net, net.Y, "ln", add_to=net.X)


def l2_experts(net):
    w, PS = net.w, net.PS
    norm(net, net.X, "ln", T=net.UT)
    route(net, "all", w["L2f_gate"][:], logit_bias=w["L2f_gb"][:], turn_weights=E)
    with net.stage("l2exp", "y_ready y_read bias_ready dve_chain") as (block, y_ready, y_read, bias_ready, dve_chain):
        @block.tensor
        def _(pe):
            weighted_biases(net, pe, E, 7, w["L2f_b"][:], bias_ready)
            for t in range(NT):
                b = 2 * (t % 3)
                if t >= 3:
                    pe.wait_ge(y_read, t - 2)
                for half in range(2):
                    ins = pe.matmul(PS[:, b + half, :], net.UT[:, t * P:(t + 1) * P], w["L2f_w"][:, half * 512:(half + 1) * 512],
                                    start=True, stop=True)
                ins.then_inc(y_ready, 1)

        @block.vector
        def _(dve):
            chain = Chain(dve, dve_chain)
            dve.wait_ge(bias_ready, 1)
            chain.link(dve.tensor_copy(net.acc[:], PS[:, 7, :].rearrange("p (t d) -> p t d", t=NT)))
            for t in range(NT):
                dve.wait_ge(y_ready, t + 1)
                for e in range(E):
                    ins = dve.scalar_tensor_tensor(out=net.acc[:, t, :], in0=PS[:, 2 * (t % 3) + e // 4, (e % 4) * P:(e % 4 + 1) * P],
                                                   scalar=net.cw[:, t, e:e + 1], in1=net.acc[:, t, :], op0=ALU.mult, op1=ALU.add)
                    if e < E - 1:
                        chain.link(ins)
                ins.then_inc(y_read, 1)
    norm(net, net.acc, "ln", add_to=net.X)


def l3_mixer(net):
    w, PS, big = net.w, net.PS, net.big
    M, DK, HP = 64, 16, 4
    spread_w = net.mask_bf["spread"].rearrange("p (k c) -> p k c", k=DK)
    stacked = [a.rearrange("p a b -> p (a b)").bitcast(BF16).rearrange("p (h t) -> p h t", h=HP)
               for a in (net.turned[0:96, 5:7, :], net.tmps[0:96, 0:2, :], net.tmps[0:96, 2:4, :])]
    bfs = [[big[:, 6 + (n % 2), :].bitcast(BF16)[:, 0:TOK], big[:, 6 + (n % 2), :].bitcast(BF16)[:, TOK:],
            big[:, 2, :].bitcast(BF16)[:, (n % 2) * TOK:(n % 2 + 1) * TOK]] for n in range(3)]
    norm(net, net.X, "ln", T=net.UT)
    with net.stage("l3proj", "p_ready s_ready g_ready dve_chain") as (block, p_ready, s_ready, g_ready, dve_chain):
        @block.tensor
        def _(pe):
            for n, name in enumerate(("L3a_wq", "L3a_wk", "L3a_wv")):
                pe.matmul(PS[:, n, :], w[name][:], net.UT[:], start=True, stop=True).then_inc(p_ready, 1)
            pe.matmul(PS[0:16, 3, :], w["L3a_wf1"][:], net.UT[:], start=True, stop=True).then_inc(p_ready, 1)
            pe.matmul(PS[0:16, 4, :], w["L3a_wg1"][:], net.UT[:], start=True, stop=True).then_inc(p_ready, 1)
            pe.wait_ge(s_ready, 5)
            for t in range(NT):
                ins = pe.matmul(PS[:, 5, t * P:(t + 1) * P], net.g_g1[:, t * P:(t + 1) * P], w["L3a_wg2"][:], start=True, stop=True)
            ins.then_inc(g_ready, 1)

        @block.scalar
        def _(act):
            for n, (dst, f) in enumerate(((net.g_q, ACT.Silu), (net.g_k, ACT.Silu), (net.g_v, ACT.Identity))):
                act.wait_ge(p_ready, n + 1)
                act.activation(dst[:], PS[:, n, :], f).then_inc(s_ready, 1)
            for n, dst in ((3, net.g_f1), (4, net.g_g1)):
                act.wait_ge(p_ready, n + 1)
                act.activation(dst[:], PS[0:16, n, :], ACT.Identity).then_inc(s_ready, 1)
            act.wait_ge(g_ready, 1)
            act.activation(net.U[:], PS[:, 5, :].rearrange("p (t d) -> p t d", t=NT), ACT.Sigmoid)

        @block.vector
        def _(dve):
            dve.wait_ge(s_ready, 3)
            for src, dst in ((net.g_k, net.g_dk), (net.g_v, net.g_dv)):
                s3, d3 = (a[:].rearrange("p (b t) -> p b t", b=PAIR) for a in (src, dst))
                dve.tensor_scalar(d3[:, :, 0:1], s3[:, :, 0:1], -1.0, None, ALU.mult)
                dve.tensor_tensor(d3[:, :, 1:], s3[:, :, 0:SEQ - 1], s3[:, :, 1:], ALU.subtract)

    with net.stage("l3parts", "part_ready left_ready dve_chain") as (block, part_ready, left_ready, dve_chain):
        @block.vector
        def _(dve):
            chain = Chain(dve, dve_chain)
            for n, src in enumerate((net.g_dk, net.g_q, net.g_dv)):
                left, rounded = big[:, 3 + n, :], bfs[n]
                x = src
                for m in range(3):
                    chain.link(dve.tensor_copy(rounded[m], x))
                    if m < 2:
                        ins = dve.tensor_tensor(left, x, rounded[m], ALU.subtract)
                        chain.link(ins)
                        x = left
                for hp in range(HP):
                    for m in range(3):
                        ins = dve.tensor_copy(stacked[n][32 * m:32 * m + 32, hp, :], rounded[m][32 * hp:32 * hp + 32, :])
            chain.link(ins)

    F, QV, a_e, a_w = ([big[:, 2 * i + j, :] for j in range(2)] for i in range(4))
    b_e, b_w, OK = [net.g_q, net.g_k], [net.g_dk, net.g_dv], net.turned[:, 7, :]
    soft = net.R
    A_DK, A_Q, A_SUM, B_DV, OUT = 0, 2, 4, 5, 7
    for step in range(HP + 1):
        first, second = step < HP, step > 0
        fa, qa = F[step % 2], QV[step % 2]
        fb, qb = F[(step - 1) % 2], QV[(step - 1) % 2]
        outs = slice(32 * (step - 1), 32 * step)
        with net.stage("l3scan", "f_ready fs_ready a_spread a_prod a_used b_spread b_state b_prod b_used scores_in turned "
                       "centred exp_ready soft_ready back dve_chain") as (
                block, f_ready, fs_ready, a_spread, a_prod, a_used, b_spread, b_state, b_prod, b_used, scores_in, turned,
                centred, exp_ready, soft_ready, back, dve_chain):
            @block.tensor
            def _(pe):
                if first:
                    pe.matmul(PS[:, A_SUM, :], w["L3a_wf2"][:, step * P:(step + 1) * P], net.g_f1, start=True, stop=True).then_inc(f_ready, 1)

                def reduce(k):
                    if first:
                        pe.wait_ge(a_prod, k + 1)
                        pe.matmul(PS[:, A_SUM, :], w["ident"][:], a_w[k % 2], start=k == 0, stop=k == DK - 1).then_inc(a_used, 1)
                    if second:
                        pe.wait_ge(b_prod, k + 1)
                        pe.matmul(PS[outs, OUT, :], w["gather"][:, k, :], b_w[k % 2], start=k == 0, stop=k == DK - 1).then_inc(b_used, 1)

                for k in range(DK):
                    if first:
                        if k >= 2:
                            pe.wait_ge(a_prod, k - 1)
                        pe.matmul(PS[:, A_DK + k % 2, :], spread_w[0:96, k, :], stacked[0][:, step, :], start=True, stop=True)
                        pe.matmul(PS[:, A_Q + k % 2, :], spread_w[0:96, k, :], stacked[1][:, step, :], start=True, stop=True).then_inc(a_spread, 1)
                    if second:
                        if k >= 2:
                            pe.wait_ge(b_state, k - 1)
                        pe.matmul(PS[:, B_DV + k % 2, :], spread_w[0:96, k, :], stacked[2][:, step - 1, :], start=True, stop=True).then_inc(b_spread, 1)
                    if k >= 1:
                        reduce(k - 1)
                reduce(DK - 1)
                if first:
                    pe.wait_ge(scores_in, 1)
                    for t in range(NT):
                        ins = pe.transpose(PS[:, A_DK, t * P:(t + 1) * P], OK[:, t * P:(t + 1) * P], w["ident"][:])
                    ins.then_inc(turned, 1)
                    pe.wait_ge(soft_ready, 1)
                    for t in range(NT):
                        ins = pe.transpose(PS[:, A_DK + 1, t * P:(t + 1) * P], soft[:, t, :], w["ident"][:])
                    ins.then_inc(back, 1)

            if first:
                @block.scalar
                def _(act):
                    act.wait_ge(f_ready, 1)
                    act.activation(fa, PS[:, A_SUM, :], ACT.Sigmoid).then_inc(fs_ready, 1)
                    act.wait_ge(a_used, DK)
                    act.activation(OK, PS[:, A_SUM, :], ACT.Identity).then_inc(scores_in, 1)
                    act.wait_ge(centred, 1)
                    act.activation(soft[:], soft[:], ACT.Exp).then_inc(exp_ready, 1)
                    act.wait_ge(back, 1)
                    act.activation(qa, PS[:, A_DK + 1, :], ACT.Identity)

            @block.vector
            def _(dve):
                chain = Chain(dve, dve_chain)

                def scan(dst, rows, f):
                    for b in range(PAIR):
                        at = slice(b * SEQ, (b + 1) * SEQ)
                        ins = dve.tensor_tensor_scan(dst[:, at], rows[:, at], f[:, at], 0.0, ALU.add, ALU.mult)
                    return ins

                if first:
                    dve.wait_ge(fs_ready, 1)
                for k in range(DK):
                    if first:
                        dve.wait_ge(a_spread, k + 1)
                        ins = scan(a_e[k % 2], PS[:, A_DK + k % 2, :], fa)
                        ins.then_inc(dve_chain, 1)
                        chain.n += 1
                    if second:
                        dve.wait_ge(b_spread, k + 1)
                        if k >= 2:
                            dve.wait_ge(b_prod, k - 1)
                        scan(b_e[k % 2], PS[:, B_DV + k % 2, :], fb).then_inc(b_state, 1)
                    if first:
                        dve.wait_ge(dve_chain, chain.n)
                        if k >= 2:
                            dve.wait_ge(a_used, k - 1)
                        dve.tensor_tensor(a_w[k % 2], PS[:, A_Q + k % 2, :], a_e[k % 2], ALU.mult).then_inc(a_prod, 1)
                if first:
                    dve.wait_ge(turned, 1)
                    s4 = PS[:, A_DK, :].rearrange("p (t h m) -> p t h m", t=NT, h=2)
                    d4 = soft[:].rearrange("p t (h m) -> p t h m", h=2)
                    top, tot = net.orec[:, :, 0:2], net.orec[:, :, 2:4]
                    chain.link(dve.tensor_reduce(top, s4, AX.X, ALU.max))
                    dve.tensor_tensor(d4, s4, bc(top.unsqueeze(3), [P, NT, 2, M]), ALU.subtract).then_inc(centred, 1)
                    dve.wait_ge(exp_ready, 1)
                    chain.link(dve.tensor_reduce(tot, d4, AX.X, ALU.add))
                    chain.link(dve.reciprocal(tot, tot))
                    dve.tensor_tensor(d4, d4, bc(tot.unsqueeze(3), [P, NT, 2, M]), ALU.mult).then_inc(soft_ready, 1)

            if second:
                @block.gpsimd
                def _(pool):
                    for k in range(DK):
                        pool.wait_ge(b_state, k + 1)
                        if k >= 2:
                            pool.wait_ge(b_used, k - 1)
                        pool.tensor_tensor(b_w[k % 2], b_e[k % 2], qb, ALU.mult).then_inc(b_prod, 1)

    with net.stage("l3out", "sum_ready turned sq_ready sd_ready dve_chain") as (block, sum_ready, turned, sq_ready, sd_ready, dve_chain):
        ovT = big[:, 0, :]

        @block.vector
        def _(dve):
            chain = Chain(dve, dve_chain)
            dve.tensor_tensor(ovT, PS[:, OUT, :], net.g_v[:], ALU.add).then_inc(sum_ready, 1)
            dve.wait_ge(turned, 1)
            chain.link(dve.tensor_tensor(net.V[:], PS[:, 0, :].rearrange("p (t d) -> p t d", t=NT), net.U[:], ALU.mult))
            chain.link(dve.tensor_tensor(net.R[:], net.V[:], net.V[:], ALU.mult))
            dve.tensor_reduce(net.ss[:, :, 0:8], net.R[:].rearrange("p t (h d) -> p t h d", h=8), AX.X, ALU.add).then_inc(sq_ready, 1)
            dve.wait_ge(sd_ready, 1)
            chain.link(dve.reciprocal(net.ss[:, :, 0:8], net.ss[:, :, 0:8]))
            v4 = net.V[:].rearrange("p t (h d) -> p t h d", h=8)
            dve.tensor_tensor(v4, v4, bc(net.ss[:, :, 0:8].unsqueeze(3), [P, NT, 8, DK]), ALU.mult)

        @block.tensor
        def _(pe):
            pe.wait_ge(sum_ready, 1)
            for t in range(NT):
                ins = pe.transpose(PS[:, 0, t * P:(t + 1) * P], ovT[:, t * P:(t + 1) * P], w["ident"][:])
            ins.then_inc(turned, 1)

        @block.scalar
        def _(act):
            act.wait_ge(sq_ready, 1)
            act.activation(net.ss[:, :, 0:8], net.ss[:, :, 0:8], ACT.Sqrt, scale=1.0 / DK, bias=w["eps"][:, 0:1]).then_inc(sd_ready, 1)
    with net.stage("l3wo", "turned scaled ready") as (block, turned, scaled, ready):
        @block.tensor
        def _(pe):
            for t in range(NT):
                ins = pe.transpose(PS[:, 0, t * P:(t + 1) * P], net.V[:, t, :], w["ident"][:])
            ins.then_inc(turned, 1)
            pe.wait_ge(scaled, 1)
            for t in range(NT):
                ins = pe.matmul(PS[:, 1, t * P:(t + 1) * P], net.RT[:, t * P:(t + 1) * P], w["L3a_wo"][:], start=True, stop=True)
            ins.then_inc(ready, 1)

        @block.scalar
        def _(act):
            act.wait_ge(turned, 1)
            act.activation(net.RT[:], PS[:, 0, :], ACT.Identity, scale=w["L3a_nw"][:, 0:1]).then_inc(scaled, 1)

        @block.vector
        def _(dve):
            dve.wait_ge(ready, 1)
            dve.tensor_copy(net.Y[:], PS[:, 1, :].rearrange("p (t d) -> p t d", t=NT))
    norm(net, net.Y, "ln", add_to=net.X)


def l3_experts(net):
    w, PS, big = net.w, net.PS, net.big
    norm(net, net.X, "ln", tok=net.U, T=net.UT)
    route(net, "sigmoid", w["L3f_gate"][:], select_bias=w["L3f_eb"][:])
    HID, HB = 176, 48
    bfv = big[:].rearrange("p a b -> p (a b)").bitcast(BF16)
    xin = [bfv[:, i * 512:(i + 1) * 512] for i in range(2)]
    xT = [bfv[:, 1024 + i * 512:1024 + (i + 1) * 512] for i in range(2)]
    hA = [bfv[:, 2048 + i * 512:2048 + (i + 1) * 512] for i in range(2)]
    hB = [bfv[0:HB, 3072 + i * 512:3072 + (i + 1) * 512] for i in range(2)]
    yb = [bfv[:, 4096 + i * 512:4096 + (i + 1) * 512] for i in range(2)]
    sA, sB = big[:, 5, :], big[0:HB, 6, :]
    XT, UP, Y = [PS[:, 6 * i, :].bitcast(BF16)[:, 0:TOK] for i in range(2)], (1, 4), (3, 7)
    with net.stage("l3exp", "x_ready turned xT_ready up hr_ready h_ready y_ready yb_ready added s_up s_relu s_sq s_down") as (
            block, x_ready, turned, xT_ready, up, hr_ready, h_ready, y_ready, yb_ready, added, s_up, s_relu, s_sq, s_down):
        @block.tensor
        def _(pe):
            def turn_rows(e):
                pe.wait_ge(x_ready, e + 1)
                if e >= 2:
                    pe.wait_ge(xT_ready, e - 1)
                for t in range(NT):
                    c = slice(t * P, (t + 1) * P)
                    ins = pe.transpose(XT[e % 2][:, c], xin[e % 2][:, c], net.ident_bf[:])
                ins.then_inc(turned, 1)

            def up_rows(e):
                pe.wait_ge(xT_ready, e + 1)
                if e == 1:
                    pe.wait_ge(s_relu, 1)
                if e >= 2:
                    pe.wait_ge(hr_ready, 2 * (e - 1))
                pe.matmul(PS[:, UP[e % 2], :], net.up_bf[:, e, 0:P], xT[e % 2], start=True, stop=True)
                pe.matmul(PS[0:HB, UP[e % 2] + 1, :], net.up_bf[:, e, P:HID], xT[e % 2], start=True, stop=True).then_inc(up, 1)

            def down_rows(e):
                pe.wait_ge(h_ready, 2 * (e + 1))
                if e == 0:
                    pe.wait_ge(added, 1)
                if e >= 2:
                    pe.wait_ge(yb_ready, e - 1)
                for t in range(NT):
                    c = slice(t * P, (t + 1) * P)
                    pe.matmul(PS[:, Y[e % 2], c], hA[e % 2][:, c], net.dnA_bf[:, e, :], start=True, stop=False)
                    ins = pe.matmul(PS[:, Y[e % 2], c], hB[e % 2][:, c], net.dnB_bf[:, e, :], start=False, stop=True)
                ins.then_inc(y_ready, 1)

            pe.matmul(PS[:, 4, :], w["L3f_sup"][:, 0:P], net.UT[:], start=True, stop=True)
            pe.matmul(PS[0:HB, 5, :], w["L3f_sup"][:, P:HID], net.UT[:], start=True, stop=True).then_inc(s_up, 1)
            turn_rows(0)
            turn_rows(1)
            up_rows(0)
            pe.wait_ge(s_sq, 1)
            for t in range(NT):
                c = slice(t * P, (t + 1) * P)
                pe.matmul(PS[:, 3, c], sA[:, c], w["L3f_sdnA"][:], start=True, stop=False)
                ins = pe.matmul(PS[:, 3, c], sB[:, c], w["L3f_sdnB"][:], start=False, stop=True)
            ins.then_inc(s_down, 1)
            for e in range(E):
                if e + 1 < E:
                    up_rows(e + 1)
                if e + 2 < E:
                    turn_rows(e + 2)
                down_rows(e)

        @block.scalar
        def _(act):
            def take_turned(e):
                act.wait_ge(turned, e + 1)
                if e >= 2:
                    act.wait_ge(up, e - 1)
                act.activation(xT[e % 2], XT[e % 2], ACT.Identity).then_inc(xT_ready, 1)

            def take_out(e):
                act.wait_ge(y_ready, e + 1)
                if e >= 2:
                    act.wait_ge(added, e)
                act.activation(yb[e % 2], PS[:, Y[e % 2], :], ACT.Identity).then_inc(yb_ready, 1)

            act.wait_ge(s_up, 1)
            act.activation(sA, PS[:, 4, :], ACT.Relu)
            act.activation(sB, PS[0:HB, 5, :], ACT.Relu).then_inc(s_relu, 1)
            take_turned(0)
            take_turned(1)
            for e in range(E):
                act.wait_ge(up, e + 1)
                if e >= 2:
                    act.wait_ge(y_ready, e - 1)
                act.activation(hA[e % 2], PS[:, UP[e % 2], :], ACT.Relu).then_inc(hr_ready, 1)
                act.activation(hB[e % 2], PS[0:HB, UP[e % 2] + 1, :], ACT.Relu).then_inc(hr_ready, 1)
                if e + 2 < E:
                    take_turned(e + 2)
                if e >= 1:
                    take_out(e - 1)
            take_out(E - 1)

        @block.vector
        def _(dve):
            def scale_rows(e):
                if e >= 2:
                    dve.wait_ge(turned, e - 1)
                for t in range(NT):
                    ins = dve.tensor_scalar(xin[e % 2][:, t * P:(t + 1) * P], net.U[:, t, :], net.cw[:, t, e:e + 1], None, ALU.mult)
                ins.then_inc(x_ready, 1)

            def add(e):
                dve.wait_ge(yb_ready, e + 1)
                dve.wait_ge(added, e + 1)
                dve.tensor_tensor(net.acc[:], net.acc[:], yb[e % 2].rearrange("p (t d) -> p t d", t=NT), ALU.add).then_inc(added, 1)

            scale_rows(0)
            scale_rows(1)
            dve.wait_ge(s_relu, 1)
            dve.tensor_tensor(sA, sA, sA, ALU.mult)
            dve.tensor_tensor(sB, sB, sB, ALU.mult).then_inc(s_sq, 1)
            dve.wait_ge(s_down, 1)
            dve.tensor_copy(net.acc[:], PS[:, 3, :].rearrange("p (t d) -> p t d", t=NT)).then_inc(added, 1)
            for e in range(E):
                dve.wait_ge(hr_ready, 2 * (e + 1))
                dve.tensor_tensor(hA[e % 2], hA[e % 2], hA[e % 2], ALU.mult).then_inc(h_ready, 1)
                dve.tensor_tensor(hB[e % 2], hB[e % 2], hB[e % 2], ALU.mult).then_inc(h_ready, 1)
                if e + 2 < E:
                    scale_rows(e + 2)
                if e >= 1:
                    add(e - 1)
            add(E - 1)
    norm(net, net.acc, "ln", add_to=net.X)


STAGES = [l0_mixer, l0_experts, l1_mixer, l1_experts, l2_mixer, l2_experts, l3_mixer, l3_experts]


def sandwich(nc, x, out, w_dram):
    x_d = x.rearrange("(i b) (t p) d -> i p (b t) d", b=PAIR, p=P)
    out_d = out.rearrange("(i b) (t p) d -> i p (b t) d", b=PAIR, p=P)
    with ExitStack() as ctx:
        net = Net(nc, ctx, w_dram)
        load_weights(net)
        with nc.Fori(0, x.shape[0] // PAIR) as i:
            with net.stage("fetch", "x_landed") as (block, x_landed):
                @block.sync
                def _(sp):
                    sp.dma_start(net.X[:], x_d[i]).then_inc(x_landed, 16)
                    sp.wait_ge(x_landed, 16)
            first = net.stages
            for f in STAGES:
                f(net)
            with net.stage("store", "stored") as (block, stored):
                @block.sync
                def _(sp):
                    sp.dma_start(out_d[i], net.X[:]).then_inc(stored, 16)
                    sp.wait_ge(stored, 16)
            if (net.stages - first) % 2 == 0:
                with net.stage("even", "unused"):
                    pass


def constants():
    c = {"ident": np.eye(P), "zeros": np.zeros((P, P)), "iota8": np.tile(np.arange(E), (P, 1)),
         "eps": np.tile([LN_EPS, RMS_EPS], (P, 1))}
    for name, base in (("G", 1e6), ("L", 1e4)):
        inv = (1.0 / np.float32(base) ** (np.arange(0, HD, 2, dtype=np.float32) / np.float32(HD))).astype(np.float32)
        fr = (np.arange(SEQ, dtype=np.float32)[:, None] * inv[None, :]).astype(np.float32)
        for fn, tag in ((np.cos, "cos"), (np.sin, "sin")):
            t = fn(fr.astype(np.float64)).reshape(TPS, P, HD // 2)
            c[tag + name] = np.tile(t, (PAIR, 1, 1)).transpose(1, 0, 2)
    r = np.arange(P)
    c["mask_qk"] = np.where(r[:, None] >= r[None, :], 0.0, MASKED)
    c["mask_kq"] = np.ascontiguousarray(c["mask_qk"].T)
    k = np.arange(P + WINDOW) - WINDOW
    d = r[:, None] - k[None, :]
    c["lmask_qk"] = np.where((d >= 0) & (d < WINDOW), 0.0, MASKED)
    d = np.arange(P + WINDOW)[None, :] - r[:, None]
    c["lmask_kq"] = np.where((d >= 0) & (d < WINDOW), 0.0, MASKED)
    pick = np.zeros((8, HEADS, HEADS, P))
    pick[:3, np.arange(HEADS), np.arange(HEADS)] = 1.0
    c["pick_max"] = pick.reshape(P, HEADS * P)
    spread = np.zeros((4, 32, 16, 2, 64))
    gather = np.zeros((2, 64, 16, 32))
    for h in range(2):
        for k in range(16):
            spread[:, h * 16 + k, k, h, :] = 1.0
            gather[h, :, k, h * 16 + k] = 1.0
    c["spread"] = spread.reshape(P, 16 * P)
    c["gather"] = gather.reshape(P, 16, 32)
    return {n: np.ascontiguousarray(a, dtype=np.float32) for n, a in c.items()}


def lay_out(a):
    def col(n):
        return a[n].reshape(P, 1)

    def row(n):
        return np.broadcast_to(a[n].reshape(1, -1), (P, a[n].size))

    cat = np.concatenate
    w = {
        "L0a_alog": col("L0_attn_a_log"), "L0a_inw": col("L0_attn_input_norm_w"), "L0a_cout": col("L0_attn_c_out"),
        "L0a_dskip": col("L0_attn_d_skip"), "L0a_ffw": col("L0_attn_ff_norm_w"),
        "L0a_fc": a["L0_attn_ff_fc_w"].T, "L0a_proj": a["L0_attn_ff_proj_w"].T.reshape(2, P, P).transpose(1, 0, 2),
        "L0f_gate": a["L0_ffn_gate_w"].T, "L0f_gb": row("L0_ffn_gate_b"),
        "L0f_b2": cat([a["L0_ffn_b2"], a["L0_ffn_sb2"][None]]),
        "L0f_w2": cat([a["L0_ffn_w2"], a["L0_ffn_sw2"][None]]).transpose(2, 0, 1),
        "L1a_n1": col("L1_attn_norm1_w"), "L1a_n2": col("L1_attn_norm2_w"),
        "g_wq": a["L1_attn_g_wq"], "g_down": a["L1_attn_g_kv_down"],
        "g_up": cat([a["L1_attn_g_k_up"], a["L1_attn_g_v_up"]], 1), "g_wo": a["L1_attn_g_wo"],
        "l_wqkv": cat([a["L1_attn_l_wq"], a["L1_attn_l_wk"], a["L1_attn_l_wv"]], 1), "l_wo": a["L1_attn_l_wo"],
        "L1f_wqkv": cat([a["L1_ffn_wq"], a["L1_ffn_wk"], a["L1_ffn_wv"]], 2).transpose(1, 0, 2),
        "L1f_wo": a["L1_ffn_wo"].transpose(1, 0, 2), "L1f_gw": a["L1_ffn_gate_w"].transpose(1, 0, 2),
        "L1f_w1": a["L1_ffn_e_w1"].transpose(2, 0, 1, 3),
        "L1f_w2": a["L1_ffn_e_w2"].reshape(2, E, 4, P, P).transpose(3, 0, 1, 2, 4),
        "L1f_b1": a["L1_ffn_e_b1"].reshape(2, E, 4, P).transpose(3, 0, 1, 2), "L1f_b2": a["L1_ffn_e_b2"].transpose(1, 0, 2),
        "L2a_wqkv": cat([a["L2_attn_Wq"], a["L2_attn_Wk"], a["L2_attn_Wv"]]).T, "L2a_wo": a["L2_attn_Wo"].T,
        "L2a_gain": row("L2_attn_q_gain"), "L2a_mix": row("L2_attn_pair_mix").reshape(P, 8, 2, 2),
        "L2f_gate": a["L2_ffn_gate_w"].T, "L2f_gb": row("L2_ffn_gate_b"),
        "L2f_w": a["L2_ffn_expert_w"].transpose(2, 0, 1).reshape(P, E * P), "L2f_b": a["L2_ffn_expert_b"],
        "L3a_wq": a["L3_attn_Wq"], "L3a_wk": a["L3_attn_Wk"], "L3a_wv": a["L3_attn_Wv"], "L3a_wf1": a["L3_attn_Wf1"],
        "L3a_wf2": a["L3_attn_Wf2"], "L3a_wg1": a["L3_attn_Wg1"], "L3a_wg2": a["L3_attn_Wg2"], "L3a_wo": a["L3_attn_Wo"],
        "L3a_nw": col("L3_attn_norm_w"), "L3f_gate": a["L3_ffn_gate_w"].T, "L3f_eb": row("L3_ffn_expert_bias"),
        "L3f_up": a["L3_ffn_w_up"].transpose(2, 0, 1),
        "L3f_sup": a["L3_ffn_shared_w_up"].T,
    }
    dn, sdn = a["L3_ffn_w_down"].transpose(2, 0, 1), a["L3_ffn_shared_w_down"].T
    w["L3f_dnA"], w["L3f_dnB"], w["L3f_sdnA"], w["L3f_sdnB"] = dn[:P], dn[P:], sdn[:P], sdn[P:]
    for j in ("1", "3"):
        ww = cat([a["L0_ffn_w" + j], a["L0_ffn_sw" + j][None]])
        bb = cat([a["L0_ffn_b" + j], a["L0_ffn_sb" + j][None]])
        w["L0f_w" + j] = ww.reshape(E + 1, P, 2, P).transpose(3, 0, 2, 1)
        w["L0f_b" + j] = bb.reshape(E + 1, P, 2).transpose(1, 0, 2)
    for n, dst in (("ln1_w", "ln1w"), ("ln1_b", "ln1b"), ("ln2_w", "ln2w"), ("ln2_b", "ln2b")):
        w["L1f_" + dst] = a["L1_ffn_" + n].T
    for n, parts in (("bqkv", ("bq", "bk", "bv")), ("bo", ("bo",)), ("gb", ("gate_b",))):
        r = cat([a["L1_ffn_" + p] for p in parts], 1)
        w["L1f_" + n] = np.broadcast_to(r[None], (P,) + r.shape)
    return {n: np.ascontiguousarray(v) for n, v in w.items()}


def kernel(**inputs):
    import concourse.bacc as _bacc
    from concourse.bass_utils import run_bass_kernel_spmd as _run

    a = {n: np.asarray(v) for n, v in inputs.items()}
    nc = _bacc.Bacc("TRN2", target_bir_lowering=False, num_devices=1)
    arrays = {**lay_out(a), **constants()}
    w_dram = {n: nc.dram_tensor("in_" + n, v.shape, F32, kind="ExternalInput").ap() for n, v in arrays.items()}
    xs = a["L0_attn_x"]
    x = nc.dram_tensor("in_x", xs.shape, F32, kind="ExternalInput").ap()
    out = nc.dram_tensor("out", xs.shape, F32, kind="ExternalOutput").ap()
    sandwich(nc, x, out, w_dram)
    feeds = {"in_" + n: v for n, v in arrays.items()}
    feeds["in_x"] = np.ascontiguousarray(xs)
    r = _run(nc, [feeds], core_ids=[0])
    return r.results[0]["out"]
```

```python
from contextlib import ExitStack

import numpy as np

import concourse.bass as bass
from concourse import mybir

ACT = mybir.ActivationFunctionType
ALU = mybir.AluOpType
AX = mybir.AxisListType
F32 = mybir.dt.float32
BF16 = mybir.dt.bfloat16
U32 = mybir.dt.uint32

P = 128
SEQ = 256
PAIR = 2
NT = PAIR * SEQ // P
TOK = NT * P
TPS = SEQ // P
HEADS = 16
HD = P // HEADS
TERMS = 8
NB = HEADS // 2
VW = 32
UH = 4
WINDOW = 32
E = 8
MASKED = -1e30
LN_EPS = 1e-5
RMS_EPS = 1e-6


MASKS = ("pick_max", "spread", "mask_qk", "mask_kq", "lmask_qk", "lmask_kq")
IN_BF16 = ("L3f_up", "L3f_dnA", "L3f_dnB") + MASKS


NSIG = 17


class Chain:

    def __init__(self, eng, sem):
        self.eng, self.sem, self.n = eng, sem, 0

    def link(self, ins):
        self.n += 1
        ins.then_inc(self.sem, 1)
        self.eng.wait_ge(self.sem, self.n)


class Stage:

    def __init__(self, nc, sets, turn, names):
        self.nc, self.sems, self.last = nc, sets[turn % 2][:len(names.split())], sets[(turn + 1) % 2]
        assert len(self.sems) == len(names.split())

    def __enter__(self):
        self.block = self.nc.Block(no_gpsimd_drain=True)
        block = self.block.__enter__()

        @block.sync
        def _(sp):
            sp.sem_clear(range(self.last[0].num, self.last[-1].num + 1))

        return [block] + self.sems

    def __exit__(self, *exc):
        self.block.__exit__(*exc)


def bc(ap, shape):
    return ap.broadcast_to(shape)


def load_table(net, act, func, place=0):
    act.activation(net.scratch[:, place:place + 1], net.w["eps"][:, 0:1], func)


class Net:
    def __init__(self, nc, ctx, w_dram):
        self.nc = nc
        sems = [ctx.enter_context(nc.semaphore(f"signal{i}")) for i in range(2 * NSIG)]
        assert [s.num for s in sems] == list(range(sems[0].num, sems[0].num + 2 * NSIG))
        self.sems, self.stages = (sems[:NSIG], sems[NSIG:]), 0

        def sb(name, shape, dt=F32):
            return ctx.enter_context(nc.sbuf_tensor(name, shape, dt))

        self.sb = sb
        self.w_dram = w_dram
        self.w = {n: sb("w_" + n, list(a.shape)) for n, a in w_dram.items() if n not in IN_BF16}
        self.PS = ctx.enter_context(nc.psum_tensor("PS", [P, 8, 512], F32))
        self.X = sb("X", [P, NT, P])
        self.U = sb("U", [P, NT, P])
        self.V = sb("V", [P, NT, P])
        self.Y = sb("Y", [P, NT, P])
        self.R = sb("R", [P, NT, P])
        self.UT = sb("UT", [P, TOK])
        self.RT = sb("RT", [P, TOK])
        self.ident_bf = sb("ident_bf", [P, P], BF16)
        self.mask_bf = {n: sb("bf_" + n, list(w_dram[n].shape), BF16)
                        for n in MASKS}
        self.stats = sb("stats", [P, NT, 6])
        self.mv = sb("mv", [P, NT, 2])
        self.m2 = sb("m2", [P, NT, 1])
        self.sd = sb("sd", [P, NT, 1])
        self.rs = sb("rs", [P, NT, 1])
        self.scratch = sb("scratch", [P, 2])
        self.cw = sb("cw", [P, NT, E + 1])
        self.cwT32 = sb("cwT", [32, TOK])
        self.cwT = self.cwT32[0:E + 1, :]
        self.g = [sb(f"gate{i}", [P, NT, E]) for i in range(6)]
        self.g1 = [sb(f"gate_row{i}", [P, NT, 1]) for i in range(3)]
        self.gidx = sb("gidx", [P, NT, E], U32)
        self.hm = sb("hm", [P, PAIR])
        self.hmb = sb("hmb", [P, PAIR, P])
        self.qtok = sb("qtok", [P, NT, HEADS, HD])
        self.ktok = sb("ktok", [P, NT, HEADS, HD])
        self.vflat = sb("vflat", [P, NT * HEADS * (HD + 1) + VW])
        self.vaug = self.vflat[:, 0:NT * HEADS * (HD + 1)].rearrange("p (t h d) -> p t h d", t=NT, h=HEADS)
        tmps = sb("tmps", [P, 4, TOK])
        self.tmps = tmps
        self.tmp = [tmps[:, i, :].rearrange("p (t h d) -> p t h d", t=NT, h=HEADS) for i in range(4)]
        self.ss = sb("ss", [P, NT, 2 * HEADS])
        self.turned = sb("turned", [P, 2 * NB // 2, TOK])
        halves = [self.turned[:, 4 * i:4 * i + 4, :].rearrange("p a b -> p (a b)").bitcast(BF16) for i in range(2)]
        self.qT, self.kT = (a.rearrange("p (j n) -> p j n", j=NB) for a in halves)
        self.negm = sb("negm", [P, NT, HEADS])
        self.mres = sb("mres", [P, NT, HEADS])
        self.mparts = sb("mparts", [P, NT, 8, HEADS], BF16)
        self.mT = sb("mT", [P, TOK], BF16)
        self.latT = sb("latT", [32, TOK])
        self.big = sb("big", [P, 8, 512])
        self.orec = sb("orec", [P, NT, HEADS])
        self.acc = self.Y
        self.g_q, self.g_k, self.g_v, self.g_dk, self.g_dv = (self.turned[:, i, :] for i in range(5))
        self.g_f1, self.g_g1 = self.cwT32[0:16, :], self.latT[0:16, :]
        self.decay = sb("decay", [P, SEQ])
        self.parts = [self.big[:, 4 * i:4 * i + 4, :].rearrange("p a b -> p (a b)").bitcast(BF16).rearrange(
            "p (t h j d) -> p t h j d", t=NT, h=HEADS, j=TERMS) for i in range(2)]
        flat = self.big[:].rearrange("p a b -> p (a b)")
        nu, nd = E * 176, E * P
        self.w["L3f_up"] = flat[:, 0:nu].rearrange("p (e h) -> p e h", e=E)
        self.w["L3f_dnA"] = flat[:, nu:nu + nd].rearrange("p (e d) -> p e d", e=E)
        self.w["L3f_dnB"] = flat[0:48, nu + nd:nu + 2 * nd].rearrange("p (e d) -> p e d", e=E)
        at = nu + 2 * nd
        self.w["pick_max"] = self.turned[:, 0:4, :].rearrange("p a b -> p (a b)")
        self.w["spread"] = self.turned[:, 4:8, :].rearrange("p a b -> p (a b)")
        for n in MASKS[2:]:
            self.w[n] = flat[:, at:at + w_dram[n].shape[1]]
            at += w_dram[n].shape[1]
        self.up_bf = sb("up_bf", [P, E, 176], BF16)
        self.dnA_bf = sb("dnA_bf", [P, E, P], BF16)
        self.dnB_bf = sb("dnB_bf", [48, E, P], BF16)

    def k_rows(self, nkv):
        return self.ktok[:].rearrange("p t h d -> p (t h d)")[:, 0:NT * nkv * HD].rearrange(
            "p (t h d) -> p t h d", t=NT, h=nkv)

    def stage(self, tag, names):
        self.stages += 1
        return Stage(self.nc, self.sems, self.stages, names)


def load_weights(net):
    w, names = net.w, sorted(net.w)
    with net.stage("load", "loaded cleared dve_chain act_chain") as (block, loaded, cleared, dve_chain, act_chain):
        @block.sync
        def _(sp):
            for n in names[0::2]:
                sp.dma_start(w[n][:], net.w_dram[n]).then_inc(loaded, 16)
            sp.wait_ge(loaded, 16 * len(names))

        @block.gpsimd
        def _(pool):
            pool.memset(net.vflat[:], 1.0).then_inc(cleared, 1)
            pool.memset(net.mparts[:], 0.0).then_inc(cleared, 1)
            pool.memset(net.cw[:], 1.0).then_inc(cleared, 1)
            pool.wait_ge(cleared, 3)

        @block.vector
        def _(dve):
            dve.wait_ge(loaded, 16 * len(names))
            dve.tensor_copy(net.ident_bf[:], w["ident"][:])
            for n, m in net.mask_bf.items():
                dve.tensor_copy(m[:], w[n][:])
            dve.tensor_copy(net.up_bf[:], w["L3f_up"][:])
            dve.tensor_copy(net.dnA_bf[:], w["L3f_dnA"][:])
            dve.tensor_copy(net.dnB_bf[:], w["L3f_dnB"][:])
            dve.memset(net.decay[:], 0.0)

        @block.scalar
        def _(act):
            chain = Chain(act, act_chain)
            for n in names[1::2]:
                act.dma_start(w[n][:], net.w_dram[n]).then_inc(loaded, 16)
            act.wait_ge(loaded, 16 * len(names))
            chain.link(act.activation(w["L0a_alog"][:], w["L0a_alog"][:], ACT.Exp))
            chain.link(act.activation(w["L0a_alog"][:], w["L0a_alog"][:], ACT.Exp, scale=-1.0))
    with net.stage("decay", "dve_chain") as (block, dve_chain):
        @block.vector
        def _(dve):
            chain = Chain(dve, dve_chain)
            chain.link(dve.tensor_scalar(net.decay[:], net.decay[:], w["L0a_alog"][:, 0:1], None, ALU.add))


def norm(net, src, kind, tok=None, T=None, scale=None, bias=None, add_to=None, before=()):
    norms(net, [*before, (src, kind, tok, T, scale, bias, add_to)])


def last_norm(src, kind, add_to):
    return [(src, kind, None, None, None, None, add_to)]


def norms(net, steps):
    PS, w = net.PS, net.w
    with net.stage("norm", "var_ready sd_ready tok_ready turned T_ready dve_chain") as (
            block, var_ready, sd_ready, tok_ready, turned, T_ready, dve_chain):
        @block.vector
        def _(dve):
            chain = Chain(dve, dve_chain)
            for s, (src, kind, tok, T, scale, bias, add_to) in enumerate(steps):
                tok = net.R if tok is None else tok
                for t in range(NT):
                    last = dve.bn_stats(net.stats[:, t, :], src[:, t, :])
                chain.link(last)
                for t in range(NT):
                    last = dve.bn_aggr(net.mv[:, t, :], net.stats[:, t, :])
                if kind == "rms":
                    chain.link(last)
                    chain.link(dve.tensor_tensor(net.m2[:], net.mv[:, :, 0:1], net.mv[:, :, 0:1], ALU.mult))
                    last = dve.tensor_tensor(net.mv[:, :, 1:2], net.mv[:, :, 1:2], net.m2[:], ALU.add)
                last.then_inc(var_ready, 1)
                dve.wait_ge(sd_ready, s + 1)
                chain.link(dve.reciprocal(net.rs[:], net.sd[:]))
                for t in range(NT):
                    if kind == "ln":
                        ins = dve.tensor_scalar(tok[:, t, :], src[:, t, :], net.mv[:, t, 0:1], net.rs[:, t, 0:1],
                                                ALU.subtract, ALU.mult)
                    else:
                        ins = dve.tensor_scalar(tok[:, t, :], src[:, t, :], net.rs[:, t, 0:1], None, ALU.mult)
                    ins.then_inc(tok_ready, 1)
                if add_to is not None or s + 1 < len(steps):
                    dve.wait_ge(tok_ready, NT * (s + 1))
                if add_to is not None:
                    chain.link(dve.tensor_tensor(add_to[:], add_to[:], tok[:], ALU.add))

        @block.scalar
        def _(act):
            load_table(net, act, ACT.Sqrt)
            for s, (src, kind, tok, T, scale, bias, add_to) in enumerate(steps):
                act.wait_ge(var_ready, s + 1)
                act.activation(net.sd[:], net.mv[:, :, 1:2], ACT.Sqrt,
                               bias=w["eps"][:, 0:1] if kind == "ln" else w["eps"][:, 1:2]).then_inc(sd_ready, 1)
            if T is not None:
                act.wait_ge(turned, 1)
                act.activation(T[:], PS[:, 0, :], ACT.Identity, scale=1.0 if scale is None else scale,
                               bias=0.0 if bias is None else bias).then_inc(T_ready, 1)

        src, kind, tok, T, scale, bias, add_to = steps[-1]
        if T is not None:
            @block.tensor
            def _(pe):
                done = NT * (len(steps) - 1)
                for t in range(NT):
                    pe.wait_ge(tok_ready, done + t + 1)
                    ins = pe.transpose(PS[:, 0, t * P:(t + 1) * P], (net.R if tok is None else tok)[:, t, :], w["ident"][:])
                ins.then_inc(turned, 1)


def l0_mixer(net, before):
    w, PS, big = net.w, net.PS, net.big
    pre = (net.X, "ln", net.U, None, None, None, None)
    norm(net, net.U, "rms", T=net.RT, scale=w["L0a_inw"][:, 0:1], before=[*before, pre])
    scanT, skipT = big[:, 0, :], big[:, 1, :]
    with net.stage("l0scan", "mixed turned dve_chain") as (block, mixed, turned, dve_chain):
        @block.vector
        def _(dve):
            chain = Chain(dve, dve_chain)
            for b in range(PAIR):
                at = slice(b * SEQ, (b + 1) * SEQ)
                dve.tensor_tensor_scan(scanT[:, at], net.decay[:], net.RT[:, at], 0.0, ALU.mult, ALU.add)
            chain.link(dve.tensor_scalar(skipT, net.RT[:], w["L0a_dskip"][:, 0:1], None, ALU.mult))
            dve.scalar_tensor_tensor(out=scanT, in0=scanT, scalar=w["L0a_cout"][:, 0:1], in1=skipT,
                                     op0=ALU.mult, op1=ALU.add).then_inc(mixed, 1)
            dve.wait_ge(turned, 1)
            dve.tensor_tensor(net.V[:], PS[:, 0, :].rearrange("p (t d) -> p t d", t=NT), net.U[:], ALU.add)

        @block.tensor
        def _(pe):
            pe.wait_ge(mixed, 1)
            for t in range(NT):
                ins = pe.transpose(PS[:, 0, t * P:(t + 1) * P], scanT[:, t * P:(t + 1) * P], w["ident"][:])
            ins.then_inc(turned, 1)
    norm(net, net.V, "rms", T=net.RT, scale=w["L0a_ffw"][:, 0:1])
    with net.stage("l0mlp", "up hidden down") as (block, up, hidden, down):
        @block.tensor
        def _(pe):
            for f in range(2):
                pe.matmul(PS[:, f, :], w["L0a_fc"][:, f * P:(f + 1) * P], net.RT[:], start=True, stop=True).then_inc(up, 1)
            pe.wait_ge(hidden, 2)
            for t in range(NT):
                for f in range(2):
                    ins = pe.matmul(PS[:, 2, t * P:(t + 1) * P], big[:, f, t * P:(t + 1) * P], w["L0a_proj"][:, f, :],
                                    start=f == 0, stop=f == 1)
            ins.then_inc(down, 1)

        @block.scalar
        def _(act):
            load_table(net, act, ACT.Silu)
            for f in range(2):
                act.wait_ge(up, f + 1)
                act.activation(big[:, f, :], PS[:, f, :], ACT.Silu).then_inc(hidden, 1)

        @block.vector
        def _(dve):
            dve.wait_ge(down, 1)
            dve.tensor_tensor(net.Y[:], PS[:, 2, :].rearrange("p (t d) -> p t d", t=NT), net.V[:], ALU.add)
    return last_norm(net.Y, "ln", add_to=net.X)


def route(net, mode, gate_w, logit_bias=None, select_bias=None, turn_weights=0, mean=False):
    PS = net.PS
    with net.stage("route", "mean_ready logits_ready centred exp_ready weights_ready turned dve_chain") as (
            block, mean_ready, logits_ready, centred, exp_ready, weights_ready, turned, dve_chain):
        @block.tensor
        def _(pe):
            if mean:
                pe.wait_ge(mean_ready, 1)
            gate_logits(net, pe, 0, gate_w, mean, logits_ready)
            if turn_weights:
                pe.wait_ge(weights_ready, 1)
                turn_routing(net, pe, 1, turn_weights, turned)

        @block.scalar
        def _(act):
            load_table(net, act, ACT.Sigmoid if mode == "sigmoid" else ACT.Exp)
            act.wait_ge(centred, 1)
            routing_exp(net, act, mode, exp_ready)
            if turn_weights:
                act.wait_ge(turned, 1)
                act.activation(net.cwT[0:turn_weights, :], PS[0:turn_weights, 1, :], ACT.Identity)

        @block.vector
        def _(dve):
            chain = Chain(dve, dve_chain)
            if mean:
                sequence_means(net, dve, chain, mean_ready)
            choose(net, dve, chain, mode, 0, logits_ready, centred, exp_ready, weights_ready, logit_bias, select_bias)


def gate_logits(net, pe, bank, gate_w, mean, logits_ready):
    for t in range(NT):
        rows = net.hmb[:, t // TPS, :] if mean else net.UT[:, t * P:(t + 1) * P]
        ins = pe.matmul(net.PS[:, bank, t * E:(t + 1) * E], rows, gate_w, start=True, stop=True)
    ins.then_inc(logits_ready, 1)


def turn_routing(net, pe, bank, rows, turned):
    for t in range(NT):
        ins = pe.transpose(net.PS[0:rows, bank, t * P:(t + 1) * P], net.cw[:, t, 0:rows], net.w["ident"][:])
    ins.then_inc(turned, 1)


def routing_exp(net, act, mode, exp_ready):
    logits, ex = net.g[0:2]
    act.activation(ex[:], logits[:], ACT.Sigmoid if mode == "sigmoid" else ACT.Exp).then_inc(exp_ready, 1)


def sequence_means(net, dve, chain, mean_ready):
    chain.link(dve.tensor_reduce(net.hm[:], net.UT[:].rearrange("p (b s) -> p b s", b=PAIR), AX.X, ALU.add))
    chain.link(dve.tensor_scalar(net.hm[:], net.hm[:], 1.0 / SEQ, None, ALU.mult))
    for b in range(PAIR):
        last = dve.tensor_scalar(net.hmb[:, b, :], net.w["zeros"][:], net.hm[:, b:b + 1], None, ALU.add)
    last.then_inc(mean_ready, 1)


def choose(net, dve, chain, mode, bank, logits_ready, centred, exp_ready, weights_ready, logit_bias=None, select_bias=None):
    w, PS = net.w, net.PS
    logits, ex, score, pick, sel0, sel1 = net.g
    top, total, rec = net.g1
    dve.wait_ge(logits_ready, 1)
    raw = PS[:, bank, 0:NT * E].rearrange("p (t e) -> p t e", t=NT)
    if logit_bias is not None:
        chain.link(dve.tensor_tensor(logits[:], raw, bc(logit_bias.unsqueeze(1), [P, NT, E]), ALU.add))
    else:
        chain.link(dve.tensor_copy(logits[:], raw))
    if mode == "sigmoid":
        last = dve.tensor_copy(sel0[:], logits[:])
    else:
        chain.link(dve.tensor_reduce(top[:], logits[:], AX.X, ALU.max))
        last = dve.tensor_tensor(logits[:], logits[:], bc(top[:], [P, NT, E]), ALU.subtract)
    last.then_inc(centred, 1)
    dve.wait_ge(exp_ready, 1)
    dve.wait_ge(centred, 1)
    if mode == "all":
        chain.link(dve.tensor_reduce(total[:], ex[:], AX.X, ALU.add))
        chain.link(dve.reciprocal(rec[:], total[:]))
        chain.link(dve.tensor_tensor(score[:], ex[:], bc(rec[:], [P, NT, E]), ALU.mult))
    else:
        chain.link(dve.tensor_copy(score[:], ex[:]))
    if select_bias is not None:
        chain.link(dve.tensor_tensor(pick[:], score[:], bc(select_bias.unsqueeze(1), [P, NT, E]), ALU.add))
    else:
        chain.link(dve.tensor_copy(pick[:], logits[:] if mode == "two" else score[:]))
    for t in range(NT):
        last = dve.max(sel0[:, t, :], pick[:, t, :])
    chain.link(last)
    for t in range(NT):
        last = dve.max_index(net.gidx[:, t, :], sel0[:, t, :], pick[:, t, :])
    chain.link(last)
    chain.link(dve.tensor_copy(pick[:], net.gidx[:]))
    places = bc(w["iota8"][:].unsqueeze(1), [P, NT, E])
    dve.tensor_tensor(sel0[:], places, bc(pick[:, :, 0:1], [P, NT, E]), ALU.is_equal)
    chain.link(dve.tensor_tensor(sel1[:], places, bc(pick[:, :, 1:2], [P, NT, E]), ALU.is_equal))
    chain.link(dve.tensor_tensor(sel0[:], sel0[:], sel1[:], ALU.add))
    last = dve.tensor_tensor(net.cw[:, :, 0:E], score[:], sel0[:], ALU.mult)
    if mode == "two":
        chain.link(last)
        chain.link(dve.tensor_reduce(total[:], net.cw[:, :, 0:E], AX.X, ALU.add))
        chain.link(dve.reciprocal(rec[:], total[:]))
        last = dve.tensor_tensor(net.cw[:, :, 0:E], net.cw[:, :, 0:E], bc(rec[:], [P, NT, E]), ALU.mult)
    last.then_inc(weights_ready, 1)


def weighted_biases(net, pe, rows, bank, biases, done):
    for t in range(NT):
        ins = pe.matmul(net.PS[:, bank, t * P:(t + 1) * P], net.cwT[0:rows, t * P:(t + 1) * P], biases, start=True, stop=True)
    ins.then_inc(done, 1)


def l0_experts(net, before):
    w, PS, big = net.w, net.PS, net.big
    norm(net, net.X, "ln", T=net.UT, before=before)
    n = E + 1
    h1 = [big[:, i, :] for i in range(2)]
    prod = [big[:, 2 + i, :] for i in range(2)]
    gated, act_out = big[:, 4, :], [big[:, 6 + i, :] for i in range(2)]
    sig = big[:, 5, :]
    with net.stage("l0exp", "up h1_ready prod_ready gate_ready sig_ready lin_ready a_ready y_ready acc_ready bias_ready "
                   "logits_ready centred exp_ready weights_ready turned cwT_ready dve_chain") as (
            block, up, h1_ready, prod_ready, gate_ready, sig_ready, lin_ready, a_ready, y_ready, acc_ready, bias_ready,
            logits_ready, centred, exp_ready, weights_ready, turned, cwT_ready, dve_chain):
        @block.tensor
        def _(pe):
            gate_logits(net, pe, 7, w["L0f_gate"][:], False, logits_ready)

            def down(e):
                pe.wait_ge(a_ready, e + 1)
                if e == 1:
                    pe.wait_ge(acc_ready, 1)
                if e >= 2:
                    pe.wait_ge(acc_ready, e)
                for t in range(NT):
                    ins = pe.matmul(PS[:, 6 + e % 2, t * P:(t + 1) * P], act_out[e % 2][:, t * P:(t + 1) * P],
                                    w["L0f_w2"][:, e, :], start=True, stop=True)
                ins.then_inc(y_ready, 1)

            for e in range(n):
                if e == 2:
                    pe.wait_ge(cwT_ready, 1)
                    weighted_biases(net, pe, n, 7, w["L0f_b2"][:], bias_ready)
                for half in range(2):
                    u = 2 * e + half
                    b = 2 * (u % 3)
                    if u >= 3:
                        pe.wait_ge(h1_ready, u - 2)
                        pe.wait_ge(prod_ready, u - 2)
                    pe.matmul(PS[:, b, :], w["L0f_w1"][:, e, half, :], net.UT[:], start=True, stop=True)
                    pe.matmul(PS[:, b + 1, :], w["L0f_w3"][:, e, half, :], net.UT[:], start=True, stop=True).then_inc(up, 1)
                if e == 1:
                    pe.wait_ge(weights_ready, 1)
                    turn_routing(net, pe, 7, n, turned)
                if e >= 2:
                    down(e - 2)
            down(n - 2)
            down(n - 1)

        @block.scalar
        def _(act):
            def take_h1(u):
                act.wait_ge(up, u + 1)
                if u >= 2:
                    act.wait_ge(prod_ready, u - 1)
                act.activation(h1[u % 2], PS[:, 2 * (u % 3), :], ACT.Identity,
                               bias=w["L0f_b1"][:, u // 2, u % 2:u % 2 + 1]).then_inc(h1_ready, 1)

            load_table(net, act, ACT.Exp)
            take_h1(0)
            act.wait_ge(centred, 1)
            routing_exp(net, act, "all", exp_ready)
            load_table(net, act, ACT.Sigmoid, place=1)
            take_h1(1)
            for e in range(n):
                if e == 1:
                    act.wait_ge(turned, 1)
                    act.activation(net.cwT[:], PS[0:n, 7, :], ACT.Identity).then_inc(cwT_ready, 1)
                act.wait_ge(gate_ready, e + 1)
                if e >= 1:
                    act.wait_ge(a_ready, e)
                act.activation(sig, gated, ACT.Sigmoid, scale=1.702).then_inc(sig_ready, 1)
                if e + 1 < n:
                    take_h1(2 * e + 2)
                    take_h1(2 * e + 3)

        @block.gpsimd
        def _(pool):
            for e in range(n):
                pool.wait_ge(prod_ready, 2 * e + 2)
                pool.tensor_scalar(prod[1], prod[1], 7.0, -7.0, ALU.min, ALU.max).then_inc(lin_ready, 1)

        @block.vector
        def _(dve):
            chain = Chain(dve, dve_chain)
            choose(net, dve, chain, "all", 7, logits_ready, centred, exp_ready, weights_ready, select_bias=w["L0f_gb"][:])

            def add(e):
                dve.wait_ge(y_ready, e + 1)
                dve.wait_ge(acc_ready, e + 1)
                for t in range(NT):
                    ins = dve.scalar_tensor_tensor(out=net.acc[:, t, :], in0=PS[:, 6 + e % 2, t * P:(t + 1) * P],
                                                   scalar=net.cw[:, t, e:e + 1], in1=net.acc[:, t, :],
                                                   op0=ALU.mult, op1=ALU.add)
                ins.then_inc(acc_ready, 1)

            for u in range(2 * n):
                e, half = u // 2, u % 2
                if u == 4:
                    dve.wait_ge(weights_ready, 1)
                    dve.wait_ge(bias_ready, 1)
                    dve.tensor_copy(net.acc[:], PS[:, 7, :].rearrange("p (t d) -> p t d", t=NT)).then_inc(acc_ready, 1)
                dve.wait_ge(h1_ready, u + 1)
                dve.scalar_tensor_tensor(out=prod[half], in0=PS[:, 2 * (u % 3) + 1, :],
                                         scalar=w["L0f_b3"][:, e, half:half + 1], in1=h1[u % 2],
                                         op0=ALU.add, op1=ALU.mult).then_inc(prod_ready, 1)
                dve.wait_ge(prod_ready, u + 1)
                if half == 0:
                    if e >= 1:
                        dve.wait_ge(sig_ready, e)
                    dve.tensor_scalar(gated, prod[0], 7.0, None, ALU.min).then_inc(gate_ready, 1)
                else:
                    if e >= 3:
                        add(e - 3)
                    dve.wait_ge(lin_ready, e + 1)
                    chain.link(dve.scalar_tensor_tensor(out=prod[1], in0=prod[1], scalar=1.0, in1=gated,
                                                        op0=ALU.add, op1=ALU.mult))
                    dve.wait_ge(sig_ready, e + 1)
                    if e >= 2:
                        dve.wait_ge(y_ready, e - 1)
                    dve.tensor_tensor(act_out[e % 2], prod[1], sig, ALU.mult).then_inc(a_ready, 1)
            for e in range(n - 3, n):
                add(e)
    return last_norm(net.acc, "ln", add_to=net.X)


def rotate(dve, chain, net, src, dst, nh, cos, sin, halves):
    if halves:
        a, b = src[:, :, 0:nh, 0:4], src[:, :, 0:nh, 4:8]
        oa, ob = dst[:, :, 0:nh, 0:4], dst[:, :, 0:nh, 4:8]
    else:
        a, b = src[:, :, 0:nh, 0::2], src[:, :, 0:nh, 1::2]
        oa, ob = dst[:, :, 0:nh, 0::2], dst[:, :, 0:nh, 1::2]
    shape = [P, NT, nh, 4]
    c, s = bc(cos.unsqueeze(2), shape), bc(sin.unsqueeze(2), shape)
    t = net.tmp
    ac, bs = t[0][:, :, 0:nh, 0:4], t[0][:, :, 0:nh, 4:8]
    as_, bcs = t[1][:, :, 0:nh, 0:4], t[1][:, :, 0:nh, 4:8]
    dve.tensor_tensor(ac, a, c, ALU.mult)
    dve.tensor_tensor(bs, b, s, ALU.mult)
    dve.tensor_tensor(as_, a, s, ALU.mult)
    chain.link(dve.tensor_tensor(bcs, b, c, ALU.mult))
    dve.tensor_tensor(oa, ac, bs, ALU.add if halves else ALU.subtract)
    chain.link(dve.tensor_tensor(ob, bcs, as_, ALU.subtract if halves else ALU.add))


def project(net, kind, wqkv, nkv, cos=None, sin=None, bias=None, gain=None):
    w, PS = net.w, net.PS
    kvw = nkv * HD
    width = P + 2 * kvw
    with net.stage("proj", "lat_ready latT_ready proj_ready sq_ready sd_ready dve_chain") as (
            block, lat_ready, latT_ready, proj_ready, sq_ready, sd_ready, dve_chain):
        @block.tensor
        def _(pe):
            if kind == "latent":
                pe.matmul(PS[0:32, 4, :], w["g_down"][:], net.UT[:], start=True, stop=True).then_inc(lat_ready, 1)
                pe.wait_ge(latT_ready, 1)
            for t in range(NT):
                u = net.UT[:, t * P:(t + 1) * P]
                if kind == "latent":
                    pe.matmul(PS[:, t, 0:P], u, w["g_wq"][:], start=True, stop=True)
                    ins = pe.matmul(PS[:, t, P:width], net.latT[:, t * P:(t + 1) * P], w["g_up"][:], start=True, stop=True)
                else:
                    ins = pe.matmul(PS[:, t, 0:width], u, wqkv, start=True, stop=True)
            ins.then_inc(proj_ready, 1)

        @block.scalar
        def _(act):
            if kind == "latent":
                act.wait_ge(lat_ready, 1)
                act.activation(net.latT[:], PS[0:32, 4, :], ACT.Identity).then_inc(latT_ready, 1)
            if kind != "plain":
                load_table(net, act, ACT.Sqrt)
                act.wait_ge(sq_ready, 1)
                act.activation(net.ss[:, :, 0:HEADS + nkv], net.ss[:, :, 0:HEADS + nkv], ACT.Sqrt, scale=1.0 / HD,
                               bias=w["eps"][:, 1:2]).then_inc(sd_ready, 1)

        @block.vector
        def _(dve):
            chain = Chain(dve, dve_chain)
            dve.wait_ge(proj_ready, 1)
            q = PS[:, 0:NT, 0:P].rearrange("p t (h d) -> p t h d", d=HD)
            k = PS[:, 0:NT, P:P + kvw].rearrange("p t (h d) -> p t h d", d=HD)
            v = PS[:, 0:NT, P + kvw:width].rearrange("p t (h d) -> p t h d", d=HD)
            K = net.k_rows(nkv)
            if kind == "plain":
                for src, dst, o in ((q, net.qtok, 0), (k, net.ktok, P)):
                    brow = bias[:, o:o + P].rearrange("p (h d) -> p h d", d=HD).unsqueeze(1)
                    last = dve.tensor_tensor(dst[:], src, bc(brow, [P, NT, HEADS, HD]), ALU.add)
                brow = bias[:, 2 * P:3 * P].rearrange("p (h d) -> p h d", d=HD).unsqueeze(1)
                dve.tensor_tensor(net.vaug[:, :, :, 0:HD], v, bc(brow, [P, NT, HEADS, HD]), ALU.add)
                chain.link(last)
            else:
                dve.tensor_copy(net.vaug[:, :, 0:nkv, 0:HD], v)
                if kind == "norm_rope":
                    dve.tensor_copy(net.qtok[:], q)
                    chain.link(dve.tensor_copy(K, k))
                else:
                    rotate(dve, chain, net, q, net.qtok, HEADS, cos, sin, False)
                    rotate(dve, chain, net, k, K, nkv, cos, sin, False)
                dve.tensor_tensor(net.tmp[2], net.qtok[:], net.qtok[:], ALU.mult)
                chain.link(dve.tensor_tensor(net.tmp[3][:, :, 0:nkv, :], K, K, ALU.mult))
                dve.tensor_reduce(net.ss[:, :, 0:HEADS], net.tmp[2], AX.X, ALU.add)
                dve.tensor_reduce(net.ss[:, :, HEADS:HEADS + nkv], net.tmp[3][:, :, 0:nkv, :], AX.X, ALU.add).then_inc(sq_ready, 1)
                dve.wait_ge(sd_ready, 1)
                chain.link(dve.reciprocal(net.ss[:, :, 0:HEADS + nkv], net.ss[:, :, 0:HEADS + nkv]))
                dve.tensor_tensor(net.qtok[:], net.qtok[:], bc(net.ss[:, :, 0:HEADS].unsqueeze(3), [P, NT, HEADS, HD]), ALU.mult)
                chain.link(dve.tensor_tensor(K, K, bc(net.ss[:, :, HEADS:HEADS + nkv].unsqueeze(3), [P, NT, nkv, HD]), ALU.mult))
                if kind == "norm_rope":
                    rotate(dve, chain, net, net.qtok, net.tmp[2], HEADS, cos, sin, True)
                    rotate(dve, chain, net, K, net.tmp[3], nkv, cos, sin, True)
                    g = gain.unsqueeze(1).unsqueeze(3)
                    dve.tensor_tensor(net.qtok[:], net.tmp[2], bc(g, [P, NT, HEADS, HD]), ALU.mult)
                    chain.link(dve.tensor_copy(K, net.tmp[3][:, :, 0:nkv, :]))


def attend(net, local, with_max, scale, nkv):
    w, PS = net.w, net.PS
    mask_qk, mask_kq = (net.mask_bf[("l" if local else "") + m] for m in ("mask_qk", "mask_kq"))
    pick_max = net.mask_bf["pick_max"].rearrange("p (h c) -> p h c", h=HEADS)
    wide = P + WINDOW if local else 2 * P
    cols = wide + P
    units = [(b, g) for b in range(PAIR) for g in range(HEADS // UH)]
    NU = len(units)
    ex = [net.big[:, 4 * n:4 * n + 4, :] for n in range(2)]
    gqa = nkv < HEADS
    nkb = nkv if gqa else NB
    Q = net.qtok
    q_parts, k_parts = net.parts
    psb = PS[:].bitcast(BF16)

    with net.stage("split", "q_split k_split k_rounded turned dve_chain pool_chain") as (
            block, q_split, k_split, k_rounded, turned, dve_chain, pool_chain):
        @block.vector
        def _(dve):
            chain = Chain(dve, dve_chain)
            qh = Q[:].rearrange("p t h d -> p (t h) d")
            parts = q_parts.rearrange("p t h j d -> p (t h) j d")
            r = net.tmp[0].rearrange("p t h d -> p (t h) d")
            src, at = qh, 0
            for n in (3, 3, 2):
                ins = dve.tensor_copy(parts[:, :, at:at + n, :], bc(src.unsqueeze(2), [P, NT * HEADS, n, HD]))
                if at < 6:
                    chain.link(ins)
                    chain.link(dve.tensor_tensor(r, src, parts[:, :, at, :], ALU.subtract))
                    src, at = r, at + n
            ins.then_inc(q_split, 1)
            for n in range(NB // 2):
                dve.wait_ge(turned, n + 1)
                dve.tensor_copy(net.qT[:, 2 * n:2 * n + 2, :], psb[:, n, :].rearrange("p (j n) -> p j n", j=2))

        if gqa:
            kk = k_parts.rearrange("p t h j d -> p (t h j d)")[:, 0:NT * nkv * P].rearrange(
                "p (t h u j d) -> p (t h) u j d", t=NT, h=nkv, u=2, j=TERMS)
            spots = [kk[:, :, u] for u in range(2)]
        else:
            spots = [k_parts.rearrange("p t h j d -> p (t h) j d")]
        nth = NT * nkv
        keys_all = net.k_rows(nkv).rearrange("p t h d -> p (t h) d")
        res = net.tmp[1].rearrange("p t h d -> p (t h) d")[:, 0:nth, :]

        @block.scalar
        def _(act):
            for m in range(3):
                if m:
                    act.wait_ge(k_split, m)
                for spot in spots:
                    at = spot[:, :, m::3, :]
                    n = at.shape[2]
                    src = keys_all if m == 0 else res
                    ins = act.activation(at, bc(src.unsqueeze(2), [P, nth, n, HD]), ACT.Identity)
                ins.then_inc(k_rounded, 1)
            for n in range(nkb // 2):
                act.wait_ge(turned, NB // 2 + n + 1)
                act.activation(net.kT[:, 2 * n:2 * n + 2, :], psb[:, 4 + n, :].rearrange("p (j n) -> p j n", j=2), ACT.Identity)

        @block.gpsimd
        def _(pool):
            for m in range(2):
                pool.wait_ge(k_rounded, m + 1)
                src = keys_all if m == 0 else res
                pool.tensor_tensor(res, src, spots[0][:, :, m, :], ALU.subtract).then_inc(k_split, 1)
                if m == 0:
                    pool.wait_ge(k_split, 1)

        @block.tensor
        def _(pe):
            pe.wait_ge(q_split, 1)
            for j in range(NB):
                for t in range(NT):
                    rows = q_parts[:, t, 2 * j:2 * j + 2].rearrange("p h j d -> p (h j d)")
                    ins = pe.transpose(psb[:, j // 2, (j % 2) * TOK + t * P:(j % 2) * TOK + (t + 1) * P], rows, net.ident_bf[:])
                if j % 2:
                    ins.then_inc(turned, 1)
            pe.wait_ge(k_rounded, 3)
            for j in range(nkb):
                for t in range(NT):
                    at = (t * nkb + j) * P
                    rows = k_parts.rearrange("p t h j d -> p (t h j d)")[:, at:at + P]
                    ins = pe.transpose(psb[:, 4 + j // 2, (j % 2) * TOK + t * P:(j % 2) * TOK + (t + 1) * P], rows, net.ident_bf[:])
                if j % 2:
                    ins.then_inc(turned, 1)

    def head_rows(h):
        return slice(64 * (h % 2), 64 * (h % 2) + 64)

    def queries(h, q0, n):
        return net.qT[head_rows(h), h // 2, q0:q0 + n]

    def keys(h, k0, n):
        return net.kT[head_rows(h), h // UH if gqa else h // 2, k0:k0 + n]

    if with_max:
        with net.stage("rowmax", "scores_ready max_ready turned parts_ready dve_chain") as (
                block, scores_ready, max_ready, turned, parts_ready, dve_chain):
            @block.tensor
            def _(pe):
                for n, (b, g) in enumerate(units):
                    if n >= 2:
                        pe.wait_ge(max_ready, n - 1)
                    base = 4 * (n % 2)
                    k0 = P - WINDOW if local else 0
                    for t, (c, klo) in enumerate(((0, 0), (P, k0))):
                        wd = P if t == 0 else wide
                        for s in range(UH):
                            h = UH * g + s
                            pe.matmul(PS[:, base + s, c:c + wd], queries(h, b * SEQ + t * P, P), keys(h, b * SEQ + klo, wd),
                                      start=t == 0, stop=False, skip_group_check=True)
                    for t, c in enumerate((0, P)):
                        wd = P if t == 0 else wide
                        m = wd if local and t == 1 else P
                        for s in range(UH):
                            ins = pe.matmul(PS[:, base + s, c + wd - m:c + wd], net.ident_bf[:],
                                            mask_qk[:, mask_qk.shape[1] - m:], start=False, stop=True, skip_group_check=True)
                    ins.then_inc(scores_ready, 1)
                pe.wait_ge(parts_ready, 1)
                for t in range(NT):
                    ins = pe.transpose(psb[:, 0, t * P:(t + 1) * P], net.mparts[:, t].rearrange("p a h -> p (a h)"), net.ident_bf[:])
                ins.then_inc(turned, 1)

            @block.vector
            def _(dve):
                chain = Chain(dve, dve_chain)
                for n, (b, g) in enumerate(units):
                    dve.wait_ge(scores_ready, n + 1)
                    base = 4 * (n % 2)
                    heads = slice(UH * g, UH * g + UH)
                    dve.tensor_reduce(net.negm[:, TPS * b, heads], PS[:, base:base + 4, 0:P], AX.X, ALU.max, negate=True)
                    dve.tensor_reduce(net.negm[:, TPS * b + 1, heads], PS[:, base:base + 4, P:cols], AX.X, ALU.max,
                                      negate=True).then_inc(max_ready, 1)
                dve.wait_ge(max_ready, NU)
                src = net.negm
                for m in range(3):
                    ins = dve.tensor_copy(net.mparts[:, :, m, :], src[:])
                    if m < 2:
                        chain.link(ins)
                        chain.link(dve.tensor_tensor(net.mres[:], src[:], net.mparts[:, :, m, :], ALU.subtract))
                        src = net.mres
                ins.then_inc(parts_ready, 1)
                dve.wait_ge(turned, 1)
                dve.tensor_copy(net.mT[:], psb[:, 0, 0:TOK])

    outT = net.tmps[:].rearrange("p a b -> p (a b)").rearrange("p (n q) -> p n q", n=NU)
    with net.stage("attend", "scores_ready exp_ready out_ready out_read turned rec_ready") as (
            block, scores_ready, exp_ready, out_ready, out_read, turned, rec_ready):
        @block.tensor
        def _(pe):
            def scores(n):
                b, g = units[n]
                base = 4 * (n % 2)
                tiles = [(c, wd, b * SEQ + kt * P) for kt, (c, wd) in enumerate(((0, wide), (wide, P)))]
                for heads in (range(1, UH), range(1)):
                    if n >= 2 and 0 in heads:
                        pe.wait_ge(out_read, n - 1)
                    for c, wd, q0 in tiles:
                        for s in heads:
                            h = UH * g + s
                            pe.matmul(PS[:, base + s, c:c + wd], keys(h, q0, P), queries(h, q0, wd), start=c == 0, stop=False,
                                      skip_group_check=True)
                    for c, wd, q0 in tiles:
                        m = wd if local else P
                        for s in heads:
                            ins = pe.matmul(PS[:, base + s, c:c + m], net.ident_bf[:], mask_kq[:, 0:m], start=False,
                                            stop=not with_max, skip_group_check=True)
                    if with_max:
                        for c, wd, q0 in tiles:
                            for s in heads:
                                ins = pe.matmul(PS[:, base + s, c:c + wd], pick_max[:, UH * g + s, :], net.mT[:, q0:q0 + wd],
                                                start=False, stop=True, skip_group_check=True)
                ins.then_inc(scores_ready, 1)

            def outputs(n):
                b, g = units[n]
                base = 4 * (n % 2)
                for half in range(2):
                    pe.wait_ge(exp_ready, 2 * n + half + 1)
                    for kt, (c, wd) in enumerate(((0, wide), (wide, P))):
                        for s in range(UH // 2 * half, UH // 2 * (half + 1)):
                            at = ((TPS * b + kt) * HEADS + (g if gqa else UH * g + s)) * (HD + 1)
                            ins = pe.matmul(PS[VW * s:VW * s + VW, base, kt * P:kt * P + wd], net.vflat[:, at:at + VW],
                                            ex[n % 2][:, s, c:c + wd], start=kt == 0, stop=kt == 1, skip_group_check=True)
                ins.then_inc(out_ready, 1)

            for n in range(NU + 1):
                if n < NU:
                    scores(n)
                if n >= 1:
                    outputs(n - 1)
            pe.wait_ge(out_read, NU)
            for n, (b, g) in enumerate(units):
                for qt in range(TPS):
                    ins = pe.transpose(PS[:, TPS * b + qt, g * P:(g + 1) * P], outT[:, n, qt * P:(qt + 1) * P], w["ident"][:])
            ins.then_inc(turned, 1)

        @block.scalar
        def _(act):
            load_table(net, act, ACT.Exp)
            for n in range(NU):
                act.wait_ge(scores_ready, n + 1)
                if n >= 2:
                    act.wait_ge(out_ready, n - 1)
                for half in range(2):
                    heads, bank = slice(UH // 2 * half, UH // 2 * (half + 1)), 4 * (n % 2) + UH // 2 * half
                    act.activation(ex[n % 2][:, heads, 0:cols], PS[:, bank:bank + UH // 2, 0:cols], ACT.Exp,
                                   scale=scale).then_inc(exp_ready, 1)

        @block.vector
        def _(dve):
            for n, (b, g) in enumerate(units):
                dve.wait_ge(out_ready, n + 1)
                dve.tensor_copy(outT[:, n, :], PS[:, 4 * (n % 2), 0:SEQ]).then_inc(out_read, 1)
            dve.wait_ge(turned, 1)
            o4 = PS[:, 0:NT, :].rearrange("p t (h d) -> p t h d", h=HEADS)
            dve.reciprocal(net.orec[:], o4[:, :, :, HD]).then_inc(rec_ready, 1)
            dve.wait_ge(rec_ready, 1)
            dve.tensor_tensor(net.V[:].rearrange("p t (h d) -> p t h d", d=HD), o4[:, :, :, 0:HD],
                              bc(net.orec[:].unsqueeze(3), [P, NT, HEADS, HD]), ALU.mult)


def out_project(net, src, wo, dst, add=None, bias=None):
    with net.stage("wo", "turned in_sbuf ready dve_chain") as (block, turned, in_sbuf, ready, dve_chain):
        @block.tensor
        def _(pe):
            for t in range(NT):
                ins = pe.transpose(net.PS[:, 0, t * P:(t + 1) * P], src[:, t, :], net.w["ident"][:])
            ins.then_inc(turned, 1)
            pe.wait_ge(in_sbuf, 1)
            for t in range(NT):
                ins = pe.matmul(net.PS[:, 1, t * P:(t + 1) * P], net.RT[:, t * P:(t + 1) * P], wo, start=True, stop=True)
            ins.then_inc(ready, 1)

        @block.scalar
        def _(act):
            act.wait_ge(turned, 1)
            act.activation(net.RT[:], net.PS[:, 0, :], ACT.Identity).then_inc(in_sbuf, 1)

        @block.vector
        def _(dve):
            chain = Chain(dve, dve_chain)
            if bias is not None:
                chain.link(dve.tensor_tensor(net.R[:], add[:], bc(bias.unsqueeze(1), [P, NT, P]), ALU.add))
            dve.wait_ge(ready, 1)
            y = net.PS[:, 1, :].rearrange("p (t d) -> p t d", t=NT)
            if add is None:
                dve.tensor_copy(dst[:], y)
            else:
                dve.tensor_tensor(dst[:], y, net.R[:] if bias is not None else add[:], ALU.add)


def l1_mixer(net, before):
    w = net.w
    pre = (net.X, "ln", net.U, None, None, None, None)
    norm(net, net.U, "rms", T=net.UT, scale=w["L1a_n1"][:, 0:1], before=[*before, pre])
    project(net, "latent", None, 4, w["cosG"][:], w["sinG"][:])
    attend(net, False, False, HD ** -0.5, 4)
    out_project(net, net.V, w["g_wo"][:], net.U, add=net.U)
    norm(net, net.U, "rms", T=net.UT, scale=w["L1a_n2"][:, 0:1])
    project(net, "rope_norm", w["l_wqkv"][:], 4, w["cosL"][:], w["sinL"][:])
    attend(net, True, False, HD ** -0.5, 4)
    out_project(net, net.V, w["l_wo"][:], net.Y, add=net.U)
    return last_norm(net.Y, "ln", add_to=net.X)


def gelu_experts(net, l):
    w, PS, big = net.w, net.PS, net.big
    NF = 4
    hid = [big[:, 4 * i:4 * i + 4, :] for i in range(2)]
    mean = l % 2 == 1
    with net.stage("l1exp", "up h_ready y_ready acc_ready bias_ready mean_ready logits_ready centred exp_ready weights_ready "
                   "turned cwT_ready dve_chain") as (block, up, h_ready, y_ready, acc_ready, bias_ready, mean_ready,
                                                     logits_ready, centred, exp_ready, weights_ready, turned, cwT_ready, dve_chain):
        @block.tensor
        def _(pe):
            if not mean:
                gate_logits(net, pe, 7, w["L1f_gw"][:, l, :], mean, logits_ready)

            def down(e):
                pe.wait_ge(h_ready, NF * (e + 1))
                if e >= 1:
                    pe.wait_ge(acc_ready, e)
                for t in range(NT):
                    for f in range(NF):
                        ins = pe.matmul(PS[:, 6 + e % 2, t * P:(t + 1) * P], hid[e % 2][:, f, t * P:(t + 1) * P],
                                        w["L1f_w2"][:, l, e, f, :], start=f == 0, stop=f == NF - 1)
                ins.then_inc(y_ready, 1)

            for e in range(E):
                if e == 2:
                    pe.wait_ge(cwT_ready, 1)
                    weighted_biases(net, pe, E, 7, w["L1f_b2"][:, l, :], bias_ready)
                for f in range(NF):
                    u = NF * e + f
                    if u >= 6:
                        pe.wait_ge(h_ready, u - 5)
                    pe.matmul(PS[:, u % 6, :], w["L1f_w1"][:, l, e, f * P:(f + 1) * P], net.UT[:], start=True, stop=True).then_inc(up, 1)
                    if mean and u == 1:
                        pe.wait_ge(mean_ready, 1)
                        gate_logits(net, pe, 7, w["L1f_gw"][:, l, :], mean, logits_ready)
                if e == 1:
                    pe.wait_ge(weights_ready, 1)
                    turn_routing(net, pe, 7, E, turned)
                if e >= 1:
                    down(e - 1)
            down(E - 1)

        @block.scalar
        def _(act):
            load_table(net, act, ACT.Exp)
            act.wait_ge(centred, 1)
            routing_exp(net, act, "two", exp_ready)
            load_table(net, act, ACT.Gelu, place=1)
            for u in range(NF * E):
                e, f = u // NF, u % NF
                if u == 2 * NF:
                    act.wait_ge(turned, 1)
                    act.activation(net.cwT[0:E, :], PS[0:E, 7, :], ACT.Identity).then_inc(cwT_ready, 1)
                act.wait_ge(up, u + 1)
                if e >= 2:
                    act.wait_ge(y_ready, e - 1)
                act.activation(hid[e % 2][:, f, :], PS[:, u % 6, :], ACT.Gelu,
                               bias=w["L1f_b1"][:, l, e, f:f + 1]).then_inc(h_ready, 1)

        @block.vector
        def _(dve):
            chain = Chain(dve, dve_chain)
            if mean:
                sequence_means(net, dve, chain, mean_ready)
            choose(net, dve, chain, "two", 7, logits_ready, centred, exp_ready, weights_ready, logit_bias=w["L1f_gb"][:, l, :])
            dve.wait_ge(weights_ready, 1)
            dve.wait_ge(bias_ready, 1)
            dve.tensor_copy(net.acc[:], PS[:, 7, :].rearrange("p (t d) -> p t d", t=NT)).then_inc(acc_ready, 1)
            for e in range(E):
                dve.wait_ge(y_ready, e + 1)
                dve.wait_ge(acc_ready, e + 1)
                for t in range(NT):
                    ins = dve.scalar_tensor_tensor(out=net.acc[:, t, :], in0=PS[:, 6 + e % 2, t * P:(t + 1) * P],
                                                   scalar=net.cw[:, t, e:e + 1], in1=net.acc[:, t, :],
                                                   op0=ALU.mult, op1=ALU.add)
                ins.then_inc(acc_ready, 1)
            dve.wait_ge(acc_ready, E + 1)
            dve.tensor_tensor(net.U[:], net.U[:], net.acc[:], ALU.add)


def l1_experts(net, before):
    w = net.w
    before = [*before, (net.X, "ln", net.U, None, None, None, None)]
    for l in range(2):
        norm(net, net.U, "ln", T=net.UT, scale=w["L1f_ln1w"][:, l:l + 1], bias=w["L1f_ln1b"][:, l:l + 1],
             before=() if l else before)
        project(net, "plain", w["L1f_wqkv"][:, l, :], HEADS, bias=w["L1f_bqkv"][:, l, :])
        attend(net, False, True, HD ** -0.5, HEADS)
        out_project(net, net.V, w["L1f_wo"][:, l, :], net.U, add=net.U, bias=w["L1f_bo"][:, l, :])
        norm(net, net.U, "ln", T=net.UT, scale=w["L1f_ln2w"][:, l:l + 1], bias=w["L1f_ln2b"][:, l:l + 1])
        gelu_experts(net, l)
    return last_norm(net.U, "ln", add_to=net.X)


def l2_mixer(net, before):
    w = net.w
    norm(net, net.X, "ln", T=net.UT, before=before)
    project(net, "norm_rope", w["L2a_wqkv"][:], 4, w["cosL"][:], w["sinL"][:], gain=w["L2a_gain"][:])
    attend(net, True, True, HD ** -0.5, 4)
    with net.stage("pairmix", "dve_chain") as (block, dve_chain):
        @block.vector
        def _(dve):
            chain = Chain(dve, dve_chain)
            y = net.V[:].rearrange("p t (q i d) -> p t q i d", i=2, d=HD)
            out = net.R[:].rearrange("p t (q o d) -> p t q o d", o=2, d=HD)
            t = net.tmp[0][:, :, 0:HEADS // 2, :]
            mix = w["L2a_mix"]
            shape = [P, NT, HEADS // 2, HD]
            for o in range(2):
                dve.tensor_tensor(out[:, :, :, o, :], y[:, :, :, 0, :], bc(mix[:, :, o, 0].unsqueeze(1).unsqueeze(3), shape), ALU.mult)
                chain.link(dve.tensor_tensor(t, y[:, :, :, 1, :], bc(mix[:, :, o, 1].unsqueeze(1).unsqueeze(3), shape), ALU.mult))
                chain.link(dve.tensor_tensor(out[:, :, :, o, :], out[:, :, :, o, :], t, ALU.add))
    out_project(net, net.R, w["L2a_wo"][:], net.Y)
    return last_norm(net.Y, "ln", add_to=net.X)


def l2_experts(net, before):
    w, PS = net.w, net.PS
    norm(net, net.X, "ln", T=net.UT, before=before)
    with net.stage("l2exp", "y_ready y_read bias_ready logits_ready centred exp_ready weights_ready turned cwT_ready "
                   "dve_chain") as (block, y_ready, y_read, bias_ready, logits_ready, centred, exp_ready, weights_ready,
                                    turned, cwT_ready, dve_chain):
        @block.scalar
        def _(act):
            load_table(net, act, ACT.Exp)
            act.wait_ge(centred, 1)
            routing_exp(net, act, "all", exp_ready)
            act.wait_ge(turned, 1)
            act.activation(net.cwT[0:E, :], PS[0:E, 7, :], ACT.Identity).then_inc(cwT_ready, 1)

        @block.tensor
        def _(pe):
            gate_logits(net, pe, 7, w["L2f_gate"][:], False, logits_ready)
            for t in range(NT):
                if t == 3:
                    pe.wait_ge(weights_ready, 1)
                    turn_routing(net, pe, 7, E, turned)
                    pe.wait_ge(cwT_ready, 1)
                    weighted_biases(net, pe, E, 7, w["L2f_b"][:], bias_ready)
                b = 2 * (t % 3)
                if t >= 3:
                    pe.wait_ge(y_read, t - 2)
                for half in range(2):
                    ins = pe.matmul(PS[:, b + half, :], net.UT[:, t * P:(t + 1) * P], w["L2f_w"][:, half * 512:(half + 1) * 512],
                                    start=True, stop=True)
                ins.then_inc(y_ready, 1)

        @block.vector
        def _(dve):
            chain = Chain(dve, dve_chain)
            choose(net, dve, chain, "all", 7, logits_ready, centred, exp_ready, weights_ready, logit_bias=w["L2f_gb"][:])
            dve.wait_ge(weights_ready, 1)
            dve.wait_ge(bias_ready, 1)
            chain.link(dve.tensor_copy(net.acc[:], PS[:, 7, :].rearrange("p (t d) -> p t d", t=NT)))
            for t in range(NT):
                dve.wait_ge(y_ready, t + 1)
                for e in range(E):
                    ins = dve.scalar_tensor_tensor(out=net.acc[:, t, :], in0=PS[:, 2 * (t % 3) + e // 4, (e % 4) * P:(e % 4 + 1) * P],
                                                   scalar=net.cw[:, t, e:e + 1], in1=net.acc[:, t, :], op0=ALU.mult, op1=ALU.add)
                    if e < E - 1:
                        chain.link(ins)
                ins.then_inc(y_read, 1)
    return last_norm(net.acc, "ln", add_to=net.X)


def l3_mixer(net, before):
    w, PS, big = net.w, net.PS, net.big
    M, DK, HP = 64, 16, 4
    spread_w = net.mask_bf["spread"].rearrange("p (k c) -> p k c", k=DK)
    stacked = [a.rearrange("p a b -> p (a b)").bitcast(BF16).rearrange("p (h t) -> p h t", h=HP)
               for a in (net.turned[0:96, 5:7, :], net.tmps[0:96, 0:2, :], net.tmps[0:96, 2:4, :])]
    left = [big[:, n, :] for n in range(3)]
    halves = [big[:, 3 + n // 2, :].bitcast(BF16)[:, (n % 2) * TOK:(n % 2 + 1) * TOK] for n in range(9)]
    rounded = [halves[3 * n:3 * n + 3] for n in range(3)]
    norm(net, net.X, "ln", T=net.UT, before=before)
    with net.stage("l3proj", "p_ready s_ready g_ready dve_chain") as (block, p_ready, s_ready, g_ready, dve_chain):
        @block.tensor
        def _(pe):
            for n, name in enumerate(("L3a_wq", "L3a_wk", "L3a_wv")):
                pe.matmul(PS[:, n, :], w[name][:], net.UT[:], start=True, stop=True).then_inc(p_ready, 1)
            pe.matmul(PS[0:16, 3, :], w["L3a_wf1"][:], net.UT[:], start=True, stop=True).then_inc(p_ready, 1)
            pe.matmul(PS[0:16, 4, :], w["L3a_wg1"][:], net.UT[:], start=True, stop=True).then_inc(p_ready, 1)
            pe.wait_ge(s_ready, 5)
            for t in range(NT):
                ins = pe.matmul(PS[:, 5, t * P:(t + 1) * P], net.g_g1[:, t * P:(t + 1) * P], w["L3a_wg2"][:], start=True, stop=True)
            ins.then_inc(g_ready, 1)

        @block.scalar
        def _(act):
            load_table(net, act, ACT.Silu)
            for n, (dst, f) in enumerate(((net.g_q, ACT.Silu), (net.g_k, ACT.Silu), (net.g_v, ACT.Identity))):
                act.wait_ge(p_ready, n + 1)
                act.activation(dst[:], PS[:, n, :], f).then_inc(s_ready, 1)
            for n, dst in ((3, net.g_f1), (4, net.g_g1)):
                act.wait_ge(p_ready, n + 1)
                act.activation(dst[:], PS[0:16, n, :], ACT.Identity).then_inc(s_ready, 1)
            act.wait_ge(g_ready, 1)
            act.activation(net.U[:], PS[:, 5, :].rearrange("p (t d) -> p t d", t=NT), ACT.Sigmoid)

        @block.vector
        def _(dve):
            dve.wait_ge(s_ready, 3)
            for src, dst in ((net.g_k, net.g_dk), (net.g_v, net.g_dv)):
                s3, d3 = (a[:].rearrange("p (b t) -> p b t", b=PAIR) for a in (src, dst))
                dve.tensor_scalar(d3[:, :, 0:1], s3[:, :, 0:1], -1.0, None, ALU.mult)
                dve.tensor_tensor(d3[:, :, 1:], s3[:, :, 0:SEQ - 1], s3[:, :, 1:], ALU.subtract)

    with net.stage("l3parts", "parts_ready dve_chain") as (block, parts_ready, dve_chain):
        rows = [slice(32 * m, 32 * m + 32) for m in range(4)]

        @block.vector
        def _(dve):
            chain = Chain(dve, dve_chain)
            xs = [net.g_dk, net.g_q, net.g_dv]
            for m in range(3):
                for n in range(3):
                    dve.tensor_copy(rounded[n][m], xs[n]).then_inc(parts_ready, 1)
                if m < 2:
                    dve.wait_ge(parts_ready, 3 * (m + 1))
                    for n in range(3):
                        ins = dve.tensor_tensor(left[n], xs[n], rounded[n][m], ALU.subtract)
                    chain.link(ins)
                    xs = left
            dve.wait_ge(parts_ready, 9)
            for n in range(3):
                for m in (1, 2):
                    if (n, m) != (2, 1):
                        for hp in range(HP):
                            dve.tensor_copy(stacked[n][rows[m], hp, :], rounded[n][m][rows[hp], :])

        @block.scalar
        def _(act):
            for n, m in ((0, 0), (1, 0), (2, 0), (2, 1)):
                act.wait_ge(parts_ready, 3 * m + n + 1)
                for hp in range(HP):
                    act.activation(stacked[n][rows[m], hp, :], rounded[n][m][rows[hp], :], ACT.Identity)

    F, QV, a_e, a_w = ([big[:, 2 * i + j, :] for j in range(2)] for i in range(4))
    b_e, b_w, OK = [net.g_q, net.g_k], [net.g_dk, net.g_dv], net.turned[:, 7, :]
    soft = net.R
    A_DK, A_Q, A_SUM, B_DV, OUT = 0, 2, 4, 5, 7
    for step in range(HP + 1):
        first, second = step < HP, step > 0
        fa, qa = F[step % 2], QV[step % 2]
        fb, qb = F[(step - 1) % 2], QV[(step - 1) % 2]
        outs = slice(32 * (step - 1), 32 * step)
        with net.stage("l3scan", "f_ready fs_ready a_spread a_prod a_used b_spread b_state b_prod b_used scores_in turned "
                       "centred exp_ready soft_ready back b_even dve_chain") as (
                block, f_ready, fs_ready, a_spread, a_prod, a_used, b_spread, b_state, b_prod, b_used, scores_in, turned,
                centred, exp_ready, soft_ready, back, b_even, dve_chain):
            lag = 2 if first and second else 0
            shared = not first

            def wait_product(engine, k):
                if shared:
                    engine.wait_ge(b_prod if k % 2 else b_even, k // 2 + 1)
                else:
                    engine.wait_ge(b_prod, k + 1)

            @block.tensor
            def _(pe):
                if first:
                    pe.matmul(PS[:, A_SUM, :], w["L3a_wf2"][:, step * P:(step + 1) * P], net.g_f1, start=True, stop=True).then_inc(f_ready, 1)

                def reduce_a(k):
                    pe.wait_ge(a_prod, k + 1)
                    pe.matmul(PS[:, A_SUM, :], w["ident"][:], a_w[k % 2], start=k == 0, stop=k == DK - 1).then_inc(a_used, 1)

                def spread_b(k):
                    if k >= 2:
                        pe.wait_ge(b_state, k - 1)
                    pe.matmul(PS[:, B_DV + k % 2, :], spread_w[0:96, k, :], stacked[2][:, step - 1, :], start=True, stop=True).then_inc(b_spread, 1)

                def reduce_b(k):
                    wait_product(pe, k)
                    pe.matmul(PS[outs, OUT, :], w["gather"][:, k, :], b_w[k % 2], start=k == 0, stop=k == DK - 1).then_inc(b_used, 1)

                for k in range(DK):
                    if first:
                        if k >= 2:
                            pe.wait_ge(a_prod, k - 1)
                        pe.matmul(PS[:, A_DK + k % 2, :], spread_w[0:96, k, :], stacked[0][:, step, :], start=True, stop=True)
                        pe.matmul(PS[:, A_Q + k % 2, :], spread_w[0:96, k, :], stacked[1][:, step, :], start=True, stop=True).then_inc(a_spread, 1)
                    if second and k >= lag:
                        spread_b(k - lag)
                    if first and k >= 1:
                        reduce_a(k - 1)
                    if second and k - lag >= 1:
                        reduce_b(k - lag - 1)
                if first:
                    reduce_a(DK - 1)
                if lag:
                    spread_b(DK - 2)
                    reduce_b(DK - 3)
                elif second:
                    reduce_b(DK - 1)
                if first:
                    pe.wait_ge(scores_in, 1)
                    for t in range(NT):
                        ins = pe.transpose(PS[:, A_DK, t * P:(t + 1) * P], OK[:, t * P:(t + 1) * P], w["ident"][:])
                    ins.then_inc(turned, 1)
                    if lag:
                        spread_b(DK - 1)
                        reduce_b(DK - 2)
                    pe.wait_ge(soft_ready, 1)
                    for t in range(NT):
                        ins = pe.transpose(PS[:, A_DK + 1, t * P:(t + 1) * P], soft[:, t, :], w["ident"][:])
                    ins.then_inc(back, 1)
                    if lag:
                        reduce_b(DK - 1)

            if first:
                @block.scalar
                def _(act):
                    act.wait_ge(f_ready, 1)
                    act.activation(fa, PS[:, A_SUM, :], ACT.Sigmoid).then_inc(fs_ready, 1)
                    load_table(net, act, ACT.Exp)
                    act.wait_ge(a_used, DK)
                    act.activation(OK, PS[:, A_SUM, :], ACT.Identity).then_inc(scores_in, 1)
                    act.wait_ge(centred, 1)
                    act.activation(soft[:], soft[:], ACT.Exp).then_inc(exp_ready, 1)
                    act.wait_ge(back, 1)
                    act.activation(qa, PS[:, A_DK + 1, :], ACT.Identity)

            @block.vector
            def _(dve):
                chain = Chain(dve, dve_chain)

                def scan(dst, rows, f):
                    for b in range(PAIR):
                        at = slice(b * SEQ, (b + 1) * SEQ)
                        ins = dve.tensor_tensor_scan(dst[:, at], rows[:, at], f[:, at], 0.0, ALU.add, ALU.mult)
                    return ins

                def state_b(k):
                    dve.wait_ge(b_spread, k + 1)
                    if k >= 2:
                        wait_product(dve, k - 2)
                    scan(b_e[k % 2], PS[:, B_DV + k % 2, :], fb).then_inc(b_state, 1)
                    if shared and k % 2 == 0:
                        dve.wait_ge(b_state, k + 1)
                        if k >= 2:
                            dve.wait_ge(b_used, k - 1)
                        dve.tensor_tensor(b_w[0], b_e[0], qb, ALU.mult).then_inc(b_even, 1)

                if first:
                    dve.wait_ge(fs_ready, 1)
                for k in range(DK):
                    if first:
                        dve.wait_ge(a_spread, k + 1)
                        ins = scan(a_e[k % 2], PS[:, A_DK + k % 2, :], fa)
                        ins.then_inc(dve_chain, 1)
                        chain.n += 1
                    if second and k >= lag:
                        state_b(k - lag)
                    if first:
                        dve.wait_ge(dve_chain, chain.n)
                        if k >= 2:
                            dve.wait_ge(a_used, k - 1)
                        dve.tensor_tensor(a_w[k % 2], PS[:, A_Q + k % 2, :], a_e[k % 2], ALU.mult).then_inc(a_prod, 1)
                if lag:
                    state_b(DK - 2)
                if first:
                    dve.wait_ge(turned, 1)
                    s4 = PS[:, A_DK, :].rearrange("p (t h m) -> p t h m", t=NT, h=2)
                    d4 = soft[:].rearrange("p t (h m) -> p t h m", h=2)
                    top, tot = net.orec[:, :, 0:2], net.orec[:, :, 2:4]
                    chain.link(dve.tensor_reduce(top, s4, AX.X, ALU.max))
                    dve.tensor_tensor(d4, s4, bc(top.unsqueeze(3), [P, NT, 2, M]), ALU.subtract).then_inc(centred, 1)
                    if lag:
                        state_b(DK - 1)
                    dve.wait_ge(exp_ready, 1)
                    chain.link(dve.tensor_reduce(tot, d4, AX.X, ALU.add))
                    chain.link(dve.reciprocal(tot, tot))
                    dve.tensor_tensor(d4, d4, bc(tot.unsqueeze(3), [P, NT, 2, M]), ALU.mult).then_inc(soft_ready, 1)

            if second:
                @block.gpsimd
                def _(pool):
                    for k in range(1 if shared else 0, DK, 2 if shared else 1):
                        pool.wait_ge(b_state, k + 1)
                        if k >= 2:
                            pool.wait_ge(b_used, k - 1)
                        pool.tensor_tensor(b_w[k % 2], b_e[k % 2], qb, ALU.mult).then_inc(b_prod, 1)

    with net.stage("l3out", "sum_ready turned sq_ready sd_ready dve_chain") as (block, sum_ready, turned, sq_ready, sd_ready, dve_chain):
        ovT = big[:, 0, :]

        @block.vector
        def _(dve):
            chain = Chain(dve, dve_chain)
            dve.tensor_tensor(ovT, PS[:, OUT, :], net.g_v[:], ALU.add).then_inc(sum_ready, 1)
            dve.wait_ge(turned, 1)
            chain.link(dve.tensor_tensor(net.V[:], PS[:, 0, :].rearrange("p (t d) -> p t d", t=NT), net.U[:], ALU.mult))
            chain.link(dve.tensor_tensor(net.R[:], net.V[:], net.V[:], ALU.mult))
            dve.tensor_reduce(net.ss[:, :, 0:8], net.R[:].rearrange("p t (h d) -> p t h d", h=8), AX.X, ALU.add).then_inc(sq_ready, 1)
            dve.wait_ge(sd_ready, 1)
            chain.link(dve.reciprocal(net.ss[:, :, 0:8], net.ss[:, :, 0:8]))
            v4 = net.V[:].rearrange("p t (h d) -> p t h d", h=8)
            dve.tensor_tensor(v4, v4, bc(net.ss[:, :, 0:8].unsqueeze(3), [P, NT, 8, DK]), ALU.mult)

        @block.tensor
        def _(pe):
            pe.wait_ge(sum_ready, 1)
            for t in range(NT):
                ins = pe.transpose(PS[:, 0, t * P:(t + 1) * P], ovT[:, t * P:(t + 1) * P], w["ident"][:])
            ins.then_inc(turned, 1)

        @block.scalar
        def _(act):
            load_table(net, act, ACT.Sqrt)
            act.wait_ge(sq_ready, 1)
            act.activation(net.ss[:, :, 0:8], net.ss[:, :, 0:8], ACT.Sqrt, scale=1.0 / DK, bias=w["eps"][:, 0:1]).then_inc(sd_ready, 1)
    with net.stage("l3wo", "turned scaled ready") as (block, turned, scaled, ready):
        @block.tensor
        def _(pe):
            for t in range(NT):
                ins = pe.transpose(PS[:, 0, t * P:(t + 1) * P], net.V[:, t, :], w["ident"][:])
            ins.then_inc(turned, 1)
            pe.wait_ge(scaled, 1)
            for t in range(NT):
                ins = pe.matmul(PS[:, 1, t * P:(t + 1) * P], net.RT[:, t * P:(t + 1) * P], w["L3a_wo"][:], start=True, stop=True)
            ins.then_inc(ready, 1)

        @block.scalar
        def _(act):
            act.wait_ge(turned, 1)
            act.activation(net.RT[:], PS[:, 0, :], ACT.Identity, scale=w["L3a_nw"][:, 0:1]).then_inc(scaled, 1)

        @block.vector
        def _(dve):
            dve.wait_ge(ready, 1)
            dve.tensor_copy(net.Y[:], PS[:, 1, :].rearrange("p (t d) -> p t d", t=NT))
    return last_norm(net.Y, "ln", add_to=net.X)


def l3_experts(net, before):
    w, PS, big = net.w, net.PS, net.big
    norm(net, net.X, "ln", tok=net.U, T=net.UT, before=before)
    route(net, "sigmoid", w["L3f_gate"][:], select_bias=w["L3f_eb"][:])
    HID, HB = 176, 48
    bfv = big[:].rearrange("p a b -> p (a b)").bitcast(BF16)
    xin = [bfv[:, i * 512:(i + 1) * 512] for i in range(2)]
    xT = [bfv[:, 1024 + i * 512:1024 + (i + 1) * 512] for i in range(2)]
    hA = [bfv[:, 2048 + i * 512:2048 + (i + 1) * 512] for i in range(2)]
    hB = [bfv[0:HB, 3072 + i * 512:3072 + (i + 1) * 512] for i in range(2)]
    yb = [bfv[:, 4096 + i * 512:4096 + (i + 1) * 512] for i in range(2)]
    sA, sB = big[:, 5, :], big[0:HB, 6, :]
    XT, UP, Y = [PS[:, 6 * i, :].bitcast(BF16)[:, 0:TOK] for i in range(2)], (1, 4), (3, 7)
    with net.stage("l3exp", "x_ready turned xT_ready up hr_ready h_ready hb_ready y_ready yb_ready added s_up s_relu s_sq s_down") as (
            block, x_ready, turned, xT_ready, up, hr_ready, h_ready, hb_ready, y_ready, yb_ready, added, s_up, s_relu, s_sq, s_down):
        @block.tensor
        def _(pe):
            def turn_rows(e):
                pe.wait_ge(x_ready, e + 1)
                if e >= 2:
                    pe.wait_ge(xT_ready, e - 1)
                for t in range(NT):
                    c = slice(t * P, (t + 1) * P)
                    ins = pe.transpose(XT[e % 2][:, c], xin[e % 2][:, c], net.ident_bf[:])
                ins.then_inc(turned, 1)

            def up_rows(e):
                pe.wait_ge(xT_ready, e + 1)
                if e == 1:
                    pe.wait_ge(s_relu, 1)
                if e >= 2:
                    pe.wait_ge(hr_ready, 2 * (e - 1))
                pe.matmul(PS[:, UP[e % 2], :], net.up_bf[:, e, 0:P], xT[e % 2], start=True, stop=True)
                pe.matmul(PS[0:HB, UP[e % 2] + 1, :], net.up_bf[:, e, P:HID], xT[e % 2], start=True, stop=True).then_inc(up, 1)

            def down_rows(e):
                pe.wait_ge(h_ready, e + 1)
                pe.wait_ge(hb_ready, e + 1)
                if e >= 2:
                    pe.wait_ge(yb_ready, e - 1)
                for t in range(NT):
                    c = slice(t * P, (t + 1) * P)
                    pe.matmul(PS[:, Y[e % 2], c], hA[e % 2][:, c], net.dnA_bf[:, e, :], start=True, stop=False)
                    ins = pe.matmul(PS[:, Y[e % 2], c], hB[e % 2][:, c], net.dnB_bf[:, e, :], start=False, stop=True)
                ins.then_inc(y_ready, 1)

            pe.matmul(PS[:, 4, :], w["L3f_sup"][:, 0:P], net.UT[:], start=True, stop=True)
            pe.matmul(PS[0:HB, 5, :], w["L3f_sup"][:, P:HID], net.UT[:], start=True, stop=True).then_inc(s_up, 1)
            turn_rows(0)
            turn_rows(1)
            up_rows(0)
            for e in range(E):
                if e + 1 < E:
                    up_rows(e + 1)
                if e + 2 < E:
                    turn_rows(e + 2)
                if e == E - 1:
                    pe.wait_ge(s_sq, 2)
                    pe.wait_ge(hr_ready, 2 * (E - 1))
                    for t in range(NT):
                        c = slice(t * P, (t + 1) * P)
                        pe.matmul(PS[:, UP[0], c], sA[:, c], w["L3f_sdnA"][:], start=True, stop=False)
                        ins = pe.matmul(PS[:, UP[0], c], sB[:, c], w["L3f_sdnB"][:], start=False, stop=True)
                    ins.then_inc(s_down, 1)
                down_rows(e)

        @block.scalar
        def _(act):
            def take_turned(e):
                act.wait_ge(turned, e + 1)
                if e >= 2:
                    act.wait_ge(up, e - 1)
                act.activation(xT[e % 2], XT[e % 2], ACT.Identity).then_inc(xT_ready, 1)

            def take_out(e):
                act.wait_ge(y_ready, e + 1)
                if e >= 2:
                    act.wait_ge(added, e)
                act.activation(yb[e % 2], PS[:, Y[e % 2], :], ACT.Identity).then_inc(yb_ready, 1)

            act.wait_ge(s_up, 1)
            act.activation(sA, PS[:, 4, :], ACT.Relu)
            act.activation(sB, PS[0:HB, 5, :], ACT.Relu).then_inc(s_relu, 1)
            take_turned(0)
            take_turned(1)
            for e in range(E):
                act.wait_ge(up, e + 1)
                if e >= 2:
                    act.wait_ge(y_ready, e - 1)
                act.activation(hA[e % 2], PS[:, UP[e % 2], :], ACT.Relu).then_inc(hr_ready, 1)
                act.activation(hB[e % 2], PS[0:HB, UP[e % 2] + 1, :], ACT.Relu).then_inc(hr_ready, 1)
                if e + 2 < E:
                    take_turned(e + 2)
                if e >= 1:
                    take_out(e - 1)
            take_out(E - 1)

        @block.vector
        def _(dve):
            def scale_rows(e):
                if e >= 2:
                    dve.wait_ge(turned, e - 1)
                for t in range(NT):
                    ins = dve.tensor_scalar(xin[e % 2][:, t * P:(t + 1) * P], net.U[:, t, :], net.cw[:, t, e:e + 1], None, ALU.mult)
                ins.then_inc(x_ready, 1)

            def add(e):
                dve.wait_ge(yb_ready, e + 1)
                dve.wait_ge(added, e + 1)
                dve.tensor_tensor(net.acc[:], net.acc[:], yb[e % 2].rearrange("p (t d) -> p t d", t=NT), ALU.add).then_inc(added, 1)

            scale_rows(0)
            scale_rows(1)
            dve.memset(net.acc[:], 0.0).then_inc(added, 1)
            for e in range(E):
                dve.wait_ge(hr_ready, 2 * e + 1)
                dve.tensor_tensor(hA[e % 2], hA[e % 2], hA[e % 2], ALU.mult).then_inc(h_ready, 1)
                if e + 2 < E:
                    scale_rows(e + 2)
                if e >= 1:
                    add(e - 1)
            add(E - 1)
            dve.wait_ge(s_down, 1)
            dve.wait_ge(added, E + 1)
            dve.tensor_tensor(net.acc[:], net.acc[:], PS[:, UP[0], :].rearrange("p (t d) -> p t d", t=NT), ALU.add)

        @block.gpsimd
        def _(pool):
            pool.wait_ge(s_relu, 1)
            pool.tensor_tensor(sA, sA, sA, ALU.mult).then_inc(s_sq, 1)
            pool.tensor_tensor(sB, sB, sB, ALU.mult).then_inc(s_sq, 1)
            for e in range(E):
                pool.wait_ge(hr_ready, 2 * (e + 1))
                pool.tensor_tensor(hB[e % 2], hB[e % 2], hB[e % 2], ALU.mult).then_inc(hb_ready, 1)
    return last_norm(net.acc, "ln", add_to=net.X)


STAGES = [l0_mixer, l0_experts, l1_mixer, l1_experts, l2_mixer, l2_experts, l3_mixer, l3_experts]


def sandwich(nc, x, out, w_dram):
    x_d = x.rearrange("(i b) (t p) d -> i p (b t) d", b=PAIR, p=P)
    out_d = out.rearrange("(i b) (t p) d -> i p (b t) d", b=PAIR, p=P)
    with ExitStack() as ctx:
        net = Net(nc, ctx, w_dram)
        load_weights(net)
        with nc.Fori(0, x.shape[0] // PAIR) as i:
            with net.stage("fetch", "x_landed") as (block, x_landed):
                @block.sync
                def _(sp):
                    sp.dma_start(net.X[:], x_d[i]).then_inc(x_landed, 16)
                    sp.wait_ge(x_landed, 16)
            first = net.stages
            left = ()
            for f in STAGES:
                left = f(net, left)
            norms(net, left)
            with net.stage("store", "stored") as (block, stored):
                @block.sync
                def _(sp):
                    sp.dma_start(out_d[i], net.X[:]).then_inc(stored, 16)
                    sp.wait_ge(stored, 16)
            if (net.stages - first) % 2 == 0:
                with net.stage("even", "unused"):
                    pass


def constants():
    c = {"ident": np.eye(P), "zeros": np.zeros((P, P)), "iota8": np.tile(np.arange(E), (P, 1)),
         "eps": np.tile([LN_EPS, RMS_EPS], (P, 1))}
    for name, base in (("G", 1e6), ("L", 1e4)):
        inv = (1.0 / np.float32(base) ** (np.arange(0, HD, 2, dtype=np.float32) / np.float32(HD))).astype(np.float32)
        fr = (np.arange(SEQ, dtype=np.float32)[:, None] * inv[None, :]).astype(np.float32)
        for fn, tag in ((np.cos, "cos"), (np.sin, "sin")):
            t = fn(fr.astype(np.float64)).reshape(TPS, P, HD // 2)
            c[tag + name] = np.tile(t, (PAIR, 1, 1)).transpose(1, 0, 2)
    r = np.arange(P)
    c["mask_qk"] = np.where(r[:, None] >= r[None, :], 0.0, MASKED)
    c["mask_kq"] = np.ascontiguousarray(c["mask_qk"].T)
    k = np.arange(P + WINDOW) - WINDOW
    d = r[:, None] - k[None, :]
    c["lmask_qk"] = np.where((d >= 0) & (d < WINDOW), 0.0, MASKED)
    d = np.arange(P + WINDOW)[None, :] - r[:, None]
    c["lmask_kq"] = np.where((d >= 0) & (d < WINDOW), 0.0, MASKED)
    pick = np.zeros((8, HEADS, HEADS, P))
    pick[:3, np.arange(HEADS), np.arange(HEADS)] = 1.0
    c["pick_max"] = pick.reshape(P, HEADS * P)
    spread = np.zeros((4, 32, 16, 2, 64))
    gather = np.zeros((2, 64, 16, 32))
    for h in range(2):
        for k in range(16):
            spread[:, h * 16 + k, k, h, :] = 1.0
            gather[h, :, k, h * 16 + k] = 1.0
    c["spread"] = spread.reshape(P, 16 * P)
    c["gather"] = gather.reshape(P, 16, 32)
    return {n: np.ascontiguousarray(a, dtype=np.float32) for n, a in c.items()}


def lay_out(a):
    def col(n):
        return a[n].reshape(P, 1)

    def row(n):
        return np.broadcast_to(a[n].reshape(1, -1), (P, a[n].size))

    cat = np.concatenate
    w = {
        "L0a_alog": col("L0_attn_a_log"), "L0a_inw": col("L0_attn_input_norm_w"), "L0a_cout": col("L0_attn_c_out"),
        "L0a_dskip": col("L0_attn_d_skip"), "L0a_ffw": col("L0_attn_ff_norm_w"),
        "L0a_fc": a["L0_attn_ff_fc_w"].T, "L0a_proj": a["L0_attn_ff_proj_w"].T.reshape(2, P, P).transpose(1, 0, 2),
        "L0f_gate": a["L0_ffn_gate_w"].T, "L0f_gb": row("L0_ffn_gate_b"),
        "L0f_b2": cat([a["L0_ffn_b2"], a["L0_ffn_sb2"][None]]),
        "L0f_w2": cat([a["L0_ffn_w2"], a["L0_ffn_sw2"][None]]).transpose(2, 0, 1),
        "L1a_n1": col("L1_attn_norm1_w"), "L1a_n2": col("L1_attn_norm2_w"),
        "g_wq": a["L1_attn_g_wq"], "g_down": a["L1_attn_g_kv_down"],
        "g_up": cat([a["L1_attn_g_k_up"], a["L1_attn_g_v_up"]], 1), "g_wo": a["L1_attn_g_wo"],
        "l_wqkv": cat([a["L1_attn_l_wq"], a["L1_attn_l_wk"], a["L1_attn_l_wv"]], 1), "l_wo": a["L1_attn_l_wo"],
        "L1f_wqkv": cat([a["L1_ffn_wq"], a["L1_ffn_wk"], a["L1_ffn_wv"]], 2).transpose(1, 0, 2),
        "L1f_wo": a["L1_ffn_wo"].transpose(1, 0, 2), "L1f_gw": a["L1_ffn_gate_w"].transpose(1, 0, 2),
        "L1f_w1": a["L1_ffn_e_w1"].transpose(2, 0, 1, 3),
        "L1f_w2": a["L1_ffn_e_w2"].reshape(2, E, 4, P, P).transpose(3, 0, 1, 2, 4),
        "L1f_b1": a["L1_ffn_e_b1"].reshape(2, E, 4, P).transpose(3, 0, 1, 2), "L1f_b2": a["L1_ffn_e_b2"].transpose(1, 0, 2),
        "L2a_wqkv": cat([a["L2_attn_Wq"], a["L2_attn_Wk"], a["L2_attn_Wv"]]).T, "L2a_wo": a["L2_attn_Wo"].T,
        "L2a_gain": row("L2_attn_q_gain"), "L2a_mix": row("L2_attn_pair_mix").reshape(P, 8, 2, 2),
        "L2f_gate": a["L2_ffn_gate_w"].T, "L2f_gb": row("L2_ffn_gate_b"),
        "L2f_w": a["L2_ffn_expert_w"].transpose(2, 0, 1).reshape(P, E * P), "L2f_b": a["L2_ffn_expert_b"],
        "L3a_wq": a["L3_attn_Wq"], "L3a_wk": a["L3_attn_Wk"], "L3a_wv": a["L3_attn_Wv"], "L3a_wf1": a["L3_attn_Wf1"],
        "L3a_wf2": a["L3_attn_Wf2"], "L3a_wg1": a["L3_attn_Wg1"], "L3a_wg2": a["L3_attn_Wg2"], "L3a_wo": a["L3_attn_Wo"],
        "L3a_nw": col("L3_attn_norm_w"), "L3f_gate": a["L3_ffn_gate_w"].T, "L3f_eb": row("L3_ffn_expert_bias"),
        "L3f_up": a["L3_ffn_w_up"].transpose(2, 0, 1),
        "L3f_sup": a["L3_ffn_shared_w_up"].T,
    }
    dn, sdn = a["L3_ffn_w_down"].transpose(2, 0, 1), a["L3_ffn_shared_w_down"].T
    w["L3f_dnA"], w["L3f_dnB"], w["L3f_sdnA"], w["L3f_sdnB"] = dn[:P], dn[P:], sdn[:P], sdn[P:]
    for j in ("1", "3"):
        ww = cat([a["L0_ffn_w" + j], a["L0_ffn_sw" + j][None]])
        bb = cat([a["L0_ffn_b" + j], a["L0_ffn_sb" + j][None]])
        w["L0f_w" + j] = ww.reshape(E + 1, P, 2, P).transpose(3, 0, 2, 1)
        w["L0f_b" + j] = bb.reshape(E + 1, P, 2).transpose(1, 0, 2)
    for n, dst in (("ln1_w", "ln1w"), ("ln1_b", "ln1b"), ("ln2_w", "ln2w"), ("ln2_b", "ln2b")):
        w["L1f_" + dst] = a["L1_ffn_" + n].T
    for n, parts in (("bqkv", ("bq", "bk", "bv")), ("bo", ("bo",)), ("gb", ("gate_b",))):
        r = cat([a["L1_ffn_" + p] for p in parts], 1)
        w["L1f_" + n] = np.broadcast_to(r[None], (P,) + r.shape)
    return {n: np.ascontiguousarray(v) for n, v in w.items()}


def kernel(**inputs):
    import concourse.bacc as _bacc
    from concourse.bass_utils import run_bass_kernel_spmd as _run

    a = {n: np.asarray(v) for n, v in inputs.items()}
    nc = _bacc.Bacc("TRN2", target_bir_lowering=False, num_devices=1)
    arrays = {**lay_out(a), **constants()}
    w_dram = {n: nc.dram_tensor("in_" + n, v.shape, F32, kind="ExternalInput").ap() for n, v in arrays.items()}
    xs = a["L0_attn_x"]
    x = nc.dram_tensor("in_x", xs.shape, F32, kind="ExternalInput").ap()
    out = nc.dram_tensor("out", xs.shape, F32, kind="ExternalOutput").ap()
    sandwich(nc, x, out, w_dram)
    feeds = {"in_" + n: v for n, v in arrays.items()}
    feeds["in_x"] = np.ascontiguousarray(xs)
    r = _run(nc, [feeds], core_ids=[0])
    return r.results[0]["out"]
```
